# Optimizing a Trainium2 kernel written in Bass

```python
import numpy as np
import jax
import jax.numpy as jnp

def _softmax(x, axis=-1):
    return jax.nn.softmax(x, axis=axis)

def _gelu(x):
    return jax.nn.gelu(x, approximate=True)

def _silu(x):
    return jax.nn.silu(x)

def _sigmoid(x):
    return jax.nn.sigmoid(x)

def _layernorm(x, axis=-1, eps=1e-05):
    m = jnp.mean(x, axis=axis, keepdims=True)
    v = jnp.var(x, axis=axis, keepdims=True)
    return (x - m) / jnp.sqrt(v + eps)

def _scatter_add(tgt, idx, src, axis=0):
    return tgt.at[idx].add(src)

def _segment_sum(src, seg, n):
    return jax.ops.segment_sum(src, seg, n)
kernel_name = 'mk_macaron_d2_jaxref_r8_dd94d2'

def setup_inputs(seed: int=0):
    np.random.seed(seed)
    _w = jnp.asarray

    def _L0_attn_setup():
        import jax, jax.numpy as jnp
        import numpy as np
        B, L, D = (2, 256, 128)
        H, HD = (16, 64)
        LD = 32
        key = jax.random.key(seed)
        ks = jax.random.split(key, 6)
        s = lambda fan_in: 1.0 / np.sqrt(fan_in)
        x_bld = jax.random.normal(ks[0], (B, L, D), dtype=jnp.float32)
        Wq = jax.random.normal(ks[1], (D, H, HD), dtype=jnp.float32) * s(D)
        Wkv_down = jax.random.normal(ks[2], (D, LD), dtype=jnp.float32) * s(D)
        Wk_up = jax.random.normal(ks[3], (LD, H, HD), dtype=jnp.float32) * s(LD)
        Wv_up = jax.random.normal(ks[4], (LD, H, HD), dtype=jnp.float32) * s(LD)
        Wout = jax.random.normal(ks[5], (H, HD, D), dtype=jnp.float32) * s(H * HD)
        return {'x_bld': x_bld, 'Wq': Wq, 'Wkv_down': Wkv_down, 'Wk_up': Wk_up, 'Wv_up': Wv_up, 'Wout': Wout}
    _L0_attn_in = _L0_attn_setup()

    def _L0_ffn_setup():
        import jax, jax.numpy as jnp
        import numpy as np
        THRESHOLD = 0.1
        key = jax.random.key(seed)
        k1, k2, k3 = jax.random.split(key, 3)
        B, S, D, E = (4, 512, 128, 8)
        inputs = jax.random.normal(k1, (B, S, D), dtype=jnp.float32)
        gate_w = jax.random.normal(k2, (D, E), dtype=jnp.float32) * 0.02
        gate_b = jnp.zeros((E,), dtype=jnp.float32)
        expert_w = jax.random.normal(k3, (E, D, D), dtype=jnp.float32) * 0.02
        expert_b = jnp.zeros((E, D), dtype=jnp.float32)
        return {'inputs': inputs, 'gate_w': gate_w, 'gate_b': gate_b, 'expert_w': expert_w, 'expert_b': expert_b}
    _L0_ffn_in = _L0_ffn_setup()

    def _L1_attn_setup():
        import jax, jax.numpy as jnp
        import numpy as np
        HEADS = 16
        DIM_HEAD = 64
        HEIGHT = 16
        KERNEL = 5
        DILATION = 1
        ALPHA = 32 ** 2

        def stable_softmax(t, axis=-1, alpha=ALPHA):
            t = t / alpha
            t = t - jax.lax.stop_gradient(jnp.max(t, axis=axis, keepdims=True))
            return jax.nn.softmax(t * alpha, axis=axis)
        key = jax.random.key(seed)
        ks = jax.random.split(key, 5)
        b, n, dim = (4, 4097, 128)
        inner = HEADS * DIM_HEAD
        x = jax.random.normal(ks[0], (b, n, dim), dtype=jnp.float32)
        w_qkv = jax.random.normal(ks[1], (dim, 3 * inner), dtype=jnp.float32) * dim ** (-0.5)
        w_out = jax.random.normal(ks[2], (inner, dim), dtype=jnp.float32) * inner ** (-0.5)
        b_out = jax.random.normal(ks[3], (dim,), dtype=jnp.float32) * 0.02
        w_th = jax.random.normal(ks[4], (HEADS, HEADS), dtype=jnp.float32) * HEADS ** (-0.5)
        return {'x': x, 'w_qkv': w_qkv, 'w_out': w_out, 'b_out': b_out, 'w_th': w_th}
    _L1_attn_in = _L1_attn_setup()

    def _L1_ffn_setup():
        import jax, jax.numpy as jnp
        import numpy as np
        IN_DIM, OUT_DIM, N_PROTO, RANK = (128, 128, 32, 16)
        key = jax.random.key(seed)
        ks = jax.random.split(key, 5)
        x = jax.random.normal(ks[0], (2, 512, IN_DIM), dtype=jnp.float32)
        prototypes = jax.random.normal(ks[1], (N_PROTO, IN_DIM), dtype=jnp.float32) * 0.02
        B = jax.random.normal(ks[2], (N_PROTO, RANK, IN_DIM), dtype=jnp.float32) * 0.02
        A = jax.random.normal(ks[3], (N_PROTO, OUT_DIM, RANK), dtype=jnp.float32) * 0.02
        bias = jnp.zeros((N_PROTO, OUT_DIM), dtype=jnp.float32)
        temp = jnp.asarray(1.0, dtype=jnp.float32)
        return {'x': x, 'prototypes': prototypes, 'B': B, 'A': A, 'bias': bias, 'temp': temp}
    _L1_ffn_in = _L1_ffn_setup()
    _d = {'L0_attn_x_bld': _L0_attn_in['x_bld'], 'L0_attn_Wq': _L0_attn_in['Wq'], 'L0_attn_Wkv_down': _L0_attn_in['Wkv_down'], 'L0_attn_Wk_up': _L0_attn_in['Wk_up'], 'L0_attn_Wv_up': _L0_attn_in['Wv_up'], 'L0_attn_Wout': _L0_attn_in['Wout'], 'L0_ffn_gate_w': _L0_ffn_in['gate_w'], 'L0_ffn_gate_b': _L0_ffn_in['gate_b'], 'L0_ffn_expert_w': _L0_ffn_in['expert_w'], 'L0_ffn_expert_b': _L0_ffn_in['expert_b'], 'L1_attn_w_qkv': _L1_attn_in['w_qkv'], 'L1_attn_w_out': _L1_attn_in['w_out'], 'L1_attn_b_out': _L1_attn_in['b_out'], 'L1_attn_w_th': _L1_attn_in['w_th'], 'L1_ffn_prototypes': _L1_ffn_in['prototypes'], 'L1_ffn_B': _L1_ffn_in['B'], 'L1_ffn_A': _L1_ffn_in['A'], 'L1_ffn_bias': _L1_ffn_in['bias'], 'L1_ffn_temp': _L1_ffn_in['temp']}
    _x0 = _d['L0_attn_x_bld']
    _d['L0_attn_x_bld'] = jax.random.normal(jax.random.fold_in(jax.random.key(seed), 1), (16, 512, 128), dtype=_x0.dtype)
    del _x0
    return _d

def reference(L0_attn_x_bld, L0_attn_Wq, L0_attn_Wkv_down, L0_attn_Wk_up, L0_attn_Wv_up, L0_attn_Wout, L0_ffn_gate_w, L0_ffn_gate_b, L0_ffn_expert_w, L0_ffn_expert_b, L1_attn_w_qkv, L1_attn_w_out, L1_attn_b_out, L1_attn_w_th, L1_ffn_prototypes, L1_ffn_B, L1_ffn_A, L1_ffn_bias, L1_ffn_temp):

    def _L0_attn_ref(x_bld, Wq, Wkv_down, Wk_up, Wv_up, Wout):
        import jax, jax.numpy as jnp
        import numpy as np
        B, L, D = (2, 256, 128)
        H, HD = (16, 64)
        LD = 32
        q_blhd = jnp.einsum('bld,dhk->blhk', x_bld, Wq)
        latent_bll = jnp.einsum('bld,dc->blc', x_bld, Wkv_down)
        k_blhd = jnp.einsum('blc,chk->blhk', latent_bll, Wk_up)
        v_blhd = jnp.einsum('blc,chk->blhk', latent_bll, Wv_up)
        attn = jnp.einsum('bqhd,bkhd->bhqk', q_blhd, k_blhd) / jnp.sqrt(jnp.asarray(HD, dtype=x_bld.dtype))
        l = x_bld.shape[1]
        mask = (jnp.arange(l)[None, :] <= jnp.arange(l)[:, None])[None, None]
        neg_inf = jnp.finfo(attn.dtype).min
        attn = jax.nn.softmax(jnp.where(mask, attn, neg_inf), axis=-1)
        y_blhd = jnp.einsum('bhqk,bkhd->bqhd', attn, v_blhd)
        return jnp.einsum('bqhd,hdo->bqo', y_blhd, Wout)

    def _L0_ffn_ref(inputs, gate_w, gate_b, expert_w, expert_b):
        import jax, jax.numpy as jnp
        import numpy as np
        THRESHOLD = 0.1
        d = inputs.shape[-1]
        x = inputs.reshape(-1, d)
        gate_logits = jax.nn.softmax(x @ gate_w + gate_b, axis=-1)
        selected = (gate_logits >= THRESHOLD).astype(x.dtype)
        weights = gate_logits * selected
        wsum = jnp.sum(weights, axis=-1, keepdims=True)
        weights = weights / jnp.where(wsum == 0, jnp.ones_like(wsum), wsum)
        E = expert_w.shape[0]
        out = jnp.zeros((x.shape[0], expert_w.shape[-1]), dtype=x.dtype)
        for e in range(E):
            out = out + weights[:, e:e + 1] * (x @ expert_w[e] + expert_b[e])
        return out.reshape(*inputs.shape[:-1], out.shape[-1])

    def _L1_attn_ref(x, w_qkv, w_out, b_out, w_th):
        import jax, jax.numpy as jnp
        import numpy as np
        HEADS = 16
        DIM_HEAD = 64
        HEIGHT = 16
        KERNEL = 5
        DILATION = 1
        ALPHA = 32 ** 2

        def stable_softmax(t, axis=-1, alpha=ALPHA):
            t = t / alpha
            t = t - jax.lax.stop_gradient(jnp.max(t, axis=axis, keepdims=True))
            return jax.nn.softmax(t * alpha, axis=axis)
        b, n, dim = x.shape
        h, d = (HEADS, DIM_HEAD)
        height, K, dil = (HEIGHT, KERNEL, DILATION)
        pad = dil * (K - 1) // 2
        scale = d ** (-0.5)
        kernel_numel = K * height
        seq_pad = -(n - 1) % height
        xp = jnp.pad(x, ((0, 0), (0, seq_pad), (0, 0))) if seq_pad > 0 else x
        qkv = xp @ w_qkv
        q, k, v = jnp.split(qkv, 3, axis=-1)
        if n == 1:
            return v @ w_out + b_out
        out_bos = v[:, :1]

        def to_heads(t):
            return t.reshape(b, -1, h, d).transpose(0, 2, 1, 3)
        q, k, v = map(to_heads, (q, k, v))
        q = q * scale
        k_bos, k = (k[:, :, 0], k[:, :, 1:])
        v_bos, v = (v[:, :, 0], v[:, :, 1:])
        q = q[:, :, 1:]
        X = q.shape[2] // height
        k = k.reshape(b, h, X, height, d)
        v = v.reshape(b, h, X, height, d)
        kp = jnp.pad(k, ((0, 0), (0, 0), (pad, pad), (0, 0), (0, 0)))
        vp = jnp.pad(v, ((0, 0), (0, 0), (pad, pad), (0, 0), (0, 0)))
        idx = jnp.arange(X)[:, None] + jnp.arange(K)[None, :] * dil
        kw = kp[:, :, idx].reshape(b, h, X, kernel_numel, d)
        vw = vp[:, :, idx].reshape(b, h, X, kernel_numel, d)
        kb = jnp.broadcast_to(k_bos[:, :, None, None, :], (b, h, X, 1, d))
        vb = jnp.broadcast_to(v_bos[:, :, None, None, :], (b, h, X, 1, d))
        kw = jnp.concatenate([kb, kw], axis=3)
        vw = jnp.concatenate([vb, vw], axis=3)
        qw = q.reshape(b, h, X, height, d)
        sim = jnp.einsum('bhnid,bhnjd->bhnij', qw, kw)
        seq_len = X * height
        q_range = jnp.arange(seq_len).reshape(X, height)
        k_range = jnp.pad(jnp.arange(seq_len).reshape(X, height), ((pad, pad), (0, 0)), constant_values=seq_len)
        kr = k_range[idx].reshape(X, kernel_numel)
        mask = q_range[:, :, None] < kr[:, None, :]
        mask = jnp.pad(mask, ((0, 0), (0, 0), (1, 0)), constant_values=False)
        mask_value = -jnp.finfo(sim.dtype).max
        sim = jnp.where(mask[None, None], mask_value, sim)
        attn = stable_softmax(sim, axis=-1)
        attn = jnp.einsum('gh,bhnij->bgnij', w_th, attn)
        out = jnp.einsum('bhnij,bhnjd->bhnid', attn, vw)
        out = out.transpose(0, 2, 3, 1, 4).reshape(b, X * height, h * d)
        out = jnp.concatenate([out_bos, out], axis=1)
        return (out @ w_out + b_out)[:, :n]

    def _L1_ffn_ref(x, prototypes, B, A, bias, temp):
        import jax, jax.numpy as jnp
        import numpy as np
        IN_DIM, OUT_DIM, N_PROTO, RANK = (128, 128, 32, 16)
        lead = x.shape[:-1]
        xf = x.reshape(-1, IN_DIM)
        x2 = jnp.sum(xf * xf, axis=1, keepdims=True)
        p2 = jnp.sum(prototypes * prototypes, axis=1)
        d2 = x2 + p2[None, :] - 2.0 * (xf @ prototypes.T)
        dists = jnp.sqrt(jnp.maximum(d2, 0.0))
        t = jnp.maximum(jnp.abs(temp), 0.1)
        w = jax.nn.softmax(-dists / t, axis=1)
        topw, topi = jax.lax.top_k(w, 2)
        topw = topw / jnp.sum(topw, axis=1, keepdims=True)
        out = jnp.zeros((xf.shape[0], OUT_DIM), dtype=xf.dtype)
        for tslot in range(2):
            idx = topi[:, tslot]
            wt = topw[:, tslot:tslot + 1]
            h = jnp.einsum('nri,ni->nr', B[idx], xf)
            y = jnp.einsum('nor,nr->no', A[idx], h) + bias[idx]
            out = out + wt * y
        return out.reshape(*lead, OUT_DIM)
    x = L0_attn_x_bld
    x = x + 0.5 * _L0_ffn_ref(_layernorm(x, axis=-1), L0_ffn_gate_w, L0_ffn_gate_b, L0_ffn_expert_w, L0_ffn_expert_b)
    x = x + _L0_attn_ref(_layernorm(x, axis=-1), L0_attn_Wq, L0_attn_Wkv_down, L0_attn_Wk_up, L0_attn_Wv_up, L0_attn_Wout)
    x = x + 0.5 * _L0_ffn_ref(_layernorm(x, axis=-1), L0_ffn_gate_w, L0_ffn_gate_b, L0_ffn_expert_w, L0_ffn_expert_b)
    x = x + 0.5 * _L1_ffn_ref(_layernorm(x, axis=-1), L1_ffn_prototypes, L1_ffn_B, L1_ffn_A, L1_ffn_bias, L1_ffn_temp)
    x = x + _L1_attn_ref(_layernorm(x, axis=-1), L1_attn_w_qkv, L1_attn_w_out, L1_attn_b_out, L1_attn_w_th)
    x = x + 0.5 * _L1_ffn_ref(_layernorm(x, axis=-1), L1_ffn_prototypes, L1_ffn_B, L1_ffn_A, L1_ffn_bias, L1_ffn_temp)
    return x

_drawn_inputs = setup_inputs


def setup_inputs(seed=0):
    import zlib

    import numpy as np

    out = dict(_drawn_inputs(seed))
    spreads = {'L0_ffn_gate_b': (0.0, 0.1), 'L0_ffn_expert_b': (0.0, 0.1), 'L1_ffn_bias': (0.0, 0.1)}
    factors = {'L1_attn_b_out': 2.836, 'L1_ffn_B': 4.76, 'L1_ffn_A': 4.748}
    for name, (base, spread) in spreads.items():
        noise = np.random.default_rng([zlib.crc32(name.encode()), seed]).standard_normal(out[name].shape)
        drawn = base * np.exp(spread * noise) if base else spread * noise
        out[name] = jnp.asarray(drawn.astype(out[name].dtype))
    for name, factor in factors.items():
        out[name] = (out[name] * factor).astype(out[name].dtype)
    return out
```

```python
import concourse.bass as bass
from concourse import mybir
from contextlib import ExitStack

F32 = mybir.dt.float32
BF16 = mybir.dt.bfloat16
ALU = mybir.AluOpType
ACT = mybir.ActivationFunctionType
AX = mybir.AxisListType

P = 128
NB, L, D = 16, 512, 128
NT = L // P
H, HD = 16, 64
HG = 4
NE = 8
LD = 32
NPROTO, RANK = 32, 16
NR = NPROTO * RANK
QW = 32
NW = L // QW
KW = 65
EPS = 1e-5
GATE_MIN = 0.1
MASKED = -1e30
BIG = 1e30
STAGES = "ABADED"


def bc(ap, dim, n):
    shape = list(ap.shape)
    return ap.unsqueeze(dim).broadcast_to(shape[:dim] + [n] + shape[dim:])


class Count:

    def __init__(self, m, name, per=1, frees=False):
        self.sem, self.per, self.base = m.semaphore(name), per, int(frees)

    def open(self, eng):
        assert self.base == 1
        eng.sem_inc(self.sem, 1)

    def wait(self, eng, batch, k=None):
        k = self.per if k is None else k
        eng.wait_ge(self.sem, batch * self.per + (k + self.base))

    def wait_before(self, eng, batch):
        eng.wait_ge(self.sem, batch * self.per + self.base)

    def up(self, ins):
        return ins.then_inc(self.sem, 1)


class Chain(Count):

    def start(self, eng, batch):
        self.eng, self.batch, self.n = eng, batch, 0

    def step(self, ins):
        self.n += 1
        self.up(ins)

    def settle(self, back=0):
        self.wait(self.eng, self.batch, self.n - back)

    def link(self, ins):
        self.step(ins)
        self.settle()

    def end(self):
        assert self.n == self.per, (self.n, self.per)


class Norm:

    def __init__(self, nc, m, tag, xnT, psT):
        self.nc, self.m, self.xnT, self.psT = nc, m, xnT, psT
        self.bn = Count(m, tag + "_bn_partials")
        self.sums = Count(m, tag + "_sums")
        self.diff = Count(m, tag + "_square_of_difference")
        self.stats = Count(m, tag + "_mean_var")
        self.ve = Count(m, tag + "_var_eps")
        self.rstd = Count(m, tag + "_rstd")
        self.xn = Count(m, tag + "_xn")
        self.tr = Count(m, tag + "_xn_transposed")
        self.out = Count(m, tag + "_xnT")

    def dve_stats(self, eng, b):
        nc, m = self.nc, self.m
        for k in range(NT):
            last = nc.vector.bn_stats(m.st[:, k, :], m.x[:, bass.ds(b * NT + k, 1), :])
        self.bn.up(last)
        self.bn.wait(eng, b)
        nc.vector.tensor_tensor(m.sums[:, 0, :], m.st[:, :, 1], m.st[:, :, 4], ALU.add)
        nc.vector.tensor_tensor(m.sums[:, 1, :], m.st[:, :, 1], m.st[:, :, 4], ALU.subtract)
        self.sums.up(nc.vector.tensor_tensor(m.sums[:, 2, :], m.st[:, :, 2], m.st[:, :, 5], ALU.add))
        self.sums.wait(eng, b)
        nc.vector.tensor_scalar(m.mean[:, :], m.sums[:, 0, :], 0.5, None, ALU.mult)
        self.diff.up(nc.vector.scalar_tensor_tensor(m.sums[:, 3, :], m.sums[:, 1, :], 0.25, m.sums[:, 1, :],
                                                    ALU.mult, ALU.mult))
        self.diff.wait(eng, b)
        self.stats.up(nc.vector.scalar_tensor_tensor(m.var[:, :], m.sums[:, 2, :], 1.0 / D, m.sums[:, 3, :],
                                                     ALU.mult, ALU.add))

    def pool_rstd(self, eng, b):
        nc, m = self.nc, self.m
        self.stats.wait(eng, b)
        self.ve.up(nc.gpsimd.tensor_tensor(m.var_eps[:, :], m.var[:, :], m.eps[:, :], ALU.add))
        self.ve.wait(eng, b)
        self.rstd.up(nc.gpsimd.tensor_tensor(m.rstd[:, :], m.var_eps[:, :], m.neg_half[:, :], ALU.pow))

    def dve_apply(self, eng, b, first=False):
        nc, m = self.nc, self.m
        self.stats.wait(eng, b)
        self.rstd.wait(eng, b)
        if not first:
            self.tr.wait_before(eng, b)
        for k in range(NT):
            last = nc.vector.tensor_scalar(m.xn[:, k, :], m.x[:, b * NT + k, :], m.mean[:, k:k + 1],
                                           m.rstd[:, k:k + 1], ALU.subtract, ALU.mult)
        self.xn.up(last)

    def pe(self, eng, b, first=False):
        nc, m = self.nc, self.m
        self.xn.wait(eng, b)
        if not first:
            self.out.wait_before(eng, b)
        for k in range(NT):
            last = nc.tensor.transpose(self.psT[:, k * P:(k + 1) * P], m.xn[:, k, :], m.ident[:, :])
        self.tr.up(last)

    def act(self, eng, b, parity):
        self.tr.wait(eng, b)
        self.out.up(self.nc.scalar.copy(self.xnT(parity), self.psT[:, 0:L]))


def both_parities(eng, body):
    with eng.Fori(0, NB // 2) as i:
        for parity in range(2):
            body(i * 2 + parity, parity)


def moe_stage(nc, m, tag, loads_x=False):
    c = lambda name, per=1, frees=False: Count(m, f"{tag}_{name}", per, frees)
    logits, lg_c, e_done, w_done = c("logits"), c("logits_centred"), c("gate_exp"), c("weights")
    wt_ps, wt_sb, bias_ps = c("weightsT"), c("weightsT_copied"), c("bias_product")
    y, yact, ysum = c("expert_products", NT), c("y_used_by_act", NT, True), c("upper_sum", NT, True)
    added = c("tile_added", NT, True)
    bias_used = c("bias_added", 1, True)
    gate = Chain(m, f"{tag}_gate_steps", 9)
    mix = Chain(m, f"{tag}_mix_steps", NT * 4, True)
    sums = Chain(m, f"{tag}_sum_steps", 2)
    ctx = ExitStack()
    with ctx:
        sb = lambda n, s: ctx.enter_context(nc.sbuf_tensor(f"{tag}_{n}", s, F32))
        lg = sb("lg", [P, NT, NE])
        ex = sb("ex", [P, NT, NE])
        small = sb("small", [P, 8, NT])
        w = sb("w", [P, 2, NT, 32])
        wT = sb("wT", [P, P])
        upper = sb("upper", [P, 2, NE // 2, D])
        pair = sb("pair", [P, 2, 2, D])
        up1 = sb("up1", [P, 2, D])
        odd = sb("odd", [P, 2, D])
        total = sb("total", [P, 2, D])
        xnT = sb("xnT", [P, 2, L])
        psT, psG, psW, psB = m.ps[0], m.ps[1], m.ps[1], m.ps[2]
        psY = [m.ps[3:5], m.ps[5:7]]
        norm = Norm(nc, m, tag, lambda par: xnT[:, par, :], psT)
        w_zero = m.semaphore(f"{tag}_w_zeroed")

        block = ctx.enter_context(nc.Block())

        @block.gpsimd
        def _(pool):
            ysum.open(pool)
            norm.pool_rstd(pool, 0)

            def body(b, par):
                norm.pool_rstd(pool, b + 1)
                for k in range(NT):
                    q = k % 2
                    yact.wait(pool, b, k + 1)
                    sums.start(pool, b * NT + k)
                    sums.link(nc.gpsimd.tensor_tensor(pair[:, q], upper[:, q, 0:2], upper[:, q, 2:4], ALU.add))
                    sums.link(nc.gpsimd.tensor_tensor(up1[:, q], pair[:, q, 0], pair[:, q, 1], ALU.add))
                    sums.end()
                    mix.wait(pool, b, 4 * (k + 1))
                    if k >= 2:
                        added.wait(pool, b, k - 1)
                    else:
                        added.wait_before(pool, b)
                    ysum.up(nc.gpsimd.tensor_tensor(total[:, q], up1[:, q], odd[:, q], ALU.add))
            both_parities(pool, body)

        @block.vector
        def _(dve):
            mix.open(dve)
            added.open(dve)
            bias_used.open(dve)
            nc.vector.memset(w[:, :, :, :], 0.0).then_inc(w_zero, 1)
            dve.wait_ge(w_zero, 1)

            def front(b, par, first=False):
                norm.dve_stats(dve, b)
                norm.dve_apply(dve, b, first)

            def gates_in(b):
                gate.start(dve, b)
                logits.wait(dve, b)
                gate.link(nc.vector.tensor_tensor(lg[:, :, :], psG[:, 0:NT * NE].rearrange("p (k e) -> p k e", e=NE),
                                                  bc(m.gate_b[:, :], 1, NT), ALU.add))
                gate.link(nc.vector.tensor_reduce(small[:, 0, :], lg[:, :, :], AX.X, ALU.max))
                lg_c.up(nc.vector.tensor_tensor(lg[:, :, :], lg[:, :, :], bc(small[:, 0, :], 2, NE), ALU.subtract))

            def gates_out(b, par):
                e_done.wait(dve, b)
                gate.link(nc.vector.tensor_reduce(small[:, 1, :], ex[:, :, :], AX.X, ALU.add))
                gate.link(nc.vector.reciprocal(small[:, 2, :], small[:, 1, :]))
                gate.link(nc.vector.tensor_tensor(ex[:, :, :], ex[:, :, :], bc(small[:, 2, :], 2, NE), ALU.mult))
                gate.link(nc.vector.scalar_tensor_tensor(lg[:, :, :], ex[:, :, :], GATE_MIN, ex[:, :, :],
                                                         ALU.is_ge, ALU.mult))
                gate.link(nc.vector.tensor_reduce(small[:, 3, :], lg[:, :, :], AX.X, ALU.add))
                gate.link(nc.vector.scalar_tensor_tensor(small[:, 4, :], small[:, 3, :], 0.0, small[:, 3, :],
                                                         ALU.is_equal, ALU.add))
                gate.link(nc.vector.reciprocal(small[:, 5, :], small[:, 4, :]))
                w_done.up(nc.vector.scalar_tensor_tensor(w[:, par, :, 0:NE], lg[:, :, :], 0.5,
                                                         bc(small[:, 5, :], 2, NE), ALU.mult, ALU.mult))
                gate.end()

            front(0, 0, True)
            gates_in(0)
            gates_out(0, 0)

            def body(b, par):
                mix.start(dve, b)
                w_done.wait(dve, b)

                def tile(k):
                    y.wait(dve, b, k + 1)
                    if k >= 2:
                        ysum.wait(dve, b, k - 1)
                    else:
                        ysum.wait_before(dve, b)
                    xk, acc = m.x[:, b * NT + k, :], odd[:, k % 2]
                    for e in range(NE // 2):
                        ye, we = psY[k % 2][0][:, e * D:(e + 1) * D], w[:, par, k, e:e + 1]
                        if e >= 2:
                            mix.settle(back=1)
                        if e == 1:
                            mix.step(nc.vector.tensor_scalar(acc, ye, we, None, ALU.mult))
                        else:
                            into = acc if e == 3 else xk
                            mix.step(nc.vector.scalar_tensor_tensor(into, ye, we, into, ALU.mult, ALU.add))

                def finish(k):
                    mix.wait(dve, b, 4 * k + 3)
                    ysum.wait(dve, b, k + 1)
                    xk = m.x[:, b * NT + k, :]
                    added.up(nc.vector.tensor_tensor(xk, xk, total[:, k % 2], ALU.add))
                norm.dve_stats(dve, b + 1)
                tile(0)
                norm.dve_apply(dve, b + 1)
                tile(1)
                finish(0)
                gates_in(b + 1)
                tile(2)
                finish(1)
                gates_out(b + 1, 1 - par)
                tile(3)
                finish(2)
                finish(3)
                bias_ps.wait(dve, b)
                added.wait(dve, b)
                xb = m.x[:, bass.ds(b * NT, NT), :]
                bias_used.up(nc.vector.tensor_tensor(xb, xb, psB[:, :].rearrange("p (k o) -> p k o", o=D), ALU.add))
                mix.end()
            both_parities(dve, body)

        @block.scalar
        def _(act):
            yact.open(act)

            def gate_exp(b):
                lg_c.wait(act, b)
                e_done.up(nc.scalar.activation(ex[:, :, :], lg[:, :, :], ACT.Exp))
            norm.act(act, 0, 0)
            gate_exp(0)

            def body(b, par):
                w_done.wait(act, b)

                def tile(k):
                    y.wait(act, b, k + 1)
                    if k >= 2:
                        ysum.wait(act, b, k - 1)
                    else:
                        ysum.wait_before(act, b)
                    for e in range(NE // 2):
                        ins = nc.scalar.activation(upper[:, k % 2, e], psY[k % 2][1][:, e * D:(e + 1) * D],
                                                   ACT.Copy, scale=w[:, par, k, NE // 2 + e:NE // 2 + e + 1])
                    yact.up(ins)
                wt_ps.wait(act, b)
                wt_sb.up(nc.scalar.copy(wT[:, :], psW[:, 256:384]))
                tile(0)
                norm.act(act, b + 1, 1 - par)
                tile(1)
                gate_exp(b + 1)
                tile(2)
                tile(3)
            both_parities(act, body)

        @block.tensor
        def _(pe):
            def gates(b, par, first=False):
                norm.out.wait(pe, b)
                if not first:
                    wt_sb.wait_before(pe, b)
                for k in range(NT):
                    last = nc.tensor.matmul(psG[:, k * NE:(k + 1) * NE], xnT[:, par, k * P:(k + 1) * P],
                                            m.gate_w[:, :], start=True, stop=True)
                logits.up(last)
            norm.pe(pe, 0, True)
            gates(0, 0, True)

            def body(b, par):
                def tile(k):
                    if k >= 2:
                        mix.wait(pe, b, 4 * (k - 1))
                        yact.wait(pe, b, k - 1)
                    else:
                        mix.wait_before(pe, b)
                        yact.wait_before(pe, b)
                    for half in range(2):
                        last = nc.tensor.matmul(psY[k % 2][half][:, :], xnT[:, par, k * P:(k + 1) * P],
                                                m.expert_w[:, half * L:(half + 1) * L], start=True, stop=True)
                    y.up(last)
                w_done.wait(pe, b)
                wt_ps.up(nc.tensor.transpose(psW[:, 256:384], w[:, par, :, :].rearrange("p k e -> p (k e)"),
                                             m.ident[:, :]))
                tile(0)
                norm.pe(pe, b + 1)
                tile(1)
                gates(b + 1, 1 - par)
                tile(2)
                wt_sb.wait(pe, b)
                bias_used.wait_before(pe, b)
                bias_ps.up(nc.tensor.matmul(psB[:, :], wT[:, :], m.expert_b[:, :, :].rearrange("p k o -> p (k o)"),
                                            start=True, stop=True))
                tile(3)
            both_parities(pe, body)


def proto_stage(nc, m, tag):
    c = lambda name, per=1, frees=False: Count(m, f"{tag}_{name}", per, frees)
    cross, sq, pair_done, dist_done = c("cross_products"), c("xn_squares"), c("two_smallest"), c("distances")
    gap, e_done, w_done = c("distance_gap"), c("second_exp"), c("weights")
    wt_ps, wt_sb, bias_ps, bias_used = c("weightsT"), c("weightsT_copied", 1, True), c("bias_product"), c("bias_added", 1, True)
    h, hw_done, ht, ht_sb = c("down", NT), c("down_weighted", NT, True), c("downT", NT), c("downT_copied", NT, True)
    up, up_sb, o, added = c("up"), c("up_copied"), c("up_transposed"), c("x_added", 1, True)
    near = Chain(m, f"{tag}_distance_steps", 3)
    top = Chain(m, f"{tag}_nearest_steps", 16)
    ctx = ExitStack()
    with ctx:
        sb = lambda n, s: ctx.enter_context(nc.sbuf_tensor(f"{tag}_{n}", s, F32))
        scratch = sb("square_out", [P, NT, D])
        x2 = sb("x2", [P, NT])
        d2 = sb("d2", [P, NT, NPROTO])
        dist = sb("dist", [P, 2, NT])
        eq = sb("eq", [P, NT, NPROTO])
        rest = sb("rest", [P, NT, NPROTO])
        key = sb("key", [P, NT, NPROTO])
        first = sb("first", [P, NT, NPROTO])
        second = sb("second", [P, NT, NPROTO])
        small = sb("small", [P, 10, NT])
        w = sb("w", [P, NT, NPROTO])
        wT = sb("wT", [P, P])
        hw = sb("hw", [P, 2, NPROTO, RANK])
        hwT = sb("hwT", [P, NR // P, L])
        upT = sb("upT", [P, L])
        xnT = sb("xnT", [P, 2, L])
        psT, psD, psW, psB, psU = m.ps[0], m.ps[1], m.ps[1], m.ps[2], m.ps[7]
        psH, psHT = m.ps[3:5], m.ps[5:7]
        norm = Norm(nc, m, tag, lambda par: xnT[:, par, :], psT)
        block = ctx.enter_context(nc.Block())

        @block.gpsimd
        def _(pool):
            def distances(b):
                pair_done.wait(pool, b)
                dist_done.up(nc.gpsimd.tensor_tensor(dist[:, :, :], small[:, 0:3:2, :], m.half[:, :, :], ALU.pow))
            norm.pool_rstd(pool, 0)
            distances(0)

            def body(b, par):
                norm.pool_rstd(pool, b + 1)
                distances(b + 1)
            both_parities(pool, body)

        @block.vector
        def _(dve):
            def square_distance(b):
                near.start(dve, b)
                cross.wait(dve, b)
                near.link(nc.vector.scalar_tensor_tensor(d2[:, :, :], psD[:, 0:P].rearrange("p (k n) -> p k n", n=NPROTO),
                                                         -2.0, bc(m.proto_sq[:, :], 1, NT), ALU.mult, ALU.add))
                sq.wait(dve, b)
                near.link(nc.vector.tensor_tensor(d2[:, :, :], d2[:, :, :], bc(x2[:, :], 2, NPROTO), ALU.add))
                near.link(nc.vector.tensor_scalar(d2[:, :, :], d2[:, :, :], 0.0, None, ALU.max))
                near.end()

            def smallest(value, onehot, at, last):
                v, kmax = small[:, at, :], small[:, at + 1, :]
                top.link(nc.vector.tensor_reduce(v, value, AX.X, ALU.min))
                top.link(nc.vector.tensor_tensor(eq[:, :, :], value, bc(v, 2, NPROTO), ALU.is_equal))
                top.link(nc.vector.tensor_tensor(key[:, :, :], eq[:, :, :], bc(m.rank_back[:, :], 1, NT), ALU.mult))
                top.link(nc.vector.tensor_reduce(kmax, key[:, :, :], AX.X, ALU.max))
                last(nc.vector.tensor_tensor(onehot, key[:, :, :], bc(kmax, 2, NPROTO), ALU.is_equal))

            def nearest_in(b):
                top.start(dve, b)
                smallest(d2[:, :, :], first[:, :, :], 0, top.link)
                top.link(nc.vector.scalar_tensor_tensor(rest[:, :, :], first[:, :, :], BIG, d2[:, :, :], ALU.mult, ALU.add))
                smallest(rest[:, :, :], second[:, :, :], 2, pair_done.up)

            def nearest_gap(b):
                dist_done.wait(dve, b)
                gap.up(nc.vector.tensor_tensor(small[:, 4, :], dist[:, 1, :], dist[:, 0, :], ALU.subtract))

            def nearest_out(b):
                pair_done.wait(dve, b)
                e_done.wait(dve, b)
                top.link(nc.vector.tensor_scalar(small[:, 6, :], small[:, 5, :], 1.0, None, ALU.add))
                top.link(nc.vector.reciprocal(small[:, 7, :], small[:, 6, :]))
                top.step(nc.vector.tensor_scalar(small[:, 8, :], small[:, 7, :], 0.5, None, ALU.mult))
                top.link(nc.vector.scalar_tensor_tensor(small[:, 9, :], small[:, 5, :], 0.5, small[:, 7, :], ALU.mult, ALU.mult))
                top.step(nc.vector.tensor_tensor(first[:, :, :], first[:, :, :], bc(small[:, 8, :], 2, NPROTO), ALU.mult))
                top.link(nc.vector.tensor_tensor(second[:, :, :], second[:, :, :], bc(small[:, 9, :], 2, NPROTO), ALU.mult))
                top.end()
                w_done.up(nc.vector.tensor_tensor(w[:, :, :], first[:, :, :], second[:, :, :], ALU.add))

            hw_done.open(dve)
            bias_used.open(dve)
            added.open(dve)
            norm.dve_stats(dve, 0)
            norm.dve_apply(dve, 0, True)
            square_distance(0)
            nearest_in(0)
            nearest_gap(0)
            nearest_out(0)

            def body(b, par):
                def weigh(k):
                    h.wait(dve, b, k + 1)
                    if k >= 2:
                        ht.wait(dve, b, k - 1)
                    hw_done.up(nc.vector.tensor_tensor(hw[:, k % 2], psH[k % 2][:, :].rearrange("p (n r) -> p n r", r=RANK),
                                                       bc(w[:, k, :], 2, RANK), ALU.mult))
                norm.dve_stats(dve, b + 1)
                w_done.wait(dve, b)
                weigh(0)
                norm.dve_apply(dve, b + 1)
                weigh(1)
                weigh(2)
                square_distance(b + 1)
                weigh(3)
                nearest_in(b + 1)
                xb = m.x[:, bass.ds(b * NT, NT), :]
                bias_ps.wait(dve, b)
                bias_used.up(nc.vector.tensor_tensor(xb, xb, psB[:, :].rearrange("p (k o) -> p k o", o=D), ALU.add))
                nearest_gap(b + 1)
                o.wait(dve, b)
                bias_used.wait(dve, b)
                added.up(nc.vector.tensor_tensor(xb, xb, psU[:, :].rearrange("p (k o) -> p k o", o=D), ALU.add))
                nearest_out(b + 1)
            both_parities(dve, body)

        @block.scalar
        def _(act):
            def squares(b):
                norm.xn.wait(act, b)
                for k in range(NT):
                    last = nc.scalar.activation(scratch[:, k, :], m.xn[:, k, :], ACT.Square, accum_out=x2[:, k:k + 1])
                sq.up(last)

            def second_exp(b):
                gap.wait(act, b)
                e_done.up(nc.scalar.activation(small[:, 5, :], small[:, 4, :], ACT.Exp, scale=m.neg_inv_t[:, 0:1]))
            wt_sb.open(act)
            ht_sb.open(act)
            norm.act(act, 0, 0)
            squares(0)
            second_exp(0)

            def body(b, par):
                def copy_back(k):
                    ht.wait(act, b, k + 1)
                    ht_sb.up(nc.scalar.copy(hwT[:, :, k * P:(k + 1) * P],
                                            psHT[k % 2][:, :].rearrange("p (c t) -> p c t", t=P)))
                wt_ps.wait(act, b)
                wt_sb.up(nc.scalar.copy(wT[:, :], psW[:, 256:384]))
                copy_back(0)
                norm.act(act, b + 1, 1 - par)
                squares(b + 1)
                copy_back(1)
                copy_back(2)
                copy_back(3)
                second_exp(b + 1)
                up.wait(act, b)
                up_sb.up(nc.scalar.copy(upT[:, :], psU[:, :]))
            both_parities(act, body)

        @block.tensor
        def _(pe):
            def crosses(b, par):
                norm.out.wait(pe, b)
                wt_sb.wait_before(pe, b)
                for k in range(NT):
                    last = nc.tensor.matmul(psD[:, k * NPROTO:(k + 1) * NPROTO], xnT[:, par, k * P:(k + 1) * P],
                                            m.protoT[:, :], start=True, stop=True)
                cross.up(last)
            norm.pe(pe, 0, True)
            crosses(0, 0)

            def body(b, par):
                def down(k):
                    if k >= 2:
                        hw_done.wait(pe, b, k - 1)
                    else:
                        hw_done.wait_before(pe, b)
                    h.up(nc.tensor.matmul(psH[k % 2][:, :], xnT[:, par, k * P:(k + 1) * P],
                                          m.BT[:, :, :].rearrange("p c r -> p (c r)"), start=True, stop=True))

                def turn(k):
                    hw_done.wait(pe, b, k + 1)
                    if k >= 2:
                        ht_sb.wait(pe, b, k - 1)
                    else:
                        ht_sb.wait_before(pe, b)
                    flat = hw[:, k % 2].rearrange("p n r -> p (n r)")
                    for q in range(NR // P):
                        last = nc.tensor.transpose(psHT[k % 2][:, q * P:(q + 1) * P], flat[:, q * P:(q + 1) * P],
                                                   m.ident[:, :])
                    ht.up(last)
                down(0)
                down(1)
                w_done.wait(pe, b)
                wt_ps.up(nc.tensor.transpose(psW[:, 256:384], w[:, :, :].rearrange("p k n -> p (k n)"), m.ident[:, :]))
                turn(0)
                norm.pe(pe, b + 1)
                down(2)
                turn(1)
                crosses(b + 1, 1 - par)
                down(3)
                turn(2)
                wt_sb.wait(pe, b)
                bias_used.wait_before(pe, b)
                bias_ps.up(nc.tensor.matmul(psB[:, :], wT[:, :], m.proto_b[:, :, :].rearrange("p k o -> p (k o)"),
                                            start=True, stop=True))
                turn(3)
                ht_sb.wait(pe, b)
                added.wait_before(pe, b)
                for q in range(NR // P):
                    last = nc.tensor.matmul(psU[:, :], m.AT[:, q, :], hwT[:, q, :], start=(q == 0), stop=(q == NR // P - 1))
                up.up(last)
                up_sb.wait(pe, b)
                for k in range(NT):
                    last = nc.tensor.transpose(psU[:, k * P:(k + 1) * P], upT[:, k * P:(k + 1) * P], m.ident[:, :])
                o.up(last)
            both_parities(pe, body)


def latent_stage(nc, m, tag):
    NQ, NG = NT, H // HG
    NU = NQ * NG
    units = [(u // NG, u % NG) for u in range(NU)]
    c = lambda name, per=1, frees=False: Count(m, f"{tag}_{name}", per, frees)
    proj, proj_act, proj_dve = c("projections", 6), c("projections_copied_act", NG), c("projections_copied_dve", 2)
    scores, mx, exp, inv = c("scores", NU), c("row_maxima", NU), c("probabilities", NU, True), c("row_sums_inverted", NU)
    normed, turned = c("probabilities_normed", NU), c("probabilities_transposed", sum(q + 1 for q, _ in units), True)
    by_dve = [qb // 2 + 1 for qb, _ in units]
    by_act = [(qb + 1) // 2 for qb, _ in units]
    back_dve, back_act = c("pT_copied_dve", sum(by_dve), True), c("pT_copied_act", sum(by_act), True)
    z, z_sb, o, added = c("z", NU), c("z_copied", NU, True), c("attended", NQ), c("x_added", NQ, True)
    cleared = m.semaphore(f"{tag}_latent_blocks_cleared")
    done = lambda counts, u: sum(counts[:u])
    jobs = [qb + 1 for qb, _ in units]
    all_jobs = [(u, k) for u, (qb, _) in enumerate(units) for k in range(qb + 1)]
    ctx = ExitStack()
    with ctx:
        sb = lambda n, s: ctx.enter_context(nc.sbuf_tensor(f"{tag}_{n}", s, F32))
        xnT = sb("xnT", [P, 2, L])
        qT = sb("qT", [P, NG, L])
        latT = sb("latT", [P, NT, HG, P])
        lat = sb("lat", [P, 2, NT, LD])
        p = sb("p", [P, 4, HG, L])
        pT = sb("pT", [P, 2, NT, L])
        nmax = sb("nmax", [P, 2, HG])
        rsum = sb("rsum", [P, 4, HG])
        rinv = sb("rinv", [P, 4, HG])
        zT = sb("zT", [P, 2, NG, P])
        psS = m.psS
        psP, psZ, psO = m.ps[4:6], m.ps[6], m.ps[7]
        norm = Norm(nc, m, tag, lambda par: xnT[:, par, :], psO)

        def bank(u):
            return 2 * (u % 2) if units[u][0] < 2 else 0
        block = ctx.enter_context(nc.Block())

        @block.gpsimd
        def _(pool):
            norm.pool_rstd(pool, 0)

            def body(b, par):
                norm.pool_rstd(pool, b + 1)
                for u, (qb, g) in enumerate(units):
                    inv.wait(pool, b, u + 1)
                    n = (qb + 1) * P
                    pu = p[:, u % 4, :, 0:n]
                    normed.up(nc.gpsimd.tensor_tensor(pu, pu, bc(rinv[:, u % 4, :], 2, n), ALU.mult))
            both_parities(pool, body)

        @block.vector
        def _(dve):
            back_dve.open(dve)
            added.open(dve)
            nc.vector.memset(latT[:, :, :, :], 0.0).then_inc(cleared, 1)
            dve.wait_ge(cleared, 1)

            def copy_latents(b, par):
                proj.wait(dve, b, NG + 1)
                src = psP[0][:, :].rearrange("p (k t) -> p k t", t=P)
                for j in range(HG):
                    q = slice(j * LD, (j + 1) * LD)
                    last = nc.vector.tensor_copy(latT[q, :, j, :], src[q])
                proj_dve.up(last)
                proj.wait(dve, b, NG + 2)
                proj_dve.up(nc.vector.tensor_copy(lat[:, par, :, :], psP[1][:, 0:NT * LD].rearrange("p (k c) -> p k c", c=LD)))
            norm.dve_stats(dve, 0)
            norm.dve_apply(dve, 0, True)
            copy_latents(0, 0)

            def body(b, par):
                def maxima(u):
                    qb, g = units[u]
                    scores.wait(dve, b, u + 1)
                    s_u = psS[:, bank(u) * L:(bank(u) + qb + 1) * L].rearrange("p (k h t) -> p h k t", h=HG, t=P)
                    mx.up(nc.vector.tensor_reduce(nmax[:, u % 2, :], s_u, AX.XY, ALU.max, negate=True))

                def invert(u):
                    exp.wait(dve, b, u + 1)
                    inv.up(nc.vector.reciprocal(rinv[:, u % 4, :], rsum[:, u % 4, :]))

                def copy_back(u):
                    qb, g = units[u]
                    if u >= 2:
                        z.wait(dve, b, u - 1)
                    for k in range(0, qb + 1, 2):
                        n = done(jobs, u) + k
                        turned.wait(dve, b, n + 1)
                        back_dve.up(nc.vector.tensor_copy(pT[:, u % 2, k, :], psP[n % 2][:, :]))

                def add(qb):
                    o.wait(dve, b, qb + 1)
                    xq = m.x[:, b * NT + qb, :]
                    added.up(nc.vector.tensor_tensor(xq, xq, psO[:, 0:D], ALU.add))
                for s in range(NU + 3):
                    if s == 2:
                        norm.dve_stats(dve, b + 1)
                    if s == 5:
                        norm.dve_apply(dve, b + 1)
                    if s < NU:
                        maxima(s)
                    if s == NU:
                        copy_latents(b + 1, 1 - par)
                    if 1 <= s <= NU:
                        invert(s - 1)
                    if 2 <= s < NU + 2:
                        copy_back(s - 2)
                    if s >= 6 and (s - 6) % NG == 0:
                        add((s - 6) // NG)
            both_parities(dve, body)

        @block.scalar
        def _(act):
            exp.open(act)
            back_act.open(act)
            z_sb.open(act)

            def copy_queries(b):
                for g in range(NG):
                    proj.wait(act, b, g + 1)
                    proj_act.up(nc.scalar.copy(qT[:, g, :], psP[g % 2][:, :]))
            norm.act(act, 0, 0)
            copy_queries(0)

            def body(b, par):
                def exponents(u):
                    qb, g = units[u]
                    mx.wait(act, b, u + 1)
                    if u >= 4:
                        turned.wait(act, b, done(jobs, u - 3))
                    else:
                        turned.wait_before(act, b)
                    s_u = psS[:, bank(u) * L:(bank(u) + qb + 1) * L].rearrange("p (k h t) -> p h k t", h=HG, t=P)
                    for j in range(HG):
                        last = nc.scalar.activation(p[:, u % 4, j, 0:(qb + 1) * P].rearrange("p (k t) -> p k t", t=P),
                                                    s_u[:, j], ACT.Exp, bias=nmax[:, u % 2, j:j + 1],
                                                    accum_out=rsum[:, u % 4, j:j + 1])
                    exp.up(last)

                def copy_back(u):
                    qb, g = units[u]
                    if u >= 2 and qb:
                        z.wait(act, b, u - 1)
                    for k in range(1, qb + 1, 2):
                        n = done(jobs, u) + k
                        turned.wait(act, b, n + 1)
                        back_act.up(nc.scalar.copy(pT[:, u % 2, k, :], psP[n % 2][:, :]))

                def copy_z(u):
                    qb, g = units[u]
                    z.wait(act, b, u + 1)
                    if g == 0:
                        if qb >= 2:
                            o.wait(act, b, qb - 1)
                    z_sb.up(nc.scalar.copy(zT[:, qb % 2, g, :], psZ[:, 0:P]))
                for s in range(NU + 2):
                    if s == NU:
                        copy_queries(b + 1)
                    if s >= 2:
                        copy_back(s - 2)
                    if s < NU:
                        exponents(s)
                    if s >= 2:
                        copy_z(s - 2)
                    if s == 8:
                        norm.act(act, b + 1, 1 - par)
            both_parities(act, body)

        @block.tensor
        def _(pe):
            def project(b, par):
                norm.out.wait(pe, b)
                for g in range(NG):
                    if g >= 2:
                        proj_act.wait(pe, b, g - 1)
                    proj.up(nc.tensor.matmul(psP[g % 2][:, :], m.Wqk0[:, g * HG:(g + 1) * HG, :].rearrange("p h c -> p (h c)"),
                                             xnT[:, par, :], start=True, stop=True))
                proj_act.wait(pe, b, NG - 1)
                proj.up(nc.tensor.matmul(psP[0][:, :], m.Wdown[:, :, :].rearrange("p h c -> p (h c)"), xnT[:, par, :],
                                         start=True, stop=True))
                proj_act.wait(pe, b, NG)
                for k in range(NT):
                    last = nc.tensor.matmul(psP[1][:, k * LD:(k + 1) * LD], xnT[:, par, k * P:(k + 1) * P],
                                            m.Wdown[:, 0, :], start=True, stop=True)
                proj.up(last)
            turned.open(pe)
            norm.pe(pe, 0, True)
            project(0, 0)

            def body(b, par):
                def score(u):
                    qb, g = units[u]
                    if u < 2:
                        exp.wait_before(pe, b)
                    else:
                        exp.wait(pe, b, u - 1 if qb < 2 else u)
                    for k in range(qb + 1):
                        out = psS[:, (bank(u) + k) * L:(bank(u) + k + 1) * L]
                        if k == qb:
                            nc.tensor.matmul(out, m.identb[:, :], m.causal[:, :, :].rearrange("p h t -> p (h t)"),
                                             start=True, stop=False)
                        last = nc.tensor.matmul(out, qT[:, g, qb * P:(qb + 1) * P],
                                                latT[:, k, :, :].rearrange("p h t -> p (h t)"), start=(k < qb), stop=True)
                    scores.up(last)

                def turn(u):
                    qb, g = units[u]
                    normed.wait(pe, b, u + 1)
                    for k in range(qb + 1):
                        n = done(jobs, u) + k
                        if n >= 2:
                            v, kk = all_jobs[n - 2]
                            if kk % 2 == 0:
                                back_dve.wait(pe, b, done(by_dve, v) + kk // 2 + 1)
                            else:
                                back_act.wait(pe, b, done(by_act, v) + kk // 2 + 1)
                        else:
                            back_dve.wait_before(pe, b)
                            back_act.wait_before(pe, b)
                        for j in range(HG):
                            last = nc.tensor.transpose(psP[n % 2][:, j * P:(j + 1) * P], p[:, u % 4, j, k * P:(k + 1) * P],
                                                       m.ident[:, :])
                        turned.up(last)

                def attend(u):
                    qb, g = units[u]
                    back_dve.wait(pe, b, done(by_dve, u + 1))
                    if qb:
                        back_act.wait(pe, b, done(by_act, u + 1))
                    if u >= 1:
                        z_sb.wait(pe, b, u)
                    else:
                        z_sb.wait_before(pe, b)
                    for k in range(qb + 1):
                        for j in range(HG):
                            last = nc.tensor.matmul(psZ[j * LD:(j + 1) * LD, 0:P], lat[:, par, k, :],
                                                    pT[:, u % 2, k, j * P:(j + 1) * P], start=(k == 0), stop=(k == qb))
                    z.up(last)

                def project_out(qb):
                    z_sb.wait(pe, b, NG * (qb + 1))
                    if qb:
                        added.wait(pe, b, qb)
                    else:
                        added.wait_before(pe, b)
                    if qb == 1:
                        norm.out.wait(pe, b + 1)
                    for g in range(NG):
                        last = nc.tensor.matmul(psO[:, 0:D], zT[:, qb % 2, g, :], m.Wvo0[:, g, :], start=(g == 0),
                                                stop=(g == NG - 1))
                    o.up(last)
                proj_act.wait(pe, b)
                proj_dve.wait(pe, b)
                for s in range(NU + 3):
                    if s < NU:
                        score(s)
                    if s == NU:
                        back_dve.wait(pe, b, done(by_dve, NU - 2))
                        back_act.wait(pe, b, done(by_act, NU - 2))
                        project(b + 1, 1 - par)
                        proj_act.wait(pe, b + 1)
                        proj_dve.wait(pe, b + 1)
                    if 2 <= s < NU + 2:
                        turn(s - 2)
                    if s >= 6 and (s - 6) % NG == 0:
                        project_out((s - 6) // NG)
                    if 2 <= s < NU + 2:
                        attend(s - 2)
                    if s == 8:
                        added.wait(pe, b, 1)
                        norm.pe(pe, b + 1)
            both_parities(pe, body)


def local_stage(nc, m, tag):
    NBK, WB = L // P, P // QW
    NG = H // HG
    NPJ = H + NG
    c = lambda name, per=1, frees=False: Count(m, f"{tag}_{name}", per, frees)
    scores, mx, exp, inv = c("scores", H), c("row_maxima", H), c("probabilities", H, True), c("row_sums_inverted", H)
    normed, turned = c("probabilities_normed", H), c("probabilities_transposed", NBK * NG)
    back_act, back_dve = c("pT_copied_act", NBK * NG // 2, True), c("pT_copied_dve", NBK * NG // 2, True)
    proj, proj_act, proj_dve = c("projections", NPJ), c("projections_copied_act", NPJ // 2), c("projections_copied_dve", NPJ // 2)
    keys = c("windows_copied")
    z, z_act, z_dve = c("z", NBK * WB), c("z_copied_act", NBK * WB // 2), c("z_copied_dve", NBK * WB // 2)
    o, o_sb, oT, added = c("attended"), c("attended_copied"), c("attended_transposed"), c("x_added", 1, True)
    cleared = m.semaphore(f"{tag}_margins_cleared")
    ctx = ExitStack()
    with ctx:
        sb = lambda n, s: ctx.enter_context(nc.sbuf_tensor(f"{tag}_{n}", s, F32))
        xnT = sb("xnT", [P, 2, QW + L])
        kwin = sb("kwin", [P, 2, NW, KW])
        xwin = sb("xwin", [KW, 2, NW, D])
        qT = sb("qT", [P, H, L])
        p = sb("p", [P, 2, H, KW])
        pT = sb("pT", [KW, 2, H, P])
        zT = sb("zT", [P, H, L])
        ot = sb("ot", [P, L])
        nmax = sb("nmax", [P, 2, H])
        rsum = sb("rsum", [P, 2, H])
        rinv = sb("rinv", [P, 2, H])
        psS, psP, psZ = m.ps[0:4], m.ps[4:6], m.ps[6:8]
        norm = Norm(nc, m, tag, lambda par: xnT[:, par, QW - 1:QW - 1 + L], psZ[1])
        block = ctx.enter_context(nc.Block())

        @block.gpsimd
        def _(pool):
            norm.pool_rstd(pool, 0)

            def body(b, par):
                norm.pool_rstd(pool, b + 1)
                for u in range(NBK * NG):
                    bk, g = divmod(u, NG)
                    hs = slice(g * HG, (g + 1) * HG)
                    inv.wait(pool, b, u + 1)
                    normed.up(nc.gpsimd.tensor_tensor(p[:, bk % 2, hs, :], p[:, bk % 2, hs, :],
                                                      bc(rinv[:, bk % 2, hs], 2, KW), ALU.mult))
            both_parities(pool, body)

        def copy_projection(copy, b, par, n):
            if n < H:
                return copy(qT[:, n, :], psP[n % 2][:, :])
            w = (n - H) * WB
            return copy(xwin[:, par, w:w + WB, :], psP[n % 2][0:KW, :].rearrange("k (w d) -> k w d", d=D))

        @block.vector
        def _(dve):
            back_dve.open(dve)
            added.open(dve)
            nc.vector.memset(xnT[:, :, :], 0.0).then_inc(cleared, 1)

            def windows(b, par):
                norm.out.wait(dve, b)
                nc.vector.tensor_copy(kwin[:, par, :, 0:QW], xnT[:, par, 0:L].rearrange("p (w k) -> p w k", k=QW))
                nc.vector.tensor_copy(kwin[:, par, :, QW:2 * QW], xnT[:, par, QW:QW + L].rearrange("p (w k) -> p w k", k=QW))
                keys.up(nc.vector.tensor_copy(kwin[:, par, :, 2 * QW:KW], bc(xnT[:, par, QW - 1:QW], 1, NW)))

            def projections(b, par):
                for n in range(1, NPJ, 2):
                    proj.wait(dve, b, n + 1)
                    proj_dve.up(copy_projection(nc.vector.tensor_copy, b, par, n))
            norm.dve_stats(dve, 0)
            norm.dve_apply(dve, 0, True)
            windows(0, 0)
            projections(0, 0)

            def body(b, par):
                def maximum(u):
                    bk, g = divmod(u, NG)
                    scores.wait(dve, b, u + 1)
                    mx.up(nc.vector.tensor_reduce(nmax[:, bk % 2, g * HG:(g + 1) * HG],
                                                  psS[g][:, 0:HG * KW].rearrange("p (h k) -> p h k", k=KW),
                                                  AX.X, ALU.max, negate=True))

                def invert(u):
                    bk, g = divmod(u, NG)
                    exp.wait(dve, b, u + 1)
                    hs = slice(g * HG, (g + 1) * HG)
                    inv.up(nc.vector.reciprocal(rinv[:, bk % 2, hs], rsum[:, bk % 2, hs]))

                def copy_z(bk):
                    for j in range(1, WB, 2):
                        z.wait(dve, b, bk * WB + j + 1)
                        q = bk * P + j * QW
                        z_dve.up(nc.vector.tensor_copy(zT[:, :, q:q + QW], psZ[1][:, :].rearrange("p (h q) -> p h q", q=QW)))
                for bk in range(NBK):
                    maximum(bk * NG)
                    for g in range(1, NG):
                        maximum(bk * NG + g)
                        invert(bk * NG + g - 1)
                    if bk:
                        copy_z(bk - 1)
                    invert(bk * NG + NG - 1)
                    if bk == 0:
                        norm.dve_stats(dve, b + 1)
                        norm.dve_apply(dve, b + 1)
                    if bk == 2:
                        windows(b + 1, 1 - par)
                    if bk == NBK - 1:
                        projections(b + 1, 1 - par)
                    for g in range(1, NG, 2):
                        turned.wait(dve, b, bk * NG + g + 1)
                        back_dve.up(nc.vector.tensor_copy(pT[:, bk % 2, g * HG:(g + 1) * HG, :],
                                                          psP[1][0:KW, :].rearrange("k (h q) -> k h q", q=P)))
                copy_z(NBK - 1)
                oT.wait(dve, b)
                xb = m.x[:, bass.ds(b * NT, NT), :]
                added.up(nc.vector.tensor_tensor(xb, xb, psZ[0][:, :].rearrange("p (k o) -> p k o", o=D), ALU.add))
            both_parities(dve, body)

        @block.scalar
        def _(act):
            exp.open(act)
            back_act.open(act)

            def projections(b, par):
                for n in range(0, NPJ, 2):
                    proj.wait(act, b, n + 1)
                    proj_act.up(copy_projection(nc.scalar.copy, b, par, n))
            act.wait_ge(cleared, 1)
            norm.act(act, 0, 0)
            projections(0, 0)

            def body(b, par):
                def exponents(u):
                    bk, g = divmod(u, NG)
                    mx.wait(act, b, u + 1)
                    for j in range(HG):
                        h = g * HG + j
                        last = nc.scalar.activation(p[:, bk % 2, h, :], psS[g][:, j * KW:(j + 1) * KW], ACT.Exp,
                                                    bias=nmax[:, bk % 2, h:h + 1], accum_out=rsum[:, bk % 2, h:h + 1])
                    exp.up(last)

                def copy_z(bk):
                    for j in range(0, WB, 2):
                        z.wait(act, b, bk * WB + j + 1)
                        q = bk * P + j * QW
                        z_act.up(nc.scalar.copy(zT[:, :, q:q + QW], psZ[0][:, :].rearrange("p (h q) -> p h q", q=QW)))
                for bk in range(NBK):
                    for g in range(NG):
                        exponents(bk * NG + g)
                    if bk:
                        copy_z(bk - 1)
                    if bk == 1:
                        norm.act(act, b + 1, 1 - par)
                    if bk == NBK - 1:
                        projections(b + 1, 1 - par)
                    for g in range(0, NG, 2):
                        turned.wait(act, b, bk * NG + g + 1)
                        back_act.up(nc.scalar.copy(pT[:, bk % 2, g * HG:(g + 1) * HG, :],
                                                   psP[0][0:KW, :].rearrange("k (h q) -> k h q", q=P)))
                copy_z(NBK - 1)
                o.wait(act, b)
                nc.scalar.activation(ot[:, 1:L], psZ[0][:, 0:L - 1], ACT.Identity, bias=m.b_out[:, 0:1])
                o_sb.up(nc.scalar.activation(ot[:, 0:1], psZ[1][:, 0:1], ACT.Identity, bias=m.b_out[:, 0:1]))
            both_parities(act, body)

        @block.tensor
        def _(pe):
            def project(b, par):
                norm.out.wait(pe, b)
                for n in range(NPJ):
                    if n >= 2:
                        (proj_act, proj_dve)[n % 2].wait(pe, b, n // 2)
                    if n < H:
                        last = nc.tensor.matmul(psP[n % 2][:, :], m.Wqk1[:, n, :], xnT[:, par, QW:QW + L], start=True, stop=True)
                    else:
                        if n == H:
                            keys.wait(pe, b)
                        for j in range(WB):
                            last = nc.tensor.transpose(psP[n % 2][0:KW, j * D:(j + 1) * D],
                                                       kwin[:, par, (n - H) * WB + j, :], m.ident[:, :])
                    proj.up(last)
            norm.pe(pe, 0, True)
            project(0, 0)

            def body(b, par):
                def score(u):
                    bk, g = divmod(u, NG)
                    if bk:
                        exp.wait(pe, b, u - NG + 1)
                    else:
                        exp.wait_before(pe, b)
                    out = psS[g]
                    nc.tensor.matmul(out[:, 0:HG * KW], m.identb[:, :],
                                     m.window[:, min(bk, 1), :, :].rearrange("p h k -> p (h k)"),
                                     start=True, stop=False, skip_group_check=True)
                    for i in range(HG):
                        for j in range(WB):
                            q = bk * P + j * QW
                            last = nc.tensor.matmul(out[j * QW:(j + 1) * QW, i * KW:(i + 1) * KW],
                                                    qT[:, g * HG + i, q:q + QW], kwin[:, par, bk * WB + j, :],
                                                    start=False, stop=(i == HG - 1), skip_group_check=True)
                    scores.up(last)

                def turn(u):
                    bk, g = divmod(u, NG)
                    if u < 2:
                        (back_act, back_dve)[u % 2].wait_before(pe, b)
                    elif bk == NBK - 1 and g < 2:
                        (proj_act, proj_dve)[u % 2].wait(pe, b + 1)
                    else:
                        (back_act, back_dve)[u % 2].wait(pe, b, u // 2)
                    normed.wait(pe, b, u + 1)
                    for i in range(HG):
                        last = nc.tensor.transpose(psP[u % 2][0:KW, i * P:(i + 1) * P], p[:, bk % 2, g * HG + i, :],
                                                   m.ident[:, :])
                    turned.up(last)

                def attend(bk):
                    back_act.wait(pe, b, (bk + 1) * NG // 2)
                    back_dve.wait(pe, b, (bk + 1) * NG // 2)
                    if bk == 0:
                        added.wait_before(pe, b)
                    if bk == 1:
                        norm.out.wait(pe, b + 1)
                    for j in range(WB):
                        n = bk * WB + j
                        if n >= 2:
                            (z_act, z_dve)[j % 2].wait(pe, b, n // 2)
                        z.up(nc.tensor.matmul(psZ[j % 2][:, :], xwin[:, par, n, :], pT[:, bk % 2, :, j * QW:(j + 1) * QW],
                                              start=True, stop=True))
                for bk in range(NBK):
                    for g in range(NG):
                        score(bk * NG + g)
                    if bk:
                        attend(bk - 1)
                    if bk == 1:
                        z_dve.wait(pe, b, WB // 2)
                        norm.pe(pe, b + 1)
                    if bk == NBK - 1:
                        back_act.wait(pe, b, (NBK - 1) * NG // 2)
                        back_dve.wait(pe, b, (NBK - 1) * NG // 2)
                        project(b + 1, 1 - par)
                    for g in range(NG):
                        turn(bk * NG + g)
                attend(NBK - 1)
                z_act.wait(pe, b)
                z_dve.wait(pe, b)
                for h in range(H):
                    nc.tensor.matmul(psZ[0][:, :], m.M1[:, h, :], zT[:, h, :], start=(h == 0), stop=(h == H - 1))
                o.up(nc.tensor.matmul(psZ[1][:, 0:2], m.M_first[:, :], xnT[:, par, QW - 1:QW + 1], start=True, stop=True))
                o_sb.wait(pe, b)
                for k in range(NT):
                    last = nc.tensor.transpose(psZ[0][:, k * D:(k + 1) * D], ot[:, k * P:(k + 1) * P], m.ident[:, :])
                oT.up(last)
            both_parities(pe, body)


def program(nc, x_in, Wq0, Wkv_down, Wk_up, Wv_up, Wout0, gate_w, gate_b, expert_w, expert_b,
            w_qkv, w_out, b_out, w_th, prototypes, Bf, Af, bias1, temp, out):
    ctx = ExitStack()
    with ctx:
        class m:
            in_stage = []

            @classmethod
            def semaphore(cls, name):
                cls.in_stage.append(nc.alloc_semaphore(name))
                return cls.in_stage[-1]

            @classmethod
            def end_stage(cls):
                nc.clear_and_free_semaphores(cls.in_stage)
                nc.all_engine_barrier()
                cls.in_stage = []
        sb = lambda n, s, dt=F32: ctx.enter_context(nc.sbuf_tensor(n, s, dt))
        m.x = sb("x_res", [P, (NB + 1) * NT, D])
        m.ident = sb("ident", [P, P])
        m.neg_half = sb("neg_half", [P, NT])
        m.xn = sb("xn", [P, NT, D])
        m.st = sb("st", [P, NT, 6])
        m.sums = sb("sums", [P, 4, NT])
        m.mean = sb("mean", [P, NT])
        m.var = sb("var", [P, NT])
        m.eps = sb("eps", [P, NT])
        m.var_eps = sb("var_eps", [P, NT])
        m.rstd = sb("rstd", [P, NT])
        m.gate_w = sb("gate_w", [P, NE])
        m.gate_b = sb("gate_b", [P, NE])
        m.expert_w = sb("expert_w", [P, NE * D])
        m.expert_b = sb("expert_b", [P, NT, D])
        m.half = sb("half", [P, 2, NT])
        m.rank_back = sb("rank_back", [P, NPROTO])
        m.protoT = sb("protoT", [P, NPROTO])
        m.proto_sq = sb("proto_sq", [P, NPROTO])
        m.proto_b = sb("proto_b", [P, NT, D])
        m.neg_inv_t = sb("neg_inv_t", [P, 1])
        m.BT = sb("BT", [P, NR // P, P])
        m.AT = sb("AT", [P, NR // P, D])
        m.Wqk0 = sb("Wqk0", [P, H, LD])
        m.Wvo0 = sb("Wvo0", [P, H // HG, D])
        m.Wdown = sb("Wdown", [P, HG, LD])
        m.Wqk1 = sb("Wqk1", [P, H, D])
        m.M1 = sb("M1", [P, H, D])
        m.M_first = sb("M_first", [P, D])
        m.b_out = sb("b_out", [P, 1])
        m.identb = sb("identb", [P, P], BF16)
        m.causal = sb("causal", [P, HG, P], BF16)
        m.window = sb("window", [P, 2, HG, KW], BF16)
        m.psS = ctx.enter_context(nc.psum_tensor("banks0to3", [P, 4 * 512], F32))
        m.ps = [m.psS[:, i * 512:(i + 1) * 512] for i in range(4)]
        m.ps += [ctx.enter_context(nc.psum_tensor(f"bank{i}", [P, 512], F32))[:, :] for i in range(4, 8)]

        x_view = x_in.rearrange("b (k p) d -> p (b k) d", p=P)
        out_view = out.rearrange("b (k p) d -> p (b k) d", p=P)
        prep_stage(nc, m, locals())
        m.end_stage()
        for n, kind in enumerate(STAGES):
            {"A": moe_stage, "D": proto_stage, "B": latent_stage, "E": local_stage}[kind](nc, m, f"s{n}")
            m.end_stage()
        stored = nc.alloc_semaphore("stored")
        with nc.Block() as block:
            @block.sync
            def _(sp):
                for q in range(4):
                    sp.dma_start(out_view[:, q * 16:(q + 1) * 16, :], m.x[:, q * 16:(q + 1) * 16, :]).then_inc(stored, 16)
                sp.wait_ge(stored, 64)


def prep_stage(nc, m, a):
    def sem(name):
        return m.semaphore("prep_" + name)
    loaded, bias_loaded, x_loaded = sem("weights_loaded"), sem("biases_loaded"), sem("x_loaded")
    cleared, filled, ident_ready = sem("cleared"), sem("filled"), sem("ident_ready")
    masks0, masks1, masks2, masks_ready = sem("masks_cleared"), sem("masks_causal"), sem("masks_rows"), sem("masks_ready")
    turned, copied = sem("transposed"), sem("transposes_copied")
    small_steps, sq_ready, scaled, scaled_used = sem("small_steps"), sem("proto_squared"), sem("wout_scaled"), sem("wout_scaled_used")
    products, products_copied, folded = sem("products"), sem("products_copied"), sem("folded")
    NC = H // 2
    ctx = ExitStack()
    with ctx:
        sb = lambda n, s, dt=F32: ctx.enter_context(nc.sbuf_tensor("prep_" + n, s, dt))
        wqkv = sb("wqkv", [P, 3, NC, P])
        wo1 = sb("wo1", [P, NC, D])
        wo0 = sb("wo0", [P, NC, D])
        wq0 = sb("wq0", [P, NC, P])
        wku = sb("wku", [LD, NC, P])
        wvu = sb("wvu", [LD, NC, P])
        Bn = sb("Bn", [P, NR // P, P])
        An = sb("An", [P, NR])
        protos = sb("protos", [NPROTO, P])
        t = sb("temp", [P, 3])
        th = sb("th", [P, NC, H])
        T1 = sb("T1", [P, 3, NC, P])
        T0q = sb("T0q", [P, NC, P])
        T0k = sb("T0k", [P, NC, LD])
        T0v = sb("T0v", [P, NC, LD])
        proto2 = sb("proto2", [P, NPROTO])
        ones = sb("ones", [P, P])
        causal = sb("causal", [P, HG, P])
        window = sb("window", [P, 2, HG, KW])
        back = sb("rank_int", [P, NPROTO], mybir.dt.int32)
        wsc = sb("wo1_scaled", [P, 2, H, D])

        groups = []
        for w in range(3):
            for half in range(2):
                q = slice(half * 4, half * 4 + 4)
                groups.append((T1[:, w, q, :], [wqkv[:, w, c, :] for c in range(8)[q]]))
        for half in range(2):
            q = slice(half * 4, half * 4 + 4)
            groups.append((T0q[:, q, :], [wq0[:, c, :] for c in range(8)[q]]))
        groups.append((T0k[:, :, :], [wku[:, c, :] for c in range(NC)]))
        groups.append((T0v[:, :, :], [wvu[:, c, :] for c in range(NC)]))
        groups.append((m.BT[:, :, :], [Bn[:, c, :] for c in range(NR // P)]))
        groups.append((m.AT[:, :, :], [An[:, c * P:(c + 1) * P] for c in range(NR // P)]))
        groups.append((m.protoT[:, :], [protos[:, :]]))

        block = ctx.enter_context(nc.Block())

        @block.sync
        def _(sp):
            loads = [(wqkv[:, w, :, :].rearrange("p c n -> p (c n)"), a["w_qkv"][:, w * H * HD:(w + 1) * H * HD])
                     for w in range(3)]
            loads += [
                (wq0[:, :, :].rearrange("p c n -> p (c n)"), a["Wq0"].rearrange("d h k -> d (h k)")),
                (wku[:, :, :].rearrange("p c n -> p (c n)"), a["Wk_up"].rearrange("d h k -> d (h k)")),
                (wvu[:, :, :].rearrange("p c n -> p (c n)"), a["Wv_up"].rearrange("d h k -> d (h k)")),
                (Bn[:, :, :], a["Bf"].rearrange("n r i -> (n r) i").rearrange("(c p) i -> p c i", p=P)),
                (An[:, :].rearrange("o (n r) -> o n r", r=RANK), a["Af"].rearrange("n o r -> o n r")),
                (protos[:, :], a["prototypes"]),
                (wo0[:, :, :], a["Wout0"].rearrange("h k o -> (h k) o").rearrange("(c p) o -> p c o", p=P)),
                (wo1[:, :, :], a["w_out"].rearrange("(c p) o -> p c o", p=P)),
                (m.Wdown[:, :, :], bc(a["Wkv_down"], 1, HG)),
                (m.gate_w[:, :], a["gate_w"]),
                (m.gate_b[:, :], a["gate_b"].partition_broadcast(P)),
                (m.expert_w[:, :].rearrange("d (e o) -> d e o", o=D), a["expert_w"].rearrange("e d o -> d e o")),
                (m.b_out[:, :], a["b_out"].rearrange("(o u) -> o u", u=1)),
                (t[:, 0:1], a["temp"].partition_broadcast(P)),
            ]
            w_th = a["w_th"].rearrange("(c s) h -> s c h", s=2)
            loads += [(th[s * HD:(s + 1) * HD, :, :], w_th[s].partition_broadcast(HD)) for s in range(2)]
            for dst, src in loads:
                sp.dma_start(dst, src).then_inc(loaded, 16)
            m.n_loads = len(loads)
            sp.wait_ge(cleared, 2)
            for k in range(NT):
                sp.dma_start(m.expert_b[32 * k:32 * k + NE, k, :], a["expert_b"]).then_inc(bias_loaded, 16)
                sp.dma_start(m.proto_b[32 * k:32 * k + NPROTO, k, :], a["bias1"]).then_inc(bias_loaded, 16)
            for q in range(4):
                sp.dma_start(m.x[:, q * 16:(q + 1) * 16, :], a["x_view"][:, q * 16:(q + 1) * 16, :]).then_inc(x_loaded, 16)
            sp.wait_ge(bias_loaded, 2 * NT * 16)
            sp.wait_ge(x_loaded, 64)

        @block.gpsimd
        def _(pool):
            for tile, value in ((m.ident[:, :], 0.0), (m.neg_half[:, :], -0.5), (m.eps[:, :], EPS),
                                (m.half[:, :, :], 0.5), (ones[:, :], 1.0), (m.x[:, NB * NT:, :], 0.0)):
                nc.gpsimd.memset(tile, value).then_inc(filled, 1)
            nc.gpsimd.memset(m.expert_b[:, :, :], 0.0).then_inc(cleared, 1)
            nc.gpsimd.memset(m.proto_b[:, :, :], 0.0).then_inc(cleared, 1)
            nc.gpsimd.memset(causal[:, :, :], 0.0).then_inc(masks0, 1)
            nc.gpsimd.memset(window[:, :, :, :], 0.0).then_inc(masks0, 1)
            pool.wait_ge(filled, 6)
            nc.gpsimd.affine_select(out=m.ident[:, :], in_=m.ident[:, :], compare_op=ALU.not_equal, fill=1.0,
                                    base=0, pattern=[[-1, P]], channel_multiplier=1).then_inc(ident_ready, 1)
            pool.wait_ge(ident_ready, 1)
            pool.wait_ge(masks0, 2)
            nc.gpsimd.affine_select(out=causal[:, :, :], in_=causal[:, :, :], compare_op=ALU.is_ge, fill=MASKED,
                                    base=0, pattern=[[0, HG], [-1, P]], channel_multiplier=1).then_inc(masks1, 1)
            for j in range(P // QW):
                q = slice(j * QW, (j + 1) * QW)
                pool.wait_ge(masks1, 1 + 2 * j)
                own = window[q, :, :, QW:2 * QW].rearrange("p a h k -> p (a h) k")
                nc.gpsimd.affine_select(out=own, in_=own, compare_op=ALU.is_ge, fill=MASKED,
                                        base=0, pattern=[[0, 2 * HG], [-1, QW]], channel_multiplier=1).then_inc(masks1, 1)
                pool.wait_ge(masks1, 2 + 2 * j)
                top = window[q, :, :, 0:16].rearrange("p a h k -> p (a h) k")
                nc.gpsimd.affine_select(out=top, in_=top, compare_op=ALU.is_ge, fill=MASKED,
                                        base=15, pattern=[[0, 2 * HG], [0, 16]], channel_multiplier=-1).then_inc(masks1, 1)
            pool.wait_ge(masks1, 1 + 2 * (P // QW))
            nc.gpsimd.memset(window[0:QW, 0, :, 0:QW], MASKED).then_inc(masks2, 1)
            nc.gpsimd.iota(back[:, :], pattern=[[-1, NPROTO]], base=NPROTO, channel_multiplier=0).then_inc(masks2, 1)
            pool.wait_ge(masks2, 2)
            pool.wait_ge(ident_ready, 1)
            nc.gpsimd.tensor_copy(m.causal[:, :, :], causal[:, :, :]).then_inc(masks_ready, 1)
            nc.gpsimd.tensor_copy(m.window[:, :, :, :], window[:, :, :, :]).then_inc(masks_ready, 1)
            nc.gpsimd.tensor_copy(m.identb[:, :], m.ident[:, :]).then_inc(masks_ready, 1)
            nc.gpsimd.tensor_copy(m.rank_back[:, :], back[:, :]).then_inc(masks_ready, 1)

        @block.vector
        def _(dve):
            dve.wait_ge(loaded, 16 * m.n_loads)
            nc.vector.tensor_scalar(t[:, 1:2], t[:, 0:1], -1.0, None, ALU.mult).then_inc(small_steps, 1)
            dve.wait_ge(small_steps, 1)
            nc.vector.tensor_tensor(t[:, 1:2], t[:, 0:1], t[:, 1:2], ALU.max).then_inc(small_steps, 1)
            dve.wait_ge(small_steps, 2)
            nc.vector.tensor_scalar(t[:, 1:2], t[:, 1:2], 0.1, -1.0, ALU.max, ALU.mult).then_inc(small_steps, 1)
            dve.wait_ge(small_steps, 3)
            nc.vector.reciprocal(m.neg_inv_t[:, :], t[:, 1:2])
            dve.wait_ge(copied, len(groups))
            nc.vector.tensor_tensor(proto2[:, :], m.protoT[:, :], m.protoT[:, :], ALU.mult).then_inc(sq_ready, 1)
            for c in range(NC):
                if c >= 2:
                    dve.wait_ge(scaled_used, c - 1)
                nc.vector.tensor_tensor(wsc[:, c % 2], bc(th[:, c, :], 2, D), bc(wo1[:, c, :], 1, H), ALU.mult)\
                  .then_inc(scaled, 1)

        @block.scalar
        def _(act):
            for n, (dst, srcs) in enumerate(groups):
                act.wait_ge(turned, n + 1)
                rows = sum(x.shape[0] for x in srcs)
                src = m.ps[n % 8][:, 0:rows]
                if len(dst.shape) == 3:
                    src = src.rearrange("p (c n) -> p c n", c=len(srcs))
                nc.scalar.copy(dst, src).then_inc(copied, 1)
            Wqk1 = m.Wqk1[:, :, :].rearrange("p (q c s) n -> p q c s n", s=2, c=4)
            Wqk0 = m.Wqk0[:, :, :].rearrange("p (c s) n -> p c s n", s=2)
            act.wait_ge(products, 8)
            for s in range(2):
                for q in range(2):
                    nc.scalar.mul(Wqk1[:, q, :, s, :], m.ps[2 * s + q][:, :].rearrange("p (c n) -> p c n", c=4), HD ** -0.5)
                nc.scalar.mul(Wqk0[:, :, s, :], m.ps[4 + s][:, 0:NC * LD].rearrange("p (c n) -> p c n", c=NC), HD ** -0.5)
            for j in range(HG):
                q = slice(j * LD, (j + 1) * LD)
                last = nc.scalar.copy(m.Wvo0[q, :, :], m.ps[6 + j % 2][q, :].rearrange("p (g o) -> p g o", o=D))
            last.then_inc(products_copied, 1)
            act.wait_ge(folded, 1)
            for j in range(4):
                nc.scalar.copy(m.M1[:, j * 4:(j + 1) * 4, :], m.ps[j][:, :].rearrange("p (h o) -> p h o", o=D))
            nc.scalar.copy(m.M_first[:, :], m.ps[4][:, 0:D])
            nc.scalar.copy(m.proto_sq[:, :], m.ps[5][:, 0:NPROTO])

        @block.tensor
        def _(pe):
            pe.wait_ge(loaded, 16 * m.n_loads)
            pe.wait_ge(ident_ready, 1)
            for n, (dst, srcs) in enumerate(groups):
                if n >= 8:
                    pe.wait_ge(copied, n - 7)
                rows = srcs[0].shape[0]
                for j, src in enumerate(srcs):
                    last = nc.tensor.transpose(m.ps[n % 8][:, j * rows:(j + 1) * rows], src, m.ident[0:rows, 0:rows])
                last.then_inc(turned, 1)
            pe.wait_ge(copied, len(groups))
            for s in range(2):
                k = slice(s * HD, (s + 1) * HD)
                for q in range(2):
                    for j in range(4):
                        c = 4 * q + j
                        last = nc.tensor.matmul(m.ps[2 * s + q][:, j * P:(j + 1) * P], T1[k, 0, c, :], T1[k, 1, c, :],
                                                start=True, stop=True)
                    last.then_inc(products, 1)
                for c in range(NC):
                    last = nc.tensor.matmul(m.ps[4 + s][:, c * LD:(c + 1) * LD], T0q[k, c, :], T0k[k, c, :],
                                            start=True, stop=True)
                last.then_inc(products, 1)
                for c in range(NC):
                    j, g = (2 * c + s) % HG, (2 * c + s) // HG
                    last = nc.tensor.matmul(m.ps[6 + s][j * LD:(j + 1) * LD, g * D:(g + 1) * D], T0v[k, c, :],
                                            wo0[k, c, :], start=True, stop=True)
                last.then_inc(products, 1)
            pe.wait_ge(products_copied, 1)
            pe.wait_ge(sq_ready, 1)
            pe.wait_ge(filled, 6)
            nc.tensor.matmul(m.ps[5][:, 0:NPROTO], ones[:, :], proto2[:, :], start=True, stop=True)
            for c in range(NC):
                nc.tensor.matmul(m.ps[4][:, 0:D], T1[:, 2, c, :], wo1[:, c, :], start=(c == 0), stop=(c == NC - 1))
                pe.wait_ge(scaled, c + 1)
                for j in range(4):
                    last = nc.tensor.matmul(m.ps[j][:, :], T1[:, 2, c, :],
                                            wsc[:, c % 2, j * 4:(j + 1) * 4, :].rearrange("p h o -> p (h o)"),
                                            start=(c == 0), stop=(c == NC - 1))
                last.then_inc(scaled_used, 1)
            pe.wait_ge(scaled_used, NC)
            pe.sem_inc(folded, 1)


_INS = ['L0_attn_x_bld', 'L0_attn_Wq', 'L0_attn_Wkv_down', 'L0_attn_Wk_up', 'L0_attn_Wv_up', 'L0_attn_Wout',
        'L0_ffn_gate_w', 'L0_ffn_gate_b', 'L0_ffn_expert_w', 'L0_ffn_expert_b', 'L1_attn_w_qkv', 'L1_attn_w_out',
        'L1_attn_b_out', 'L1_attn_w_th', 'L1_ffn_prototypes', 'L1_ffn_B', 'L1_ffn_A', 'L1_ffn_bias', 'L1_ffn_temp']


def kernel(**inputs):
    import numpy as _np
    import concourse.bacc as _bacc
    from concourse import mybir as _mybir
    from concourse.bass_utils import run_bass_kernel_spmd as _run

    nc = _bacc.Bacc("TRN2", target_bir_lowering=False, num_devices=1)
    arrays, args = {}, []
    for name in _INS:
        a = _np.ascontiguousarray(inputs[name])
        if name == 'L1_ffn_temp':
            a = a.reshape(1)
        arrays[f"in_{name}"] = a
        args.append(nc.dram_tensor(f"in_{name}", a.shape, _mybir.dt.from_np(a.dtype), kind="ExternalInput").ap())
    out = nc.dram_tensor("out", (NB, L, D), F32, kind="ExternalOutput").ap()
    program(nc, *args, out)
    r = _run(nc, [arrays], core_ids=[0])
    return r.results[0]["out"]
```

```python
import concourse.bass as bass
from concourse import mybir
from contextlib import ExitStack

F32 = mybir.dt.float32
BF16 = mybir.dt.bfloat16
F32R = mybir.dt.float32r
ALU = mybir.AluOpType
ACT = mybir.ActivationFunctionType
AX = mybir.AxisListType

P = 128
NB, L, D = 16, 512, 128
NT = L // P
H, HD = 16, 64
HG = 4
NE = 8
LD = 32
NPROTO, RANK = 32, 16
NR = NPROTO * RANK
QW = 32
NW = L // QW
KW = 65
EPS = 1e-5
GATE_MIN = 0.1
MASKED = -1e30
BIG = 1e30
STAGES = "ABADED"


def bc(ap, dim, n):
    shape = list(ap.shape)
    return ap.unsqueeze(dim).broadcast_to(shape[:dim] + [n] + shape[dim:])


class Count:

    def __init__(self, m, name, per=1, frees=False):
        self.sem, self.per, self.base = m.semaphore(name), per, int(frees)

    def open(self, eng):
        assert self.base == 1
        eng.sem_inc(self.sem, 1)

    def wait(self, eng, batch, k=None):
        k = self.per if k is None else k
        eng.wait_ge(self.sem, batch * self.per + (k + self.base))

    def wait_before(self, eng, batch):
        eng.wait_ge(self.sem, batch * self.per + self.base)

    def up(self, ins):
        return ins.then_inc(self.sem, 1)


class Chain(Count):

    def start(self, eng, batch):
        self.eng, self.batch, self.n = eng, batch, 0

    def step(self, ins):
        self.n += 1
        self.up(ins)

    def settle(self, back=0):
        self.wait(self.eng, self.batch, self.n - back)

    def link(self, ins):
        self.step(ins)
        self.settle()

    def end(self):
        assert self.n == self.per, (self.n, self.per)


class Norm:

    def __init__(self, nc, m, tag, xnT, psT):
        self.nc, self.m, self.xnT, self.psT = nc, m, xnT, psT
        self.bn = Count(m, tag + "_bn_partials")
        self.sums = Count(m, tag + "_sums")
        self.diff = Count(m, tag + "_square_of_difference")
        self.stats = Count(m, tag + "_mean_var")
        self.ve = Count(m, tag + "_var_eps")
        self.rstd = Count(m, tag + "_rstd")
        self.xn = Count(m, tag + "_xn")
        self.tr = Count(m, tag + "_xn_transposed")
        self.out = Count(m, tag + "_xnT")

    def dve_stats(self, eng, b):
        nc, m = self.nc, self.m
        for k in range(NT):
            last = nc.vector.bn_stats(m.st[:, k, :], m.x[:, bass.ds(b * NT + k, 1), :])
        self.bn.up(last)
        self.bn.wait(eng, b)
        nc.vector.tensor_tensor(m.sums[:, 0, :], m.st[:, :, 1], m.st[:, :, 4], ALU.add)
        nc.vector.tensor_tensor(m.sums[:, 1, :], m.st[:, :, 1], m.st[:, :, 4], ALU.subtract)
        self.sums.up(nc.vector.tensor_tensor(m.sums[:, 2, :], m.st[:, :, 2], m.st[:, :, 5], ALU.add))
        self.sums.wait(eng, b)
        nc.vector.tensor_scalar(m.mean[:, :], m.sums[:, 0, :], 0.5, None, ALU.mult)
        self.diff.up(nc.vector.scalar_tensor_tensor(m.sums[:, 3, :], m.sums[:, 1, :], 0.25, m.sums[:, 1, :],
                                                    ALU.mult, ALU.mult))
        self.diff.wait(eng, b)
        self.stats.up(nc.vector.scalar_tensor_tensor(m.var[:, :], m.sums[:, 2, :], 1.0 / D, m.sums[:, 3, :],
                                                     ALU.mult, ALU.add))

    def pool_rstd(self, eng, b):
        nc, m = self.nc, self.m
        self.stats.wait(eng, b)
        self.ve.up(nc.gpsimd.tensor_tensor(m.var_eps[:, :], m.var[:, :], m.eps[:, :], ALU.add))
        self.ve.wait(eng, b)
        self.rstd.up(nc.gpsimd.tensor_tensor(m.rstd[:, :], m.var_eps[:, :], m.neg_half[:, :], ALU.pow))

    def dve_apply(self, eng, b, first=False):
        nc, m = self.nc, self.m
        self.stats.wait(eng, b)
        self.rstd.wait(eng, b)
        if not first:
            self.tr.wait_before(eng, b)
        for k in range(NT):
            last = nc.vector.tensor_scalar(m.xn[:, k, :], m.x[:, b * NT + k, :], m.mean[:, k:k + 1],
                                           m.rstd[:, k:k + 1], ALU.subtract, ALU.mult)
        self.xn.up(last)

    def pe(self, eng, b, first=False):
        nc, m = self.nc, self.m
        self.xn.wait(eng, b)
        if not first:
            self.out.wait_before(eng, b)
        for k in range(NT):
            last = nc.tensor.transpose(self.psT[:, k * P:(k + 1) * P], m.xn[:, k, :], m.ident[:, :])
        self.tr.up(last)

    def act(self, eng, b, parity):
        self.tr.wait(eng, b)
        self.out.up(self.nc.scalar.copy(self.xnT(parity), self.psT[:, 0:L]))


def both_parities(eng, body):
    with eng.Fori(0, NB // 2) as i:
        for parity in range(2):
            body(i * 2 + parity, parity)


def moe_stage(nc, m, tag, loads_x=False):
    c = lambda name, per=1, frees=False: Count(m, f"{tag}_{name}", per, frees)
    logits, lg_c, e_done, w_done = c("logits"), c("logits_centred"), c("gate_exp"), c("weights")
    wt_ps, wt_sb, bias_ps = c("weightsT"), c("weightsT_copied"), c("bias_product")
    y, yact, ysum = c("expert_products", NT), c("y_used_by_act", NT, True), c("upper_sum", NT, True)
    added = c("tile_added", NT, True)
    bias_used = c("bias_added", 1, True)
    gate = Chain(m, f"{tag}_gate_steps", 9)
    mix = Chain(m, f"{tag}_mix_steps", NT * 4, True)
    sums = Chain(m, f"{tag}_sum_steps", 2)
    ctx = ExitStack()
    with ctx:
        sb = lambda n, s: ctx.enter_context(nc.sbuf_tensor(f"{tag}_{n}", s, F32))
        lg = sb("lg", [P, NT, NE])
        ex = sb("ex", [P, NT, NE])
        small = sb("small", [P, 8, NT])
        w = sb("w", [P, 2, NT, 32])
        wT = sb("wT", [P, P])
        upper = sb("upper", [P, 2, NE // 2, D])
        pair = sb("pair", [P, 2, 2, D])
        up1 = sb("up1", [P, 2, D])
        odd = sb("odd", [P, 2, D])
        total = sb("total", [P, 2, D])
        xnT = sb("xnT", [P, 2, L])
        psT, psG, psW, psB = m.ps[0], m.ps[1], m.ps[1], m.ps[2]
        psY = [m.ps[3:5], m.ps[5:7]]
        norm = Norm(nc, m, tag, lambda par: xnT[:, par, :], psT)
        w_zero = m.semaphore(f"{tag}_w_zeroed")

        block = ctx.enter_context(nc.Block())

        @block.gpsimd
        def _(pool):
            ysum.open(pool)
            norm.pool_rstd(pool, 0)

            def body(b, par):
                norm.pool_rstd(pool, b + 1)
                for k in range(NT):
                    q = k % 2
                    yact.wait(pool, b, k + 1)
                    sums.start(pool, b * NT + k)
                    sums.link(nc.gpsimd.tensor_tensor(pair[:, q], upper[:, q, 0:2], upper[:, q, 2:4], ALU.add))
                    sums.link(nc.gpsimd.tensor_tensor(up1[:, q], pair[:, q, 0], pair[:, q, 1], ALU.add))
                    sums.end()
                    mix.wait(pool, b, 4 * (k + 1))
                    if k >= 2:
                        added.wait(pool, b, k - 1)
                    else:
                        added.wait_before(pool, b)
                    ysum.up(nc.gpsimd.tensor_tensor(total[:, q], up1[:, q], odd[:, q], ALU.add))
            both_parities(pool, body)

        @block.vector
        def _(dve):
            mix.open(dve)
            added.open(dve)
            bias_used.open(dve)
            nc.vector.memset(w[:, :, :, :], 0.0).then_inc(w_zero, 1)
            dve.wait_ge(w_zero, 1)

            def front(b, par, first=False):
                norm.dve_stats(dve, b)
                norm.dve_apply(dve, b, first)

            def gates_in(b):
                gate.start(dve, b)
                logits.wait(dve, b)
                gate.link(nc.vector.tensor_tensor(lg[:, :, :], psG[:, 0:NT * NE].rearrange("p (k e) -> p k e", e=NE),
                                                  bc(m.gate_b[:, :], 1, NT), ALU.add))
                gate.link(nc.vector.tensor_reduce(small[:, 0, :], lg[:, :, :], AX.X, ALU.max))
                lg_c.up(nc.vector.tensor_tensor(lg[:, :, :], lg[:, :, :], bc(small[:, 0, :], 2, NE), ALU.subtract))

            def gates_out(b, par):
                e_done.wait(dve, b)
                gate.link(nc.vector.tensor_reduce(small[:, 1, :], ex[:, :, :], AX.X, ALU.add))
                gate.link(nc.vector.reciprocal(small[:, 2, :], small[:, 1, :]))
                gate.link(nc.vector.tensor_tensor(ex[:, :, :], ex[:, :, :], bc(small[:, 2, :], 2, NE), ALU.mult))
                gate.link(nc.vector.scalar_tensor_tensor(lg[:, :, :], ex[:, :, :], GATE_MIN, ex[:, :, :],
                                                         ALU.is_ge, ALU.mult))
                gate.link(nc.vector.tensor_reduce(small[:, 3, :], lg[:, :, :], AX.X, ALU.add))
                gate.link(nc.vector.scalar_tensor_tensor(small[:, 4, :], small[:, 3, :], 0.0, small[:, 3, :],
                                                         ALU.is_equal, ALU.add))
                gate.link(nc.vector.reciprocal(small[:, 5, :], small[:, 4, :]))
                w_done.up(nc.vector.scalar_tensor_tensor(w[:, par, :, 0:NE], lg[:, :, :], 0.5,
                                                         bc(small[:, 5, :], 2, NE), ALU.mult, ALU.mult))
                gate.end()

            front(0, 0, True)
            gates_in(0)
            gates_out(0, 0)

            def body(b, par):
                mix.start(dve, b)
                w_done.wait(dve, b)

                def tile(k):
                    y.wait(dve, b, k + 1)
                    if k >= 2:
                        ysum.wait(dve, b, k - 1)
                    else:
                        ysum.wait_before(dve, b)
                    xk, acc = m.x[:, b * NT + k, :], odd[:, k % 2]
                    for e in range(NE // 2):
                        ye, we = psY[k % 2][0][:, e * D:(e + 1) * D], w[:, par, k, e:e + 1]
                        if e >= 2:
                            mix.settle(back=1)
                        if e == 1:
                            mix.step(nc.vector.tensor_scalar(acc, ye, we, None, ALU.mult))
                        else:
                            into = acc if e == 3 else xk
                            mix.step(nc.vector.scalar_tensor_tensor(into, ye, we, into, ALU.mult, ALU.add))

                def finish(k):
                    mix.wait(dve, b, 4 * k + 3)
                    ysum.wait(dve, b, k + 1)
                    xk = m.x[:, b * NT + k, :]
                    added.up(nc.vector.tensor_tensor(xk, xk, total[:, k % 2], ALU.add))
                norm.dve_stats(dve, b + 1)
                tile(0)
                norm.dve_apply(dve, b + 1)
                tile(1)
                finish(0)
                gates_in(b + 1)
                tile(2)
                finish(1)
                gates_out(b + 1, 1 - par)
                tile(3)
                finish(2)
                finish(3)
                bias_ps.wait(dve, b)
                added.wait(dve, b)
                xb = m.x[:, bass.ds(b * NT, NT), :]
                bias_used.up(nc.vector.tensor_tensor(xb, xb, psB[:, :].rearrange("p (k o) -> p k o", o=D), ALU.add))
                mix.end()
            both_parities(dve, body)

        @block.scalar
        def _(act):
            yact.open(act)

            def gate_exp(b):
                lg_c.wait(act, b)
                e_done.up(nc.scalar.activation(ex[:, :, :], lg[:, :, :], ACT.Exp))
            norm.act(act, 0, 0)
            gate_exp(0)

            def body(b, par):
                w_done.wait(act, b)

                def tile(k):
                    y.wait(act, b, k + 1)
                    if k >= 2:
                        ysum.wait(act, b, k - 1)
                    else:
                        ysum.wait_before(act, b)
                    for e in range(NE // 2):
                        ins = nc.scalar.activation(upper[:, k % 2, e], psY[k % 2][1][:, e * D:(e + 1) * D],
                                                   ACT.Copy, scale=w[:, par, k, NE // 2 + e:NE // 2 + e + 1])
                    yact.up(ins)
                wt_ps.wait(act, b)
                wt_sb.up(nc.scalar.copy(wT[:, :], psW[:, 256:384]))
                tile(0)
                norm.act(act, b + 1, 1 - par)
                tile(1)
                gate_exp(b + 1)
                tile(2)
                tile(3)
            both_parities(act, body)

        @block.tensor
        def _(pe):
            def gates(b, par, first=False):
                norm.out.wait(pe, b)
                if not first:
                    wt_sb.wait_before(pe, b)
                for k in range(NT):
                    last = nc.tensor.matmul(psG[:, k * NE:(k + 1) * NE], xnT[:, par, k * P:(k + 1) * P],
                                            m.gate_w[:, :], start=True, stop=True)
                logits.up(last)
            norm.pe(pe, 0, True)
            gates(0, 0, True)

            def body(b, par):
                def tile(k):
                    if k >= 2:
                        mix.wait(pe, b, 4 * (k - 1))
                        yact.wait(pe, b, k - 1)
                    else:
                        mix.wait_before(pe, b)
                        yact.wait_before(pe, b)
                    for half in range(2):
                        last = nc.tensor.matmul(psY[k % 2][half][:, :], xnT[:, par, k * P:(k + 1) * P],
                                                m.expert_w[:, half * L:(half + 1) * L], start=True, stop=True)
                    y.up(last)
                w_done.wait(pe, b)
                wt_ps.up(nc.tensor.transpose(psW[:, 256:384], w[:, par, :, :].rearrange("p k e -> p (k e)"),
                                             m.ident[:, :]))
                tile(0)
                norm.pe(pe, b + 1)
                tile(1)
                gates(b + 1, 1 - par)
                tile(2)
                wt_sb.wait(pe, b)
                bias_used.wait_before(pe, b)
                bias_ps.up(nc.tensor.matmul(psB[:, :], wT[:, :], m.expert_b[:, :, :].rearrange("p k o -> p (k o)"),
                                            start=True, stop=True))
                tile(3)
            both_parities(pe, body)


def proto_stage(nc, m, tag):
    c = lambda name, per=1, frees=False: Count(m, f"{tag}_{name}", per, frees)
    cross, sq, pair_done, dist_done = c("cross_products"), c("xn_squares"), c("two_smallest"), c("distances")
    gap, e_done, w_done = c("distance_gap"), c("second_exp"), c("weights")
    wt_ps, wt_sb, bias_ps, bias_used = c("weightsT"), c("weightsT_copied", 1, True), c("bias_product"), c("bias_added", 1, True)
    h, hw_done, ht, ht_sb = c("down", NT), c("down_weighted", NT, True), c("downT", NT), c("downT_copied", NT, True)
    up, up_sb, o, added = c("up"), c("up_copied"), c("up_transposed"), c("x_added", 1, True)
    near = Chain(m, f"{tag}_distance_steps", 3)
    top = Chain(m, f"{tag}_nearest_steps", 16)
    ctx = ExitStack()
    with ctx:
        sb = lambda n, s: ctx.enter_context(nc.sbuf_tensor(f"{tag}_{n}", s, F32))
        scratch = sb("square_out", [P, NT, D])
        x2 = sb("x2", [P, NT])
        d2 = sb("d2", [P, NT, NPROTO])
        dist = sb("dist", [P, 2, NT])
        eq = sb("eq", [P, NT, NPROTO])
        rest = sb("rest", [P, NT, NPROTO])
        key = sb("key", [P, NT, NPROTO])
        first = sb("first", [P, NT, NPROTO])
        second = sb("second", [P, NT, NPROTO])
        small = sb("small", [P, 10, NT])
        w = sb("w", [P, NT, NPROTO])
        wT = sb("wT", [P, P])
        hw = sb("hw", [P, 2, NPROTO, RANK])
        hwT = sb("hwT", [P, NR // P, L])
        upT = sb("upT", [P, L])
        xnT = sb("xnT", [P, 2, L])
        psT, psD, psW, psB, psU = m.ps[0], m.ps[1], m.ps[1], m.ps[2], m.ps[7]
        psH, psHT = m.ps[3:5], m.ps[5:7]
        norm = Norm(nc, m, tag, lambda par: xnT[:, par, :], psT)
        block = ctx.enter_context(nc.Block())

        @block.gpsimd
        def _(pool):
            def distances(b):
                pair_done.wait(pool, b)
                dist_done.up(nc.gpsimd.tensor_tensor(dist[:, :, :], small[:, 0:3:2, :], m.half[:, :, :], ALU.pow))
            norm.pool_rstd(pool, 0)
            distances(0)

            def body(b, par):
                norm.pool_rstd(pool, b + 1)
                distances(b + 1)
            both_parities(pool, body)

        @block.vector
        def _(dve):
            def square_distance(b):
                near.start(dve, b)
                cross.wait(dve, b)
                near.link(nc.vector.scalar_tensor_tensor(d2[:, :, :], psD[:, 0:P].rearrange("p (k n) -> p k n", n=NPROTO),
                                                         -2.0, bc(m.proto_sq[:, :], 1, NT), ALU.mult, ALU.add))
                sq.wait(dve, b)
                near.link(nc.vector.tensor_tensor(d2[:, :, :], d2[:, :, :], bc(x2[:, :], 2, NPROTO), ALU.add))
                near.link(nc.vector.tensor_scalar(d2[:, :, :], d2[:, :, :], 0.0, None, ALU.max))
                near.end()

            def smallest(value, onehot, at, last):
                v, kmax = small[:, at, :], small[:, at + 1, :]
                top.link(nc.vector.tensor_reduce(v, value, AX.X, ALU.min))
                top.link(nc.vector.tensor_tensor(eq[:, :, :], value, bc(v, 2, NPROTO), ALU.is_equal))
                top.link(nc.vector.tensor_tensor(key[:, :, :], eq[:, :, :], bc(m.rank_back[:, :], 1, NT), ALU.mult))
                top.link(nc.vector.tensor_reduce(kmax, key[:, :, :], AX.X, ALU.max))
                last(nc.vector.tensor_tensor(onehot, key[:, :, :], bc(kmax, 2, NPROTO), ALU.is_equal))

            def nearest_in(b):
                top.start(dve, b)
                smallest(d2[:, :, :], first[:, :, :], 0, top.link)
                top.link(nc.vector.scalar_tensor_tensor(rest[:, :, :], first[:, :, :], BIG, d2[:, :, :], ALU.mult, ALU.add))
                smallest(rest[:, :, :], second[:, :, :], 2, pair_done.up)

            def nearest_gap(b):
                dist_done.wait(dve, b)
                gap.up(nc.vector.tensor_tensor(small[:, 4, :], dist[:, 1, :], dist[:, 0, :], ALU.subtract))

            def nearest_out(b):
                pair_done.wait(dve, b)
                e_done.wait(dve, b)
                top.link(nc.vector.tensor_scalar(small[:, 6, :], small[:, 5, :], 1.0, None, ALU.add))
                top.link(nc.vector.reciprocal(small[:, 7, :], small[:, 6, :]))
                top.step(nc.vector.tensor_scalar(small[:, 8, :], small[:, 7, :], 0.5, None, ALU.mult))
                top.link(nc.vector.scalar_tensor_tensor(small[:, 9, :], small[:, 5, :], 0.5, small[:, 7, :], ALU.mult, ALU.mult))
                top.step(nc.vector.tensor_tensor(first[:, :, :], first[:, :, :], bc(small[:, 8, :], 2, NPROTO), ALU.mult))
                top.link(nc.vector.tensor_tensor(second[:, :, :], second[:, :, :], bc(small[:, 9, :], 2, NPROTO), ALU.mult))
                top.end()
                w_done.up(nc.vector.tensor_tensor(w[:, :, :], first[:, :, :], second[:, :, :], ALU.add))

            hw_done.open(dve)
            bias_used.open(dve)
            added.open(dve)
            norm.dve_stats(dve, 0)
            norm.dve_apply(dve, 0, True)
            square_distance(0)
            nearest_in(0)
            nearest_gap(0)
            nearest_out(0)

            def body(b, par):
                def weigh(k):
                    h.wait(dve, b, k + 1)
                    if k >= 2:
                        ht.wait(dve, b, k - 1)
                    hw_done.up(nc.vector.tensor_tensor(hw[:, k % 2], psH[k % 2][:, :].rearrange("p (n r) -> p n r", r=RANK),
                                                       bc(w[:, k, :], 2, RANK), ALU.mult))
                norm.dve_stats(dve, b + 1)
                w_done.wait(dve, b)
                weigh(0)
                norm.dve_apply(dve, b + 1)
                weigh(1)
                weigh(2)
                square_distance(b + 1)
                weigh(3)
                nearest_in(b + 1)
                xb = m.x[:, bass.ds(b * NT, NT), :]
                bias_ps.wait(dve, b)
                bias_used.up(nc.vector.tensor_tensor(xb, xb, psB[:, :].rearrange("p (k o) -> p k o", o=D), ALU.add))
                nearest_gap(b + 1)
                o.wait(dve, b)
                bias_used.wait(dve, b)
                added.up(nc.vector.tensor_tensor(xb, xb, psU[:, :].rearrange("p (k o) -> p k o", o=D), ALU.add))
                nearest_out(b + 1)
            both_parities(dve, body)

        @block.scalar
        def _(act):
            def squares(b):
                norm.xn.wait(act, b)
                for k in range(NT):
                    last = nc.scalar.activation(scratch[:, k, :], m.xn[:, k, :], ACT.Square, accum_out=x2[:, k:k + 1])
                sq.up(last)

            def second_exp(b):
                gap.wait(act, b)
                e_done.up(nc.scalar.activation(small[:, 5, :], small[:, 4, :], ACT.Exp, scale=m.neg_inv_t[:, 0:1]))
            wt_sb.open(act)
            ht_sb.open(act)
            norm.act(act, 0, 0)
            squares(0)
            second_exp(0)

            def body(b, par):
                def copy_back(k):
                    ht.wait(act, b, k + 1)
                    ht_sb.up(nc.scalar.copy(hwT[:, :, k * P:(k + 1) * P],
                                            psHT[k % 2][:, :].rearrange("p (c t) -> p c t", t=P)))
                wt_ps.wait(act, b)
                wt_sb.up(nc.scalar.copy(wT[:, :], psW[:, 256:384]))
                copy_back(0)
                norm.act(act, b + 1, 1 - par)
                squares(b + 1)
                copy_back(1)
                copy_back(2)
                copy_back(3)
                second_exp(b + 1)
                up.wait(act, b)
                up_sb.up(nc.scalar.copy(upT[:, :], psU[:, :]))
            both_parities(act, body)

        @block.tensor
        def _(pe):
            def crosses(b, par):
                norm.out.wait(pe, b)
                wt_sb.wait_before(pe, b)
                for k in range(NT):
                    last = nc.tensor.matmul(psD[:, k * NPROTO:(k + 1) * NPROTO], xnT[:, par, k * P:(k + 1) * P],
                                            m.protoT[:, :], start=True, stop=True)
                cross.up(last)
            norm.pe(pe, 0, True)
            crosses(0, 0)

            def body(b, par):
                def down(k):
                    if k >= 2:
                        hw_done.wait(pe, b, k - 1)
                    else:
                        hw_done.wait_before(pe, b)
                    h.up(nc.tensor.matmul(psH[k % 2][:, :], xnT[:, par, k * P:(k + 1) * P],
                                          m.BT[:, :, :].rearrange("p c r -> p (c r)"), start=True, stop=True))

                def turn(k):
                    hw_done.wait(pe, b, k + 1)
                    if k >= 2:
                        ht_sb.wait(pe, b, k - 1)
                    else:
                        ht_sb.wait_before(pe, b)
                    flat = hw[:, k % 2].rearrange("p n r -> p (n r)")
                    for q in range(NR // P):
                        last = nc.tensor.transpose(psHT[k % 2][:, q * P:(q + 1) * P], flat[:, q * P:(q + 1) * P],
                                                   m.ident[:, :])
                    ht.up(last)
                down(0)
                down(1)
                w_done.wait(pe, b)
                wt_ps.up(nc.tensor.transpose(psW[:, 256:384], w[:, :, :].rearrange("p k n -> p (k n)"), m.ident[:, :]))
                turn(0)
                norm.pe(pe, b + 1)
                down(2)
                turn(1)
                crosses(b + 1, 1 - par)
                down(3)
                turn(2)
                wt_sb.wait(pe, b)
                bias_used.wait_before(pe, b)
                bias_ps.up(nc.tensor.matmul(psB[:, :], wT[:, :], m.proto_b[:, :, :].rearrange("p k o -> p (k o)"),
                                            start=True, stop=True))
                turn(3)
                ht_sb.wait(pe, b)
                added.wait_before(pe, b)
                for q in range(NR // P):
                    last = nc.tensor.matmul(psU[:, :], m.AT[:, q, :], hwT[:, q, :], start=(q == 0), stop=(q == NR // P - 1))
                up.up(last)
                up_sb.wait(pe, b)
                for k in range(NT):
                    last = nc.tensor.transpose(psU[:, k * P:(k + 1) * P], upT[:, k * P:(k + 1) * P], m.ident[:, :])
                o.up(last)
            both_parities(pe, body)


def latent_stage(nc, m, tag):
    NQ, NG = NT, H // HG
    NU = NQ * NG
    NPJ = H + 2
    FIRST_PJ = 2
    STEPS = NU + 3
    units = [(u // NG, u % NG) for u in range(NU)]
    c = lambda name, per=1, frees=False: Count(m, f"{tag}_{name}", per, frees)
    proj, high, low = c("projections", NPJ), c("high_halves", NPJ - 1), c("projections_done", NPJ)
    scores, mx, exp, inv = c("scores", 2 * NU), c("row_maxima", 2 * NU), c("probabilities", 2 * NU, True), c("row_sums_inverted", NU)
    normed, turned = c("probabilities_normed", NU), c("probabilities_transposed", sum(q + 1 for q, _ in units), True)
    z, z_sb, o, added = c("z", NU), c("z_copied", NU, True), c("attended", NQ), c("x_added", NQ, True)

    def by_dve(qb, k):
        return k >= 2 or (qb == 1 and k == 1)
    all_jobs = [(u, k) for u, (qb, _) in enumerate(units) for k in range(qb + 1)]
    back = {True: c("pT_copied_dve", sum(by_dve(units[u][0], k) for u, k in all_jobs), True),
            False: c("pT_copied_act", sum(not by_dve(units[u][0], k) for u, k in all_jobs), True)}

    def copies(dve, n):
        return sum(by_dve(units[u][0], k) == dve for u, k in all_jobs[:n])

    def jobs_before(u):
        return sum(qb + 1 for qb, _ in units[:u])

    def projections_of(step):
        n = [step - FIRST_PJ] if FIRST_PJ <= step < FIRST_PJ + NPJ - 1 else []
        return n + ([NPJ - 1] if step == STEPS - 1 else [])
    assert [n for s in range(STEPS) for n in projections_of(s)] == list(range(NPJ))
    ctx = ExitStack()
    with ctx:
        sb = lambda n, s, dt=F32: ctx.enter_context(nc.sbuf_tensor(f"{tag}_{n}", s, dt))
        xnT = sb("xnT", [P, 2, L])
        qS = sb("q_stack", [P, 2, H, L], F32R)
        latS = sb("latent_stack", [P, 2, L], F32R)
        lat = sb("lat", [P, 2, NT, LD])
        p = sb("p", [P, 4, HG, L])
        pT = sb("pT", [P, 2, NT, L])
        nmax = sb("nmax", [P, 2, HG])
        rsum = sb("rsum", [P, 4, HG])
        rinv = sb("rinv", [P, 4, HG])
        zT = sb("zT", [P, 2, NG, P])
        psS = m.psS[:, :].rearrange("p (h t) -> p h t", t=L)
        psP, psZ, psO, psJ = m.ps[4:6], m.ps[6][:, 0:P], m.ps[6][:, P:2 * P], m.ps[7]
        norm = Norm(nc, m, tag, lambda par: xnT[:, par, :], psJ)
        block = ctx.enter_context(nc.Block())

        @block.gpsimd
        def _(pool):
            norm.pool_rstd(pool, 0)

            def body(b, par):
                norm.pool_rstd(pool, b + 1)
                for u, (qb, g) in enumerate(units):
                    inv.wait(pool, b, u + 1)
                    n = (qb + 1) * P
                    pu = p[:, u % 4, :, 0:n]
                    normed.up(nc.gpsimd.tensor_tensor(pu, pu, bc(rinv[:, u % 4, :], 2, n), ALU.mult))
            both_parities(pool, body)

        @block.vector
        def _(dve):
            def lower(b, par, n):
                if n == NPJ - 1:
                    proj.wait(dve, b, n + 1)
                    low.up(nc.vector.tensor_copy(lat[:, par, :, :], psJ[:, 0:NT * LD].rearrange("p (k c) -> p k c", c=LD)))
                    return
                high.wait(dve, b, n + 1)
                stack, rows = (qS[:, par, n, :], [(2 * LD, 4 * LD)]) if n < H else (latS[:, par, :], [(LD, 2 * LD), (3 * LD, P)])
                for r0, r1 in rows:
                    last = nc.vector.tensor_tensor(stack[r0:r1], psJ[r0:r1, :], stack[r0:r1].bitcast(F32), ALU.subtract)
                low.up(last)
            back[True].open(dve)
            added.open(dve)
            norm.dve_stats(dve, 0)
            norm.dve_apply(dve, 0, True)
            for n in range(NPJ):
                lower(0, 0, n)

            def body(b, par):
                def maxima(u):
                    qb, g = units[u]
                    for pair in range(2):
                        scores.wait(dve, b, 2 * u + pair + 1)
                        hs = slice(2 * pair, 2 * pair + 2)
                        mx.up(nc.vector.tensor_reduce(nmax[:, u % 2, hs], psS[:, hs, 0:(qb + 1) * P], AX.X, ALU.max,
                                                      negate=True))

                def invert(u):
                    exp.wait(dve, b, 2 * u + 2)
                    inv.up(nc.vector.reciprocal(rinv[:, u % 4, :], rsum[:, u % 4, :]))

                def copy_back(u):
                    for k in range(units[u][0] + 1):
                        if by_dve(units[u][0], k):
                            n = jobs_before(u) + k
                            turned.wait(dve, b, n + 1)
                            back[True].up(nc.vector.tensor_copy(pT[:, u % 2, k, :], psP[n % 2][:, :]))

                def add(qb):
                    o.wait(dve, b, qb + 1)
                    xq = m.x[:, b * NT + qb, :]
                    added.up(nc.vector.tensor_tensor(xq, xq, psO, ALU.add))
                for s in range(STEPS):
                    if s < NU:
                        maxima(s)
                    if s:
                        for n in projections_of(s - 1):
                            lower(b + 1, 1 - par, n)
                    if 1 <= s <= NU:
                        invert(s - 1)
                    if s == 0:
                        norm.dve_stats(dve, b + 1)
                    if s == 1:
                        norm.dve_apply(dve, b + 1)
                    if 2 <= s < NU + 2:
                        copy_back(s - 2)
                    if s >= 6 and (s - 6) % NG == 0:
                        add((s - 6) // NG)
                for n in projections_of(STEPS - 1):
                    lower(b + 1, 1 - par, n)
            both_parities(dve, body)

        @block.scalar
        def _(act):
            def raise_(b, par, n):
                if n < NPJ - 1:
                    proj.wait(act, b, n + 1)
                    high.up(nc.scalar.copy(qS[:, par, n, :] if n < H else latS[:, par, :], psJ[:, :]))
            exp.open(act)
            back[False].open(act)
            z_sb.open(act)
            norm.act(act, 0, 0)
            for n in range(NPJ):
                raise_(0, 0, n)

            def body(b, par):
                def exponents(u):
                    qb, g = units[u]
                    if u >= 4:
                        turned.wait(act, b, jobs_before(u - 3))
                    else:
                        turned.wait_before(act, b)
                    for j in range(HG):
                        if j % 2 == 0:
                            mx.wait(act, b, 2 * u + j // 2 + 1)
                        last = nc.scalar.activation(p[:, u % 4, j, 0:(qb + 1) * P], psS[:, j, 0:(qb + 1) * P], ACT.Exp,
                                                    bias=nmax[:, u % 2, j:j + 1], accum_out=rsum[:, u % 4, j:j + 1])
                        if j % 2:
                            exp.up(last)

                def copy_back(u):
                    for k in range(units[u][0] + 1):
                        if not by_dve(units[u][0], k):
                            n = jobs_before(u) + k
                            turned.wait(act, b, n + 1)
                            back[False].up(nc.scalar.copy(pT[:, u % 2, k, :], psP[n % 2][:, :]))

                def copy_z(u):
                    qb, g = units[u]
                    z.wait(act, b, u + 1)
                    z_sb.up(nc.scalar.copy(zT[:, qb % 2, g, :], psZ))
                for s in range(STEPS):
                    if s == FIRST_PJ:
                        norm.act(act, b + 1, 1 - par)
                    if 2 <= s < NU + 2:
                        copy_back(s - 2)
                    if s < NU:
                        exponents(s)
                    for n in projections_of(s):
                        raise_(b + 1, 1 - par, n)
                    if 2 <= s < NU + 2:
                        copy_z(s - 2)
            both_parities(act, body)

        @block.tensor
        def _(pe):
            def project(b, par, n):
                norm.out.wait(pe, b)
                if n:
                    low.wait(pe, b, n)
                if n < NPJ - 1:
                    w = m.Wqk0[:, n, :] if n < H else m.Wdown[:, :]
                    proj.up(nc.tensor.matmul(psJ[:, :], w, xnT[:, par, :], start=True, stop=True))
                else:
                    for k in range(NT):
                        last = nc.tensor.matmul(psJ[:, k * LD:(k + 1) * LD], xnT[:, par, k * P:(k + 1) * P],
                                                m.Wdown[:, 0:LD], start=True, stop=True)
                    proj.up(last)
            turned.open(pe)
            norm.pe(pe, 0, True)
            for n in range(NPJ):
                project(0, 0, n)

            def body(b, par):
                def score(u):
                    qb, g = units[u]
                    n = (qb + 1) * P
                    for pair in range(2):
                        if u:
                            exp.wait(pe, b, 2 * u - 1 + pair)
                        else:
                            exp.wait_before(pe, b)
                        for j in (2 * pair, 2 * pair + 1):
                            nc.tensor.matmul(psS[:, j, 0:n], qS[:, par, g * HG + j, qb * P:n], latS[:, par, 0:n],
                                             start=True, stop=False)
                            last = nc.tensor.matmul(psS[:, j, qb * P:n], m.identb[:, :], m.causal[:, :],
                                                    start=False, stop=True)
                        scores.up(last)

                def turn(u):
                    qb, g = units[u]
                    normed.wait(pe, b, u + 1)
                    for k in range(qb + 1):
                        n = jobs_before(u) + k
                        if n >= 2:
                            dve = by_dve(units[all_jobs[n - 2][0]][0], all_jobs[n - 2][1])
                            back[dve].wait(pe, b, copies(dve, n - 1))
                        else:
                            back[True].wait_before(pe, b)
                            back[False].wait_before(pe, b)
                        for j in range(HG):
                            last = nc.tensor.transpose(psP[n % 2][:, j * P:(j + 1) * P], p[:, u % 4, j, k * P:(k + 1) * P],
                                                       m.ident[:, :])
                        turned.up(last)

                def attend(u):
                    qb, g = units[u]
                    back[False].wait(pe, b, copies(False, jobs_before(u + 1)))
                    if qb:
                        back[True].wait(pe, b, copies(True, jobs_before(u + 1)))
                    if u >= 1:
                        z_sb.wait(pe, b, u)
                    else:
                        z_sb.wait_before(pe, b)
                    if u % NG == 0 and u:
                        added.wait(pe, b, u // NG)
                    for k in range(qb + 1):
                        for j in range(HG):
                            last = nc.tensor.matmul(psZ[j * LD:(j + 1) * LD, :], lat[:, par, k, :],
                                                    pT[:, u % 2, k, j * P:(j + 1) * P], start=(k == 0), stop=(k == qb))
                    z.up(last)

                def project_out(qb):
                    z_sb.wait(pe, b, NG * (qb + 1))
                    for g in range(NG):
                        last = nc.tensor.matmul(psO, zT[:, qb % 2, g, :], m.Wvo0[:, g, :], start=(g == 0), stop=(g == NG - 1))
                    o.up(last)
                low.wait(pe, b)
                for s in range(STEPS):
                    if s < NU:
                        score(s)
                    if 2 <= s < NU + 2:
                        turn(s - 2)
                    if s >= 6 and (s - 6) % NG == 0:
                        project_out((s - 6) // NG)
                    for n in projections_of(s):
                        project(b + 1, 1 - par, n)
                    if s == 0:
                        added.wait_before(pe, b)
                    if s == 1:
                        norm.pe(pe, b + 1)
                    if 2 <= s < NU + 2:
                        attend(s - 2)
            both_parities(pe, body)


def local_stage(nc, m, tag):
    NBK, WB = L // P, P // QW
    NG = H // HG
    NPJ = H + NG
    c = lambda name, per=1, frees=False: Count(m, f"{tag}_{name}", per, frees)
    scores, mx, exp, inv = c("scores", H), c("row_maxima", H), c("probabilities", H, True), c("row_sums_inverted", H)
    normed, turned = c("probabilities_normed", H), c("probabilities_transposed", NBK * NG)
    back_act, back_dve = c("pT_copied_act", NBK * NG // 2, True), c("pT_copied_dve", NBK * NG // 2, True)
    proj, proj_act, proj_dve = c("projections", NPJ), c("projections_copied_act", NPJ // 2), c("projections_copied_dve", NPJ // 2)
    keys = c("windows_copied")
    z, z_act, z_dve = c("z", NBK * WB), c("z_copied_act", NBK * WB // 2), c("z_copied_dve", NBK * WB // 2)
    o, o_sb, oT, added = c("attended"), c("attended_copied"), c("attended_transposed"), c("x_added", 1, True)
    cleared = m.semaphore(f"{tag}_margins_cleared")
    ctx = ExitStack()
    with ctx:
        sb = lambda n, s: ctx.enter_context(nc.sbuf_tensor(f"{tag}_{n}", s, F32))
        xnT = sb("xnT", [P, 2, QW + L])
        kwin = sb("kwin", [P, 2, NW, KW])
        xwin = sb("xwin", [KW, 2, NW, D])
        qT = sb("qT", [P, H, L])
        p = sb("p", [P, 2, H, KW])
        pT = sb("pT", [KW, 2, H, P])
        zT = sb("zT", [P, H, L])
        ot = sb("ot", [P, L])
        nmax = sb("nmax", [P, 2, H])
        rsum = sb("rsum", [P, 2, H])
        rinv = sb("rinv", [P, 2, H])
        psS, psP, psZ = m.ps[0:4], m.ps[4:6], m.ps[6:8]
        norm = Norm(nc, m, tag, lambda par: xnT[:, par, QW - 1:QW - 1 + L], psZ[1])
        block = ctx.enter_context(nc.Block())

        @block.gpsimd
        def _(pool):
            norm.pool_rstd(pool, 0)

            def body(b, par):
                norm.pool_rstd(pool, b + 1)
                for u in range(NBK * NG):
                    bk, g = divmod(u, NG)
                    hs = slice(g * HG, (g + 1) * HG)
                    inv.wait(pool, b, u + 1)
                    normed.up(nc.gpsimd.tensor_tensor(p[:, bk % 2, hs, :], p[:, bk % 2, hs, :],
                                                      bc(rinv[:, bk % 2, hs], 2, KW), ALU.mult))
            both_parities(pool, body)

        def copy_projection(copy, b, par, n):
            if n < H:
                return copy(qT[:, n, :], psP[n % 2][:, :])
            w = (n - H) * WB
            return copy(xwin[:, par, w:w + WB, :], psP[n % 2][0:KW, :].rearrange("k (w d) -> k w d", d=D))

        @block.vector
        def _(dve):
            back_dve.open(dve)
            added.open(dve)
            nc.vector.memset(xnT[:, :, :], 0.0).then_inc(cleared, 1)

            def windows(b, par):
                norm.out.wait(dve, b)
                nc.vector.tensor_copy(kwin[:, par, :, 0:QW], xnT[:, par, 0:L].rearrange("p (w k) -> p w k", k=QW))
                nc.vector.tensor_copy(kwin[:, par, :, QW:2 * QW], xnT[:, par, QW:QW + L].rearrange("p (w k) -> p w k", k=QW))
                keys.up(nc.vector.tensor_copy(kwin[:, par, :, 2 * QW:KW], bc(xnT[:, par, QW - 1:QW], 1, NW)))

            def projections(b, par):
                for n in range(1, NPJ, 2):
                    proj.wait(dve, b, n + 1)
                    proj_dve.up(copy_projection(nc.vector.tensor_copy, b, par, n))
            norm.dve_stats(dve, 0)
            norm.dve_apply(dve, 0, True)
            windows(0, 0)
            projections(0, 0)

            def body(b, par):
                def maximum(u):
                    bk, g = divmod(u, NG)
                    scores.wait(dve, b, u + 1)
                    mx.up(nc.vector.tensor_reduce(nmax[:, bk % 2, g * HG:(g + 1) * HG],
                                                  psS[g][:, 0:HG * KW].rearrange("p (h k) -> p h k", k=KW),
                                                  AX.X, ALU.max, negate=True))

                def invert(u):
                    bk, g = divmod(u, NG)
                    exp.wait(dve, b, u + 1)
                    hs = slice(g * HG, (g + 1) * HG)
                    inv.up(nc.vector.reciprocal(rinv[:, bk % 2, hs], rsum[:, bk % 2, hs]))

                def copy_z(bk):
                    for j in range(1, WB, 2):
                        z.wait(dve, b, bk * WB + j + 1)
                        q = bk * P + j * QW
                        z_dve.up(nc.vector.tensor_copy(zT[:, :, q:q + QW], psZ[1][:, :].rearrange("p (h q) -> p h q", q=QW)))
                for bk in range(NBK):
                    maximum(bk * NG)
                    for g in range(1, NG):
                        maximum(bk * NG + g)
                        invert(bk * NG + g - 1)
                    if bk:
                        copy_z(bk - 1)
                    invert(bk * NG + NG - 1)
                    if bk == 0:
                        norm.dve_stats(dve, b + 1)
                        norm.dve_apply(dve, b + 1)
                    if bk == 2:
                        windows(b + 1, 1 - par)
                    if bk == NBK - 1:
                        projections(b + 1, 1 - par)
                    for g in range(1, NG, 2):
                        turned.wait(dve, b, bk * NG + g + 1)
                        back_dve.up(nc.vector.tensor_copy(pT[:, bk % 2, g * HG:(g + 1) * HG, :],
                                                          psP[1][0:KW, :].rearrange("k (h q) -> k h q", q=P)))
                copy_z(NBK - 1)
                oT.wait(dve, b)
                xb = m.x[:, bass.ds(b * NT, NT), :]
                added.up(nc.vector.tensor_tensor(xb, xb, psZ[0][:, :].rearrange("p (k o) -> p k o", o=D), ALU.add))
            both_parities(dve, body)

        @block.scalar
        def _(act):
            exp.open(act)
            back_act.open(act)

            def projections(b, par):
                for n in range(0, NPJ, 2):
                    proj.wait(act, b, n + 1)
                    proj_act.up(copy_projection(nc.scalar.copy, b, par, n))
            act.wait_ge(cleared, 1)
            norm.act(act, 0, 0)
            projections(0, 0)

            def body(b, par):
                def exponents(u):
                    bk, g = divmod(u, NG)
                    mx.wait(act, b, u + 1)
                    for j in range(HG):
                        h = g * HG + j
                        last = nc.scalar.activation(p[:, bk % 2, h, :], psS[g][:, j * KW:(j + 1) * KW], ACT.Exp,
                                                    bias=nmax[:, bk % 2, h:h + 1], accum_out=rsum[:, bk % 2, h:h + 1])
                    exp.up(last)

                def copy_z(bk):
                    for j in range(0, WB, 2):
                        z.wait(act, b, bk * WB + j + 1)
                        q = bk * P + j * QW
                        z_act.up(nc.scalar.copy(zT[:, :, q:q + QW], psZ[0][:, :].rearrange("p (h q) -> p h q", q=QW)))
                for bk in range(NBK):
                    for g in range(NG):
                        exponents(bk * NG + g)
                    if bk:
                        copy_z(bk - 1)
                    if bk == 1:
                        norm.act(act, b + 1, 1 - par)
                    if bk == NBK - 1:
                        projections(b + 1, 1 - par)
                    for g in range(0, NG, 2):
                        turned.wait(act, b, bk * NG + g + 1)
                        back_act.up(nc.scalar.copy(pT[:, bk % 2, g * HG:(g + 1) * HG, :],
                                                   psP[0][0:KW, :].rearrange("k (h q) -> k h q", q=P)))
                copy_z(NBK - 1)
                o.wait(act, b)
                nc.scalar.activation(ot[:, 1:L], psZ[0][:, 0:L - 1], ACT.Identity, bias=m.b_out[:, 0:1])
                o_sb.up(nc.scalar.activation(ot[:, 0:1], psZ[1][:, 0:1], ACT.Identity, bias=m.b_out[:, 0:1]))
            both_parities(act, body)

        @block.tensor
        def _(pe):
            def project(b, par):
                norm.out.wait(pe, b)
                for n in range(NPJ):
                    if n >= 2:
                        (proj_act, proj_dve)[n % 2].wait(pe, b, n // 2)
                    if n < H:
                        last = nc.tensor.matmul(psP[n % 2][:, :], m.Wqk1[:, n, :], xnT[:, par, QW:QW + L], start=True, stop=True)
                    else:
                        if n == H:
                            keys.wait(pe, b)
                        for j in range(WB):
                            last = nc.tensor.transpose(psP[n % 2][0:KW, j * D:(j + 1) * D],
                                                       kwin[:, par, (n - H) * WB + j, :], m.ident[:, :])
                    proj.up(last)
            norm.pe(pe, 0, True)
            project(0, 0)

            def body(b, par):
                def score(u):
                    bk, g = divmod(u, NG)
                    if bk:
                        exp.wait(pe, b, u - NG + 1)
                    else:
                        exp.wait_before(pe, b)
                    out = psS[g]
                    nc.tensor.matmul(out[:, 0:HG * KW], m.identb[:, :],
                                     m.window[:, min(bk, 1), :, :].rearrange("p h k -> p (h k)"),
                                     start=True, stop=False, skip_group_check=True)
                    for i in range(HG):
                        for j in range(WB):
                            q = bk * P + j * QW
                            last = nc.tensor.matmul(out[j * QW:(j + 1) * QW, i * KW:(i + 1) * KW],
                                                    qT[:, g * HG + i, q:q + QW], kwin[:, par, bk * WB + j, :],
                                                    start=False, stop=(i == HG - 1), skip_group_check=True)
                    scores.up(last)

                def turn(u):
                    bk, g = divmod(u, NG)
                    if u < 2:
                        (back_act, back_dve)[u % 2].wait_before(pe, b)
                    elif bk == NBK - 1 and g < 2:
                        (proj_act, proj_dve)[u % 2].wait(pe, b + 1)
                    else:
                        (back_act, back_dve)[u % 2].wait(pe, b, u // 2)
                    normed.wait(pe, b, u + 1)
                    for i in range(HG):
                        last = nc.tensor.transpose(psP[u % 2][0:KW, i * P:(i + 1) * P], p[:, bk % 2, g * HG + i, :],
                                                   m.ident[:, :])
                    turned.up(last)

                def attend(bk):
                    back_act.wait(pe, b, (bk + 1) * NG // 2)
                    back_dve.wait(pe, b, (bk + 1) * NG // 2)
                    if bk == 0:
                        added.wait_before(pe, b)
                    if bk == 1:
                        norm.out.wait(pe, b + 1)
                    for j in range(WB):
                        n = bk * WB + j
                        if n >= 2:
                            (z_act, z_dve)[j % 2].wait(pe, b, n // 2)
                        z.up(nc.tensor.matmul(psZ[j % 2][:, :], xwin[:, par, n, :], pT[:, bk % 2, :, j * QW:(j + 1) * QW],
                                              start=True, stop=True))
                for bk in range(NBK):
                    for g in range(NG):
                        score(bk * NG + g)
                    if bk:
                        attend(bk - 1)
                    if bk == 1:
                        z_dve.wait(pe, b, WB // 2)
                        norm.pe(pe, b + 1)
                    if bk == NBK - 1:
                        back_act.wait(pe, b, (NBK - 1) * NG // 2)
                        back_dve.wait(pe, b, (NBK - 1) * NG // 2)
                        project(b + 1, 1 - par)
                    for g in range(NG):
                        turn(bk * NG + g)
                attend(NBK - 1)
                z_act.wait(pe, b)
                z_dve.wait(pe, b)
                for h in range(H):
                    nc.tensor.matmul(psZ[0][:, :], m.M1[:, h, :], zT[:, h, :], start=(h == 0), stop=(h == H - 1))
                o.up(nc.tensor.matmul(psZ[1][:, 0:2], m.M_first[:, :], xnT[:, par, QW - 1:QW + 1], start=True, stop=True))
                o_sb.wait(pe, b)
                for k in range(NT):
                    last = nc.tensor.transpose(psZ[0][:, k * D:(k + 1) * D], ot[:, k * P:(k + 1) * P], m.ident[:, :])
                oT.up(last)
            both_parities(pe, body)


def program(nc, x_in, Wq0, Wkv_down, Wk_up, Wv_up, Wout0, gate_w, gate_b, expert_w, expert_b,
            w_qkv, w_out, b_out, w_th, prototypes, Bf, Af, bias1, temp, out):
    ctx = ExitStack()
    with ctx:
        class m:
            in_stage = []

            @classmethod
            def semaphore(cls, name):
                cls.in_stage.append(nc.alloc_semaphore(name))
                return cls.in_stage[-1]

            @classmethod
            def end_stage(cls):
                nc.clear_and_free_semaphores(cls.in_stage)
                nc.all_engine_barrier()
                cls.in_stage = []
        sb = lambda n, s, dt=F32: ctx.enter_context(nc.sbuf_tensor(n, s, dt))
        m.x = sb("x_res", [P, (NB + 1) * NT, D])
        m.ident = sb("ident", [P, P])
        m.neg_half = sb("neg_half", [P, NT])
        m.xn = sb("xn", [P, NT, D])
        m.st = sb("st", [P, NT, 6])
        m.sums = sb("sums", [P, 4, NT])
        m.mean = sb("mean", [P, NT])
        m.var = sb("var", [P, NT])
        m.eps = sb("eps", [P, NT])
        m.var_eps = sb("var_eps", [P, NT])
        m.rstd = sb("rstd", [P, NT])
        m.gate_w = sb("gate_w", [P, NE])
        m.gate_b = sb("gate_b", [P, NE])
        m.expert_w = sb("expert_w", [P, NE * D])
        m.expert_b = sb("expert_b", [P, NT, D])
        m.half = sb("half", [P, 2, NT])
        m.rank_back = sb("rank_back", [P, NPROTO])
        m.protoT = sb("protoT", [P, NPROTO])
        m.proto_sq = sb("proto_sq", [P, NPROTO])
        m.proto_b = sb("proto_b", [P, NT, D])
        m.neg_inv_t = sb("neg_inv_t", [P, 1])
        m.BT = sb("BT", [P, NR // P, P])
        m.AT = sb("AT", [P, NR // P, D])
        m.Wqk0 = sb("Wqk0", [P, H, HG * LD])
        m.Wvo0 = sb("Wvo0", [P, H // HG, D])
        m.Wdown = sb("Wdown", [P, HG * LD])
        m.Wqk1 = sb("Wqk1", [P, H, D])
        m.M1 = sb("M1", [P, H, D])
        m.M_first = sb("M_first", [P, D])
        m.b_out = sb("b_out", [P, 1])
        m.identb = sb("identb", [P, P], BF16)
        m.causal = sb("causal", [P, P], BF16)
        m.window = sb("window", [P, 2, HG, KW], BF16)
        m.psS = ctx.enter_context(nc.psum_tensor("banks0to3", [P, 4 * 512], F32))
        m.ps = [m.psS[:, i * 512:(i + 1) * 512] for i in range(4)]
        m.ps += [ctx.enter_context(nc.psum_tensor(f"bank{i}", [P, 512], F32))[:, :] for i in range(4, 8)]

        x_view = x_in.rearrange("b (k p) d -> p (b k) d", p=P)
        out_view = out.rearrange("b (k p) d -> p (b k) d", p=P)
        prep_stage(nc, m, locals())
        m.end_stage()
        for n, kind in enumerate(STAGES):
            {"A": moe_stage, "D": proto_stage, "B": latent_stage, "E": local_stage}[kind](nc, m, f"s{n}")
            m.end_stage()
        stored = nc.alloc_semaphore("stored")
        with nc.Block() as block:
            @block.sync
            def _(sp):
                for q in range(4):
                    sp.dma_start(out_view[:, q * 16:(q + 1) * 16, :], m.x[:, q * 16:(q + 1) * 16, :]).then_inc(stored, 16)
                sp.wait_ge(stored, 64)


def prep_stage(nc, m, a):
    def sem(name):
        return m.semaphore("prep_" + name)
    loaded, bias_loaded, x_loaded = sem("weights_loaded"), sem("biases_loaded"), sem("x_loaded")
    cleared, filled, ident_ready = sem("cleared"), sem("filled"), sem("ident_ready")
    masks0, masks1, masks2, masks_ready = sem("masks_cleared"), sem("masks_causal"), sem("masks_rows"), sem("masks_ready")
    turned, copied = sem("transposed"), sem("transposes_copied")
    small_steps, sq_ready, scaled, scaled_used = sem("small_steps"), sem("proto_squared"), sem("wout_scaled"), sem("wout_scaled_used")
    products, products_copied, folded = sem("products"), sem("products_copied"), sem("folded")
    NC = H // 2
    ctx = ExitStack()
    with ctx:
        sb = lambda n, s, dt=F32: ctx.enter_context(nc.sbuf_tensor("prep_" + n, s, dt))
        wqkv = sb("wqkv", [P, 3, NC, P])
        wo1 = sb("wo1", [P, NC, D])
        wo0 = sb("wo0", [P, NC, D])
        wq0 = sb("wq0", [P, NC, P])
        wku = sb("wku", [LD, NC, P])
        wvu = sb("wvu", [LD, NC, P])
        Bn = sb("Bn", [P, NR // P, P])
        An = sb("An", [P, NR])
        protos = sb("protos", [NPROTO, P])
        t = sb("temp", [P, 3])
        th = sb("th", [P, NC, H])
        T1 = sb("T1", [P, 3, NC, P])
        T0q = sb("T0q", [P, NC, P])
        T0k = sb("T0k", [P, NC, LD])
        T0v = sb("T0v", [P, NC, LD])
        proto2 = sb("proto2", [P, NPROTO])
        ones = sb("ones", [P, P])
        causal = sb("causal", [P, P])
        window = sb("window", [P, 2, HG, KW])
        back = sb("rank_int", [P, NPROTO], mybir.dt.int32)
        wsc = sb("wo1_scaled", [P, 2, H, D])

        groups = []
        for w in range(3):
            for half in range(2):
                q = slice(half * 4, half * 4 + 4)
                groups.append((T1[:, w, q, :], [wqkv[:, w, c, :] for c in range(8)[q]]))
        for half in range(2):
            q = slice(half * 4, half * 4 + 4)
            groups.append((T0q[:, q, :], [wq0[:, c, :] for c in range(8)[q]]))
        groups.append((T0k[:, :, :], [wku[:, c, :] for c in range(NC)]))
        groups.append((T0v[:, :, :], [wvu[:, c, :] for c in range(NC)]))
        groups.append((m.BT[:, :, :], [Bn[:, c, :] for c in range(NR // P)]))
        groups.append((m.AT[:, :, :], [An[:, c * P:(c + 1) * P] for c in range(NR // P)]))
        groups.append((m.protoT[:, :], [protos[:, :]]))

        block = ctx.enter_context(nc.Block())

        @block.sync
        def _(sp):
            loads = [(wqkv[:, w, :, :].rearrange("p c n -> p (c n)"), a["w_qkv"][:, w * H * HD:(w + 1) * H * HD])
                     for w in range(3)]
            loads += [
                (wq0[:, :, :].rearrange("p c n -> p (c n)"), a["Wq0"].rearrange("d h k -> d (h k)")),
                (wku[:, :, :].rearrange("p c n -> p (c n)"), a["Wk_up"].rearrange("d h k -> d (h k)")),
                (wvu[:, :, :].rearrange("p c n -> p (c n)"), a["Wv_up"].rearrange("d h k -> d (h k)")),
                (Bn[:, :, :], a["Bf"].rearrange("n r i -> (n r) i").rearrange("(c p) i -> p c i", p=P)),
                (An[:, :].rearrange("o (n r) -> o n r", r=RANK), a["Af"].rearrange("n o r -> o n r")),
                (protos[:, :], a["prototypes"]),
                (wo0[:, :, :], a["Wout0"].rearrange("h k o -> (h k) o").rearrange("(c p) o -> p c o", p=P)),
                (wo1[:, :, :], a["w_out"].rearrange("(c p) o -> p c o", p=P)),
                (m.Wdown[:, :].rearrange("d (r c) -> d r c", c=LD), bc(a["Wkv_down"], 1, HG)),
                (m.gate_w[:, :], a["gate_w"]),
                (m.gate_b[:, :], a["gate_b"].partition_broadcast(P)),
                (m.expert_w[:, :].rearrange("d (e o) -> d e o", o=D), a["expert_w"].rearrange("e d o -> d e o")),
                (m.b_out[:, :], a["b_out"].rearrange("(o u) -> o u", u=1)),
                (t[:, 0:1], a["temp"].partition_broadcast(P)),
            ]
            w_th = a["w_th"].rearrange("(c s) h -> s c h", s=2)
            loads += [(th[s * HD:(s + 1) * HD, :, :], w_th[s].partition_broadcast(HD)) for s in range(2)]
            for dst, src in loads:
                sp.dma_start(dst, src).then_inc(loaded, 16)
            m.n_loads = len(loads)
            sp.wait_ge(cleared, 2)
            for k in range(NT):
                sp.dma_start(m.expert_b[32 * k:32 * k + NE, k, :], a["expert_b"]).then_inc(bias_loaded, 16)
                sp.dma_start(m.proto_b[32 * k:32 * k + NPROTO, k, :], a["bias1"]).then_inc(bias_loaded, 16)
            for q in range(4):
                sp.dma_start(m.x[:, q * 16:(q + 1) * 16, :], a["x_view"][:, q * 16:(q + 1) * 16, :]).then_inc(x_loaded, 16)
            sp.wait_ge(bias_loaded, 2 * NT * 16)
            sp.wait_ge(x_loaded, 64)

        @block.gpsimd
        def _(pool):
            for tile, value in ((m.ident[:, :], 0.0), (m.neg_half[:, :], -0.5), (m.eps[:, :], EPS),
                                (m.half[:, :, :], 0.5), (ones[:, :], 1.0), (m.x[:, NB * NT:, :], 0.0)):
                nc.gpsimd.memset(tile, value).then_inc(filled, 1)
            nc.gpsimd.memset(m.expert_b[:, :, :], 0.0).then_inc(cleared, 1)
            nc.gpsimd.memset(m.proto_b[:, :, :], 0.0).then_inc(cleared, 1)
            nc.gpsimd.memset(causal[:, :], 0.0).then_inc(masks0, 1)
            nc.gpsimd.memset(window[:, :, :, :], 0.0).then_inc(masks0, 1)
            pool.wait_ge(filled, 6)
            nc.gpsimd.affine_select(out=m.ident[:, :], in_=m.ident[:, :], compare_op=ALU.not_equal, fill=1.0,
                                    base=0, pattern=[[-1, P]], channel_multiplier=1).then_inc(ident_ready, 1)
            pool.wait_ge(ident_ready, 1)
            pool.wait_ge(masks0, 2)
            nc.gpsimd.affine_select(out=causal[:, :], in_=causal[:, :], compare_op=ALU.is_ge, fill=MASKED,
                                    base=0, pattern=[[-1, P]], channel_multiplier=1).then_inc(masks1, 1)
            for j in range(P // QW):
                q = slice(j * QW, (j + 1) * QW)
                pool.wait_ge(masks1, 1 + 2 * j)
                own = window[q, :, :, QW:2 * QW].rearrange("p a h k -> p (a h) k")
                nc.gpsimd.affine_select(out=own, in_=own, compare_op=ALU.is_ge, fill=MASKED,
                                        base=0, pattern=[[0, 2 * HG], [-1, QW]], channel_multiplier=1).then_inc(masks1, 1)
                pool.wait_ge(masks1, 2 + 2 * j)
                top = window[q, :, :, 0:16].rearrange("p a h k -> p (a h) k")
                nc.gpsimd.affine_select(out=top, in_=top, compare_op=ALU.is_ge, fill=MASKED,
                                        base=15, pattern=[[0, 2 * HG], [0, 16]], channel_multiplier=-1).then_inc(masks1, 1)
            pool.wait_ge(masks1, 1 + 2 * (P // QW))
            nc.gpsimd.memset(window[0:QW, 0, :, 0:QW], MASKED).then_inc(masks2, 1)
            nc.gpsimd.iota(back[:, :], pattern=[[-1, NPROTO]], base=NPROTO, channel_multiplier=0).then_inc(masks2, 1)
            pool.wait_ge(masks2, 2)
            pool.wait_ge(ident_ready, 1)
            nc.gpsimd.tensor_copy(m.causal[:, :], causal[:, :]).then_inc(masks_ready, 1)
            nc.gpsimd.tensor_copy(m.window[:, :, :, :], window[:, :, :, :]).then_inc(masks_ready, 1)
            nc.gpsimd.tensor_copy(m.identb[:, :], m.ident[:, :]).then_inc(masks_ready, 1)
            nc.gpsimd.tensor_copy(m.rank_back[:, :], back[:, :]).then_inc(masks_ready, 1)

        @block.vector
        def _(dve):
            dve.wait_ge(loaded, 16 * m.n_loads)
            nc.vector.tensor_scalar(t[:, 1:2], t[:, 0:1], -1.0, None, ALU.mult).then_inc(small_steps, 1)
            dve.wait_ge(small_steps, 1)
            nc.vector.tensor_tensor(t[:, 1:2], t[:, 0:1], t[:, 1:2], ALU.max).then_inc(small_steps, 1)
            dve.wait_ge(small_steps, 2)
            nc.vector.tensor_scalar(t[:, 1:2], t[:, 1:2], 0.1, -1.0, ALU.max, ALU.mult).then_inc(small_steps, 1)
            dve.wait_ge(small_steps, 3)
            nc.vector.reciprocal(m.neg_inv_t[:, :], t[:, 1:2])
            dve.wait_ge(copied, len(groups))
            nc.vector.tensor_tensor(proto2[:, :], m.protoT[:, :], m.protoT[:, :], ALU.mult).then_inc(sq_ready, 1)
            for c in range(NC):
                if c >= 2:
                    dve.wait_ge(scaled_used, c - 1)
                nc.vector.tensor_tensor(wsc[:, c % 2], bc(th[:, c, :], 2, D), bc(wo1[:, c, :], 1, H), ALU.mult)\
                  .then_inc(scaled, 1)

        @block.scalar
        def _(act):
            for n, (dst, srcs) in enumerate(groups):
                act.wait_ge(turned, n + 1)
                rows = sum(x.shape[0] for x in srcs)
                src = m.ps[n % 8][:, 0:rows]
                if len(dst.shape) == 3:
                    src = src.rearrange("p (c n) -> p c n", c=len(srcs))
                nc.scalar.copy(dst, src).then_inc(copied, 1)
            Wqk1 = m.Wqk1[:, :, :].rearrange("p (q c s) n -> p q c s n", s=2, c=4)
            Wqk0 = m.Wqk0[:, :, :].rearrange("p (c s) (r n) -> p c s r n", s=2, n=LD)
            act.wait_ge(products, 8)
            for s in range(2):
                for q in range(2):
                    nc.scalar.mul(Wqk1[:, q, :, s, :], m.ps[2 * s + q][:, :].rearrange("p (c n) -> p c n", c=4), HD ** -0.5)
                for r in range(HG):
                    nc.scalar.mul(Wqk0[:, :, s, r, :], m.ps[4 + s][:, 0:NC * LD].rearrange("p (c n) -> p c n", c=NC), HD ** -0.5)
            for j in range(HG):
                q = slice(j * LD, (j + 1) * LD)
                last = nc.scalar.copy(m.Wvo0[q, :, :], m.ps[6 + j % 2][q, :].rearrange("p (g o) -> p g o", o=D))
            last.then_inc(products_copied, 1)
            act.wait_ge(folded, 1)
            for j in range(4):
                nc.scalar.copy(m.M1[:, j * 4:(j + 1) * 4, :], m.ps[j][:, :].rearrange("p (h o) -> p h o", o=D))
            nc.scalar.copy(m.M_first[:, :], m.ps[4][:, 0:D])
            nc.scalar.copy(m.proto_sq[:, :], m.ps[5][:, 0:NPROTO])

        @block.tensor
        def _(pe):
            pe.wait_ge(loaded, 16 * m.n_loads)
            pe.wait_ge(ident_ready, 1)
            for n, (dst, srcs) in enumerate(groups):
                if n >= 8:
                    pe.wait_ge(copied, n - 7)
                rows = srcs[0].shape[0]
                for j, src in enumerate(srcs):
                    last = nc.tensor.transpose(m.ps[n % 8][:, j * rows:(j + 1) * rows], src, m.ident[0:rows, 0:rows])
                last.then_inc(turned, 1)
            pe.wait_ge(copied, len(groups))
            for s in range(2):
                k = slice(s * HD, (s + 1) * HD)
                for q in range(2):
                    for j in range(4):
                        c = 4 * q + j
                        last = nc.tensor.matmul(m.ps[2 * s + q][:, j * P:(j + 1) * P], T1[k, 0, c, :], T1[k, 1, c, :],
                                                start=True, stop=True)
                    last.then_inc(products, 1)
                for c in range(NC):
                    last = nc.tensor.matmul(m.ps[4 + s][:, c * LD:(c + 1) * LD], T0q[k, c, :], T0k[k, c, :],
                                            start=True, stop=True)
                last.then_inc(products, 1)
                for c in range(NC):
                    j, g = (2 * c + s) % HG, (2 * c + s) // HG
                    last = nc.tensor.matmul(m.ps[6 + s][j * LD:(j + 1) * LD, g * D:(g + 1) * D], T0v[k, c, :],
                                            wo0[k, c, :], start=True, stop=True)
                last.then_inc(products, 1)
            pe.wait_ge(products_copied, 1)
            pe.wait_ge(sq_ready, 1)
            pe.wait_ge(filled, 6)
            nc.tensor.matmul(m.ps[5][:, 0:NPROTO], ones[:, :], proto2[:, :], start=True, stop=True)
            for c in range(NC):
                nc.tensor.matmul(m.ps[4][:, 0:D], T1[:, 2, c, :], wo1[:, c, :], start=(c == 0), stop=(c == NC - 1))
                pe.wait_ge(scaled, c + 1)
                for j in range(4):
                    last = nc.tensor.matmul(m.ps[j][:, :], T1[:, 2, c, :],
                                            wsc[:, c % 2, j * 4:(j + 1) * 4, :].rearrange("p h o -> p (h o)"),
                                            start=(c == 0), stop=(c == NC - 1))
                last.then_inc(scaled_used, 1)
            pe.wait_ge(scaled_used, NC)
            pe.sem_inc(folded, 1)


_INS = ['L0_attn_x_bld', 'L0_attn_Wq', 'L0_attn_Wkv_down', 'L0_attn_Wk_up', 'L0_attn_Wv_up', 'L0_attn_Wout',
        'L0_ffn_gate_w', 'L0_ffn_gate_b', 'L0_ffn_expert_w', 'L0_ffn_expert_b', 'L1_attn_w_qkv', 'L1_attn_w_out',
        'L1_attn_b_out', 'L1_attn_w_th', 'L1_ffn_prototypes', 'L1_ffn_B', 'L1_ffn_A', 'L1_ffn_bias', 'L1_ffn_temp']


def kernel(**inputs):
    import numpy as _np
    import concourse.bacc as _bacc
    from concourse import mybir as _mybir
    from concourse.bass_utils import run_bass_kernel_spmd as _run

    nc = _bacc.Bacc("TRN2", target_bir_lowering=False, num_devices=1)
    arrays, args = {}, []
    for name in _INS:
        a = _np.ascontiguousarray(inputs[name])
        if name == 'L1_ffn_temp':
            a = a.reshape(1)
        arrays[f"in_{name}"] = a
        args.append(nc.dram_tensor(f"in_{name}", a.shape, _mybir.dt.from_np(a.dtype), kind="ExternalInput").ap())
    out = nc.dram_tensor("out", (NB, L, D), F32, kind="ExternalOutput").ap()
    program(nc, *args, out)
    r = _run(nc, [arrays], core_ids=[0])
    return r.results[0]["out"]
```

```python
import concourse.bass as bass
from concourse import mybir
from contextlib import ExitStack

F32 = mybir.dt.float32
BF16 = mybir.dt.bfloat16
F32R = mybir.dt.float32r
ALU = mybir.AluOpType
ACT = mybir.ActivationFunctionType
AX = mybir.AxisListType

P = 128
NB, L, D = 16, 512, 128
NT = L // P
H, HD = 16, 64
HG = 4
NE = 8
LD = 32
NPROTO, RANK = 32, 16
NR = NPROTO * RANK
QW = 32
NW = L // QW
KW = 65
EPS = 1e-5
GATE_MIN = 0.1
MASKED = -1e30
BIG = 1e30


def bc(ap, dim, n):
    shape = list(ap.shape)
    return ap.unsqueeze(dim).broadcast_to(shape[:dim] + [n] + shape[dim:])


class Count:

    def __init__(self, m, name, per=1, free=0):
        self.sem, self.per, self.base = m.semaphore(name), per, free

    def at(self, batch, k=None):
        k = self.per if k is None else k
        return batch * self.per + (k + self.base)

    def before(self, batch):
        return batch * self.per + self.base


class Chain(Count):

    def start(self, batch):
        self.batch, self.n = batch, 0

    def so_far(self, back=0):
        return self.at(self.batch, self.n - back)

    def one_more(self):
        self.n += 1
        return self.so_far()

    def end(self):
        assert self.n == self.per, (self.n, self.per)


class Norm:

    def __init__(self, nc, m, tag, xnT, psT):
        self.nc, self.m, self.xnT, self.psT = nc, m, xnT, psT
        self.bn = Count(m, tag + "_bn_partials")
        self.sums = Count(m, tag + "_sums")
        self.diff = Count(m, tag + "_square_of_difference")
        self.stats = Count(m, tag + "_mean_var")
        self.ve = Count(m, tag + "_var_eps")
        self.rstd = Count(m, tag + "_rstd")
        self.xn = Count(m, tag + "_xn")
        self.tr = Count(m, tag + "_xn_transposed")
        self.out = Count(m, tag + "_xnT")

    def dve_stats(self, eng, b):
        nc, m = self.nc, self.m
        for k in range(NT):
            last = nc.vector.bn_stats(m.st[:, k, :], m.x[:, bass.ds(b * NT + k, 1), :])
        last.then_inc(self.bn.sem, 1)
        eng.wait_ge(self.bn.sem, self.bn.at(b))
        nc.vector.tensor_tensor(m.sums[:, 0, :], m.st[:, :, 1], m.st[:, :, 4], ALU.add)
        nc.vector.tensor_tensor(m.sums[:, 1, :], m.st[:, :, 1], m.st[:, :, 4], ALU.subtract)
        nc.vector.tensor_tensor(m.sums[:, 2, :], m.st[:, :, 2], m.st[:, :, 5], ALU.add).then_inc(self.sums.sem, 1)
        eng.wait_ge(self.sums.sem, self.sums.at(b))
        nc.vector.tensor_scalar(m.mean[:, :], m.sums[:, 0, :], 0.5, None, ALU.mult)
        nc.vector.scalar_tensor_tensor(m.sums[:, 3, :], m.sums[:, 1, :], 0.25, m.sums[:, 1, :],
                                       ALU.mult, ALU.mult).then_inc(self.diff.sem, 1)
        eng.wait_ge(self.diff.sem, self.diff.at(b))
        nc.vector.scalar_tensor_tensor(m.var[:, :], m.sums[:, 2, :], 1.0 / D, m.sums[:, 3, :],
                                       ALU.mult, ALU.add).then_inc(self.stats.sem, 1)

    def pool_rstd(self, eng, b):
        nc, m = self.nc, self.m
        eng.wait_ge(self.stats.sem, self.stats.at(b))
        nc.gpsimd.tensor_tensor(m.var_eps[:, :], m.var[:, :], m.eps[:, :], ALU.add).then_inc(self.ve.sem, 1)
        eng.wait_ge(self.ve.sem, self.ve.at(b))
        nc.gpsimd.tensor_tensor(m.rstd[:, :], m.var_eps[:, :], m.neg_half[:, :], ALU.pow).then_inc(self.rstd.sem, 1)

    def dve_apply(self, eng, b, first=False):
        nc, m = self.nc, self.m
        eng.wait_ge(self.stats.sem, self.stats.at(b))
        eng.wait_ge(self.rstd.sem, self.rstd.at(b))
        if not first:
            eng.wait_ge(self.tr.sem, self.tr.before(b))
        for k in range(NT):
            last = nc.vector.tensor_scalar(m.xn[:, k, :], m.x[:, b * NT + k, :], m.mean[:, k:k + 1],
                                           m.rstd[:, k:k + 1], ALU.subtract, ALU.mult)
        last.then_inc(self.xn.sem, 1)

    def pe(self, eng, b, first=False):
        nc, m = self.nc, self.m
        eng.wait_ge(self.xn.sem, self.xn.at(b))
        if not first:
            eng.wait_ge(self.out.sem, self.out.before(b))
        for k in range(NT):
            last = nc.tensor.transpose(self.psT[:, k * P:(k + 1) * P], m.xn[:, k, :], m.ident[:, :])
        last.then_inc(self.tr.sem, 1)

    def act(self, eng, b, parity):
        eng.wait_ge(self.tr.sem, self.tr.at(b))
        self.nc.scalar.copy(self.xnT(parity), self.psT[:, 0:L]).then_inc(self.out.sem, 1)


def both_parities(eng, body):
    with eng.Fori(0, NB // 2) as i:
        for parity in range(2):
            body(i * 2 + parity, parity)


def moe_stage(nc, m, tag):
    c = lambda name, per=1, free=0: Count(m, f"{tag}_{name}", per, free)
    logits, lg_c, e_done, w_done = c("logits"), c("logits_centred"), c("gate_exp"), c("weights")
    wt_ps, wt_sb, bias_ps = c("weightsT"), c("weightsT_copied"), c("bias_product")
    y, yact, ysum = c("expert_products", NT), c("parts_by_act", NT, 2), c("parts_summed", NT, 2)
    added = c("tile_added", NT, 2)
    bias_used = c("bias_added", 1, 1)
    gate = Chain(m, f"{tag}_gate_steps", 9)
    mix = Chain(m, f"{tag}_mix_steps", NT * 3, 4)
    sums = Chain(m, f"{tag}_sum_steps", 2)
    ctx = ExitStack()
    with ctx:
        sb = lambda n, s: ctx.enter_context(nc.sbuf_tensor(f"{tag}_{n}", s, F32))
        lg = sb("lg", [P, NT, NE])
        ex = sb("ex", [P, NT, NE])
        small = sb("small", [P, 8, NT])
        w = sb("w", [P, 2, NT, 32])
        wT = sb("wT", [P, P])
        part = sb("part", [P, 2, 6, D])
        sum3 = sb("sum3", [P, 2, 3, D])
        sum2 = sb("sum2", [P, 2, D])
        total = sb("total", [P, 2, D])
        xnT = sb("xnT", [P, 2, L])
        psT, psG, psW, psB = m.ps[0], m.ps[1], m.ps[1], m.ps[2]
        psY = [m.ps[3:5], m.ps[5:7]]
        norm = Norm(nc, m, tag, lambda par: xnT[:, par, :], psT)
        w_zero = m.semaphore(f"{tag}_w_zeroed")

        block = ctx.enter_context(nc.Block())

        @block.gpsimd
        def _(pool):
            pool.sem_inc(ysum.sem, 2)
            norm.pool_rstd(pool, 0)
            norm.pool_rstd(pool, 1)

            def body(b, par):
                for k in range(NT):
                    q = k % 2
                    if k == 1:
                        norm.pool_rstd(pool, b + 2)
                    sums.start(b * NT + k)
                    pool.wait_ge(yact.sem, yact.at(b, k + 1))
                    pool.wait_ge(mix.sem, mix.at(b, 3 * k + 2))
                    nc.gpsimd.tensor_tensor(sum3[:, q], part[:, q, 0:3], part[:, q, 3:6], ALU.add).then_inc(sums.sem, 1)
                    pool.wait_ge(sums.sem, sums.one_more())
                    nc.gpsimd.tensor_tensor(sum2[:, q], sum3[:, q, 0], sum3[:, q, 1], ALU.add).then_inc(sums.sem, 1)
                    pool.wait_ge(sums.sem, sums.one_more())
                    sums.end()
                    pool.wait_ge(added.sem, added.at(b, k - 1))
                    nc.gpsimd.tensor_tensor(total[:, q], sum2[:, q], sum3[:, q, 2], ALU.add).then_inc(ysum.sem, 1)
            both_parities(pool, body)

        @block.vector
        def _(dve):
            dve.sem_inc(mix.sem, 4)
            dve.sem_inc(added.sem, 2)
            dve.sem_inc(bias_used.sem, 1)
            nc.vector.memset(w[:, :, :, :], 0.0).then_inc(w_zero, 1)
            dve.wait_ge(w_zero, 1)

            def gates_in(b):
                gate.start(b)
                dve.wait_ge(logits.sem, logits.at(b))
                nc.vector.tensor_tensor(lg[:, :, :], psG[:, 0:NT * NE].rearrange("p (k e) -> p k e", e=NE),
                                        bc(m.gate_b[:, :], 1, NT), ALU.add).then_inc(gate.sem, 1)
                dve.wait_ge(gate.sem, gate.one_more())
                nc.vector.tensor_reduce(small[:, 0, :], lg[:, :, :], AX.X, ALU.max).then_inc(gate.sem, 1)
                dve.wait_ge(gate.sem, gate.one_more())
                nc.vector.tensor_tensor(lg[:, :, :], lg[:, :, :], bc(small[:, 0, :], 2, NE), ALU.subtract).then_inc(lg_c.sem, 1)

            def gates_out(b, par):
                dve.wait_ge(e_done.sem, e_done.at(b))
                nc.vector.tensor_reduce(small[:, 1, :], ex[:, :, :], AX.X, ALU.add).then_inc(gate.sem, 1)
                dve.wait_ge(gate.sem, gate.one_more())
                nc.vector.reciprocal(small[:, 2, :], small[:, 1, :]).then_inc(gate.sem, 1)
                dve.wait_ge(gate.sem, gate.one_more())
                nc.vector.tensor_tensor(ex[:, :, :], ex[:, :, :], bc(small[:, 2, :], 2, NE), ALU.mult).then_inc(gate.sem, 1)
                dve.wait_ge(gate.sem, gate.one_more())
                nc.vector.scalar_tensor_tensor(lg[:, :, :], ex[:, :, :], GATE_MIN, ex[:, :, :],
                                               ALU.is_ge, ALU.mult).then_inc(gate.sem, 1)
                dve.wait_ge(gate.sem, gate.one_more())
                nc.vector.tensor_reduce(small[:, 3, :], lg[:, :, :], AX.X, ALU.add).then_inc(gate.sem, 1)
                dve.wait_ge(gate.sem, gate.one_more())
                nc.vector.scalar_tensor_tensor(small[:, 4, :], small[:, 3, :], 0.0, small[:, 3, :],
                                               ALU.is_equal, ALU.add).then_inc(gate.sem, 1)
                dve.wait_ge(gate.sem, gate.one_more())
                nc.vector.reciprocal(small[:, 5, :], small[:, 4, :]).then_inc(gate.sem, 1)
                dve.wait_ge(gate.sem, gate.one_more())
                nc.vector.scalar_tensor_tensor(w[:, par, :, 0:NE], lg[:, :, :], 0.5,
                                               bc(small[:, 5, :], 2, NE), ALU.mult, ALU.mult).then_inc(w_done.sem, 1)
                gate.end()

            norm.dve_stats(dve, 0)
            norm.dve_apply(dve, 0, True)
            norm.dve_stats(dve, 1)
            norm.dve_apply(dve, 1)
            gates_in(0)
            gates_out(0, 0)

            def body(b, par):
                mix.start(b)
                dve.wait_ge(w_done.sem, w_done.at(b))

                def tile(k):
                    dve.wait_ge(y.sem, y.at(b, k + 1))
                    xk, bank = m.x[:, b * NT + k, :], psY[k % 2][0]
                    nc.vector.scalar_tensor_tensor(xk, bank[:, 0:D], w[:, par, k, 0:1], xk, ALU.mult, ALU.add)\
                      .then_inc(mix.sem, 1)
                    mix.one_more()
                    dve.wait_ge(ysum.sem, ysum.at(b, k - 1))
                    nc.vector.tensor_scalar(part[:, k % 2, 5], bank[:, D:2 * D], w[:, par, k, 1:2], None, ALU.mult)\
                      .then_inc(mix.sem, 1)
                    mix.one_more()
                    dve.wait_ge(mix.sem, mix.so_far(back=1))
                    nc.vector.scalar_tensor_tensor(xk, bank[:, 2 * D:3 * D], w[:, par, k, 2:3], xk, ALU.mult, ALU.add)\
                      .then_inc(mix.sem, 1)
                    mix.one_more()

                def finish(k):
                    dve.wait_ge(mix.sem, mix.at(b, 3 * k + 3))
                    dve.wait_ge(ysum.sem, ysum.at(b, k + 1))
                    xk = m.x[:, b * NT + k, :]
                    nc.vector.tensor_tensor(xk, xk, total[:, k % 2], ALU.add).then_inc(added.sem, 1)
                tile(0)
                norm.dve_stats(dve, b + 2)
                tile(1)
                finish(0)
                gates_in(b + 1)
                norm.dve_apply(dve, b + 2)
                tile(2)
                finish(1)
                gates_out(b + 1, 1 - par)
                tile(3)
                finish(2)
                dve.wait_ge(bias_ps.sem, bias_ps.at(b))
                dve.wait_ge(mix.sem, mix.so_far())
                dve.wait_ge(added.sem, added.at(b, NT - 1))
                xb = m.x[:, bass.ds(b * NT, NT), :]
                nc.vector.tensor_tensor(xb, xb, psB[:, :].rearrange("p (k o) -> p k o", o=D), ALU.add)\
                  .then_inc(bias_used.sem, 1)
                dve.wait_ge(bias_used.sem, bias_used.at(b))
                finish(3)
                mix.end()
            both_parities(dve, body)

        @block.scalar
        def _(act):
            act.sem_inc(yact.sem, 2)

            def gate_exp(b):
                act.wait_ge(lg_c.sem, lg_c.at(b))
                nc.scalar.activation(ex[:, :, :], lg[:, :, :], ACT.Exp).then_inc(e_done.sem, 1)
            norm.act(act, 0, 0)
            gate_exp(0)

            def body(b, par):
                act.wait_ge(w_done.sem, w_done.at(b))

                def tile(k):
                    act.wait_ge(y.sem, y.at(b, k + 1))
                    act.wait_ge(ysum.sem, ysum.at(b, k - 1))
                    for e in (4, 5, 6, 7, 3):
                        if e == 3:
                            act.wait_ge(mix.sem, mix.at(b, 3 * k + 3))
                        ye = psY[k % 2][e // 4][:, e % 4 * D:(e % 4 + 1) * D]
                        last = nc.scalar.activation(part[:, k % 2, e - 3], ye, ACT.Copy, scale=w[:, par, k, e:e + 1])
                    last.then_inc(yact.sem, 1)
                tile(0)
                act.wait_ge(wt_ps.sem, wt_ps.at(b))
                nc.scalar.copy(wT[:, :], psW[:, 256:384]).then_inc(wt_sb.sem, 1)
                norm.act(act, b + 1, 1 - par)
                tile(1)
                gate_exp(b + 1)
                tile(2)
                tile(3)
            both_parities(act, body)

        @block.tensor
        def _(pe):
            def gates(b, par, first=False):
                pe.wait_ge(norm.out.sem, norm.out.at(b))
                if not first:
                    pe.wait_ge(wt_sb.sem, wt_sb.before(b))
                for k in range(NT):
                    last = nc.tensor.matmul(psG[:, k * NE:(k + 1) * NE], xnT[:, par, k * P:(k + 1) * P],
                                            m.gate_w[:, :], start=True, stop=True)
                last.then_inc(logits.sem, 1)
            norm.pe(pe, 0, True)
            gates(0, 0, True)

            def body(b, par):
                def tile(k):
                    pe.wait_ge(mix.sem, mix.at(b, 3 * (k - 1)))
                    pe.wait_ge(yact.sem, yact.at(b, k - 1))
                    for half in range(2):
                        last = nc.tensor.matmul(psY[k % 2][half][:, :], xnT[:, par, k * P:(k + 1) * P],
                                                m.expert_w[:, half * L:(half + 1) * L], start=True, stop=True)
                    last.then_inc(y.sem, 1)
                tile(0)
                pe.wait_ge(w_done.sem, w_done.at(b))
                nc.tensor.transpose(psW[:, 256:384], w[:, par, :, :].rearrange("p k e -> p (k e)"),
                                    m.ident[:, :]).then_inc(wt_ps.sem, 1)
                norm.pe(pe, b + 1)
                tile(1)
                gates(b + 1, 1 - par)
                tile(2)
                pe.wait_ge(wt_sb.sem, wt_sb.at(b))
                pe.wait_ge(bias_used.sem, bias_used.before(b))
                nc.tensor.matmul(psB[:, :], wT[:, :], m.expert_b[:, :, :].rearrange("p k o -> p (k o)"),
                                 start=True, stop=True).then_inc(bias_ps.sem, 1)
                tile(3)
            both_parities(pe, body)


def proto_stage(nc, m, tag):
    c = lambda name, per=1, free=0: Count(m, f"{tag}_{name}", per, free)
    cross, sq, pair_done, dist_done = c("cross_products"), c("xn_squares"), c("two_smallest"), c("distances")
    gap, e_done, w_done = c("distance_gap"), c("second_exp"), c("weights")
    wt_ps, wt_sb, bias_ps, bias_used = c("weightsT"), c("weightsT_copied", 1, 1), c("bias_product"), c("bias_added", 1, 1)
    h, hw_done, ht, ht_sb = c("down", NT), c("down_weighted", NT, 1), c("downT", NT), c("downT_copied", NT, 1)
    up, up_sb, o, added = c("up"), c("up_copied"), c("up_transposed"), c("x_added", 1, 1)
    near = Chain(m, f"{tag}_distance_steps", 3)
    top = Chain(m, f"{tag}_nearest_steps", 16)
    ctx = ExitStack()
    with ctx:
        sb = lambda n, s: ctx.enter_context(nc.sbuf_tensor(f"{tag}_{n}", s, F32))
        scratch = sb("square_out", [P, NT, D])
        x2 = sb("x2", [P, NT])
        d2 = sb("d2", [P, NT, NPROTO])
        dist = sb("dist", [P, 2, NT])
        eq = sb("eq", [P, NT, NPROTO])
        rest = sb("rest", [P, NT, NPROTO])
        key = sb("key", [P, NT, NPROTO])
        first = sb("first", [P, NT, NPROTO])
        second = sb("second", [P, NT, NPROTO])
        small = sb("small", [P, 10, NT])
        w = sb("w", [P, NT, NPROTO])
        wT = sb("wT", [P, P])
        hw = sb("hw", [P, 2, NPROTO, RANK])
        hwT = sb("hwT", [P, NR // P, L])
        upT = sb("upT", [P, L])
        xnT = sb("xnT", [P, 2, L])
        psT, psD, psW, psB, psU = m.ps[0], m.ps[1], m.ps[1], m.ps[2], m.ps[7]
        psH, psHT = m.ps[3:5], m.ps[5:7]
        norm = Norm(nc, m, tag, lambda par: xnT[:, par, :], psT)
        block = ctx.enter_context(nc.Block())

        @block.gpsimd
        def _(pool):
            def distances(b):
                pool.wait_ge(pair_done.sem, pair_done.at(b))
                nc.gpsimd.tensor_tensor(dist[:, :, :], small[:, 0:3:2, :], m.half[:, :, :], ALU.pow).then_inc(dist_done.sem, 1)
            norm.pool_rstd(pool, 0)
            norm.pool_rstd(pool, 1)
            distances(0)

            def body(b, par):
                distances(b + 1)
                norm.pool_rstd(pool, b + 2)
            both_parities(pool, body)

        @block.vector
        def _(dve):
            def square_distance(b):
                near.start(b)
                dve.wait_ge(cross.sem, cross.at(b))
                nc.vector.scalar_tensor_tensor(d2[:, :, :], psD[:, 0:P].rearrange("p (k n) -> p k n", n=NPROTO),
                                               -2.0, bc(m.proto_sq[:, :], 1, NT), ALU.mult, ALU.add).then_inc(near.sem, 1)
                dve.wait_ge(near.sem, near.one_more())
                dve.wait_ge(sq.sem, sq.at(b))
                nc.vector.tensor_tensor(d2[:, :, :], d2[:, :, :], bc(x2[:, :], 2, NPROTO), ALU.add).then_inc(near.sem, 1)
                dve.wait_ge(near.sem, near.one_more())
                nc.vector.tensor_scalar(d2[:, :, :], d2[:, :, :], 0.0, None, ALU.max).then_inc(near.sem, 1)
                dve.wait_ge(near.sem, near.one_more())
                near.end()

            def smallest(value, onehot, at, done):
                v, kmax = small[:, at, :], small[:, at + 1, :]
                nc.vector.tensor_reduce(v, value, AX.X, ALU.min).then_inc(top.sem, 1)
                dve.wait_ge(top.sem, top.one_more())
                nc.vector.tensor_tensor(eq[:, :, :], value, bc(v, 2, NPROTO), ALU.is_equal).then_inc(top.sem, 1)
                dve.wait_ge(top.sem, top.one_more())
                nc.vector.tensor_tensor(key[:, :, :], eq[:, :, :], bc(m.rank_back[:, :], 1, NT), ALU.mult).then_inc(top.sem, 1)
                dve.wait_ge(top.sem, top.one_more())
                nc.vector.tensor_reduce(kmax, key[:, :, :], AX.X, ALU.max).then_inc(top.sem, 1)
                dve.wait_ge(top.sem, top.one_more())
                nc.vector.tensor_tensor(onehot, key[:, :, :], bc(kmax, 2, NPROTO), ALU.is_equal).then_inc(done.sem, 1)

            def nearest_in(b):
                top.start(b)
                smallest(d2[:, :, :], first[:, :, :], 0, top)
                dve.wait_ge(top.sem, top.one_more())
                nc.vector.scalar_tensor_tensor(rest[:, :, :], first[:, :, :], BIG, d2[:, :, :], ALU.mult, ALU.add).then_inc(top.sem, 1)
                dve.wait_ge(top.sem, top.one_more())
                smallest(rest[:, :, :], second[:, :, :], 2, pair_done)

            def nearest_gap(b):
                dve.wait_ge(dist_done.sem, dist_done.at(b))
                nc.vector.tensor_tensor(small[:, 4, :], dist[:, 1, :], dist[:, 0, :], ALU.subtract).then_inc(gap.sem, 1)

            def nearest_out(b):
                dve.wait_ge(pair_done.sem, pair_done.at(b))
                dve.wait_ge(e_done.sem, e_done.at(b))
                nc.vector.tensor_scalar(small[:, 6, :], small[:, 5, :], 1.0, None, ALU.add).then_inc(top.sem, 1)
                dve.wait_ge(top.sem, top.one_more())
                nc.vector.reciprocal(small[:, 7, :], small[:, 6, :]).then_inc(top.sem, 1)
                dve.wait_ge(top.sem, top.one_more())
                nc.vector.tensor_scalar(small[:, 8, :], small[:, 7, :], 0.5, None, ALU.mult).then_inc(top.sem, 1)
                top.one_more()
                nc.vector.scalar_tensor_tensor(small[:, 9, :], small[:, 5, :], 0.5, small[:, 7, :], ALU.mult, ALU.mult).then_inc(top.sem, 1)
                dve.wait_ge(top.sem, top.one_more())
                nc.vector.tensor_tensor(first[:, :, :], first[:, :, :], bc(small[:, 8, :], 2, NPROTO), ALU.mult).then_inc(top.sem, 1)
                top.one_more()
                nc.vector.tensor_tensor(second[:, :, :], second[:, :, :], bc(small[:, 9, :], 2, NPROTO), ALU.mult).then_inc(top.sem, 1)
                dve.wait_ge(top.sem, top.one_more())
                top.end()
                nc.vector.tensor_tensor(w[:, :, :], first[:, :, :], second[:, :, :], ALU.add).then_inc(w_done.sem, 1)

            dve.sem_inc(hw_done.sem, 1)
            dve.sem_inc(bias_used.sem, 1)
            dve.sem_inc(added.sem, 1)
            norm.dve_stats(dve, 0)
            norm.dve_apply(dve, 0, True)
            norm.dve_stats(dve, 1)
            dve.wait_ge(sq.sem, sq.at(0))
            norm.dve_apply(dve, 1)
            square_distance(0)
            nearest_in(0)
            nearest_gap(0)
            nearest_out(0)

            def body(b, par):
                def weigh(k):
                    dve.wait_ge(h.sem, h.at(b, k + 1))
                    if k >= 2:
                        dve.wait_ge(ht.sem, ht.at(b, k - 1))
                    nc.vector.tensor_tensor(hw[:, k % 2], psH[k % 2][:, :].rearrange("p (n r) -> p n r", r=RANK),
                                            bc(w[:, k, :], 2, RANK), ALU.mult).then_inc(hw_done.sem, 1)
                dve.wait_ge(w_done.sem, w_done.at(b))
                weigh(0)
                weigh(1)
                square_distance(b + 1)
                weigh(2)
                weigh(3)
                nearest_in(b + 1)
                norm.dve_stats(dve, b + 2)
                nearest_gap(b + 1)
                xb = m.x[:, bass.ds(b * NT, NT), :]
                dve.wait_ge(bias_ps.sem, bias_ps.at(b))
                nc.vector.tensor_tensor(xb, xb, psB[:, :].rearrange("p (k o) -> p k o", o=D), ALU.add)\
                  .then_inc(bias_used.sem, 1)
                dve.wait_ge(sq.sem, sq.at(b + 1))
                norm.dve_apply(dve, b + 2)
                nearest_out(b + 1)
                dve.wait_ge(o.sem, o.at(b))
                dve.wait_ge(bias_used.sem, bias_used.at(b))
                nc.vector.tensor_tensor(xb, xb, psU[:, :].rearrange("p (k o) -> p k o", o=D), ALU.add)\
                  .then_inc(added.sem, 1)
            both_parities(dve, body)

        @block.scalar
        def _(act):
            def squares(b):
                act.wait_ge(norm.xn.sem, norm.xn.at(b))
                for k in range(NT):
                    last = nc.scalar.activation(scratch[:, k, :], m.xn[:, k, :], ACT.Square, accum_out=x2[:, k:k + 1])
                last.then_inc(sq.sem, 1)

            def second_exp(b):
                act.wait_ge(gap.sem, gap.at(b))
                nc.scalar.activation(small[:, 5, :], small[:, 4, :], ACT.Exp, scale=m.neg_inv_t[:, 0:1]).then_inc(e_done.sem, 1)
            act.sem_inc(wt_sb.sem, 1)
            act.sem_inc(ht_sb.sem, 1)
            norm.act(act, 0, 0)
            squares(0)
            second_exp(0)

            def body(b, par):
                def copy_back(k):
                    act.wait_ge(ht.sem, ht.at(b, k + 1))
                    nc.scalar.copy(hwT[:, :, k * P:(k + 1) * P],
                                   psHT[k % 2][:, :].rearrange("p (c t) -> p c t", t=P)).then_inc(ht_sb.sem, 1)
                squares(b + 1)
                norm.act(act, b + 1, 1 - par)
                act.wait_ge(wt_ps.sem, wt_ps.at(b))
                nc.scalar.copy(wT[:, :], psW[:, 256:384]).then_inc(wt_sb.sem, 1)
                copy_back(0)
                copy_back(1)
                copy_back(2)
                copy_back(3)
                second_exp(b + 1)
                act.wait_ge(up.sem, up.at(b))
                nc.scalar.copy(upT[:, :], psU[:, :]).then_inc(up_sb.sem, 1)
            both_parities(act, body)

        @block.tensor
        def _(pe):
            def crosses(b, par):
                pe.wait_ge(norm.out.sem, norm.out.at(b))
                pe.wait_ge(wt_sb.sem, wt_sb.before(b))
                for k in range(NT):
                    last = nc.tensor.matmul(psD[:, k * NPROTO:(k + 1) * NPROTO], xnT[:, par, k * P:(k + 1) * P],
                                            m.protoT[:, :], start=True, stop=True)
                last.then_inc(cross.sem, 1)
            norm.pe(pe, 0, True)
            crosses(0, 0)

            def body(b, par):
                def down(k):
                    if k >= 2:
                        pe.wait_ge(hw_done.sem, hw_done.at(b, k - 1))
                    else:
                        pe.wait_ge(hw_done.sem, hw_done.before(b))
                    nc.tensor.matmul(psH[k % 2][:, :], xnT[:, par, k * P:(k + 1) * P],
                                     m.BT[:, :, :].rearrange("p c r -> p (c r)"), start=True, stop=True).then_inc(h.sem, 1)

                def turn(k):
                    pe.wait_ge(hw_done.sem, hw_done.at(b, k + 1))
                    if k >= 2:
                        pe.wait_ge(ht_sb.sem, ht_sb.at(b, k - 1))
                    else:
                        pe.wait_ge(ht_sb.sem, ht_sb.before(b))
                    flat = hw[:, k % 2].rearrange("p n r -> p (n r)")
                    for q in range(NR // P):
                        last = nc.tensor.transpose(psHT[k % 2][:, q * P:(q + 1) * P], flat[:, q * P:(q + 1) * P],
                                                   m.ident[:, :])
                    last.then_inc(ht.sem, 1)
                down(0)
                norm.pe(pe, b + 1)
                down(1)
                pe.wait_ge(w_done.sem, w_done.at(b))
                nc.tensor.transpose(psW[:, 256:384], w[:, :, :].rearrange("p k n -> p (k n)"), m.ident[:, :]).then_inc(wt_ps.sem, 1)
                turn(0)
                crosses(b + 1, 1 - par)
                down(2)
                turn(1)
                down(3)
                turn(2)
                pe.wait_ge(wt_sb.sem, wt_sb.at(b))
                pe.wait_ge(bias_used.sem, bias_used.before(b))
                nc.tensor.matmul(psB[:, :], wT[:, :], m.proto_b[:, :, :].rearrange("p k o -> p (k o)"),
                                 start=True, stop=True).then_inc(bias_ps.sem, 1)
                turn(3)
                pe.wait_ge(ht_sb.sem, ht_sb.at(b))
                pe.wait_ge(added.sem, added.before(b))
                for q in range(NR // P):
                    last = nc.tensor.matmul(psU[:, :], m.AT[:, q, :], hwT[:, q, :], start=(q == 0), stop=(q == NR // P - 1))
                last.then_inc(up.sem, 1)
                pe.wait_ge(up_sb.sem, up_sb.at(b))
                for k in range(NT):
                    last = nc.tensor.transpose(psU[:, k * P:(k + 1) * P], upT[:, k * P:(k + 1) * P], m.ident[:, :])
                last.then_inc(o.sem, 1)
            both_parities(pe, body)


def latent_stage(nc, m, tag):
    NQ, NG = NT, H // HG
    NU = NQ * NG
    NPJ = H + 2
    LEAD = 3
    units = [(u // NG, u % NG) for u in range(NU)]
    c = lambda name, per=1, free=0: Count(m, f"{tag}_{name}", per, free)
    proj, high, low = c("projections", NPJ), c("high_halves", NPJ - 1), c("projections_done", NPJ)
    scores, mx, exp, inv = c("scores", 2 * NU), c("row_maxima", 2 * NU), c("probabilities", 2 * NU, 1), c("row_sums_inverted", NU)
    normed, turned = c("probabilities_normed", NU), c("probabilities_transposed", sum(q + 1 for q, _ in units), 1)
    z, z_sb, o, added = c("z", NU), c("z_copied", NU, 1), c("attended", NQ), c("x_added", NQ, 1)

    def by_dve(qb, k):
        return k >= 2 or (qb in (1, 2) and k == 1)
    all_jobs = [(u, k) for u, (qb, _) in enumerate(units) for k in range(qb + 1)]
    back = {True: c("pT_copied_dve", sum(by_dve(units[u][0], k) for u, k in all_jobs), 1),
            False: c("pT_copied_act", sum(not by_dve(units[u][0], k) for u, k in all_jobs), 1)}

    def copies(dve, n):
        return sum(by_dve(units[u][0], k) == dve for u, k in all_jobs[:n])

    def jobs_before(u):
        return sum(qb + 1 for qb, _ in units[:u])

    projections_of = {s: [s - LEAD] if s < NU - 1 else [2 * s - NU - 2, 2 * s - NU - 1] for s in range(LEAD, NU + 2)}
    assert [n for s in sorted(projections_of) for n in projections_of[s]] == list(range(NPJ))

    def unit_of(b, par, s):
        return (b, par, s) if s < NU else (b + 1, 1 - par, s - NU)
    ctx = ExitStack()
    with ctx:
        sb = lambda n, s, dt=F32: ctx.enter_context(nc.sbuf_tensor(f"{tag}_{n}", s, dt))
        xnT = sb("xnT", [P, 2, L])
        qS = sb("q_stack", [P, 2, H, L], F32R)
        latS = sb("latent_stack", [P, 2, L], F32R)
        lat = sb("lat", [P, 2, NT, LD])
        p = sb("p", [P, 4, HG, L])
        pT = sb("pT", [P, 2, NT, L])
        nmax = sb("nmax", [P, 2, HG])
        rsum = sb("rsum", [P, 4, HG])
        rinv = sb("rinv", [P, 4, HG])
        zT = sb("zT", [P, 2, NG, P])
        psS = m.psS[:, :].rearrange("p (h t) -> p h t", t=L)
        psP, psZ, psO, psJ = m.ps[4:6], m.ps[6][:, 0:P], m.ps[6][:, P:2 * P], m.ps[7]
        norm = Norm(nc, m, tag, lambda par: xnT[:, par, :], psJ)
        block = ctx.enter_context(nc.Block())

        @block.gpsimd
        def _(pool):
            norm.pool_rstd(pool, 0)

            norm.pool_rstd(pool, 1)

            def normalise(b, u):
                pool.wait_ge(inv.sem, inv.at(b, u + 1))
                n = (units[u][0] + 1) * P
                pu = p[:, u % 4, :, 0:n]
                nc.gpsimd.tensor_tensor(pu, pu, bc(rinv[:, u % 4, :], 2, n), ALU.mult).then_inc(normed.sem, 1)
            for u in range(LEAD - 1):
                normalise(0, u)

            def body(b, par):
                for s in range(LEAD - 1, NU):
                    normalise(b, s)
                norm.pool_rstd(pool, b + 2)
                for u in range(LEAD - 1):
                    normalise(b + 1, u)
            both_parities(pool, body)

        @block.vector
        def _(dve):
            def lower(b, par, n):
                if n == 1:
                    dve.wait_ge(proj.sem, proj.at(b, n + 1))
                    nc.vector.tensor_copy(lat[:, par, :, :], psJ[:, 0:NT * LD].rearrange("p (k c) -> p k c", c=LD)).then_inc(low.sem, 1)
                    return
                dve.wait_ge(high.sem, high.at(b, max(n, 1)))
                stack, rows = (qS[:, par, n - 2, :], [(2 * LD, 4 * LD)]) if n else (latS[:, par, :], [(LD, 2 * LD), (3 * LD, P)])
                for r0, r1 in rows:
                    last = nc.vector.tensor_tensor(stack[r0:r1], psJ[r0:r1, :], stack[r0:r1].bitcast(F32), ALU.subtract)
                last.then_inc(low.sem, 1)

            def maxima(b, u, pair):
                dve.wait_ge(scores.sem, scores.at(b, 2 * u + pair + 1))
                hs = slice(2 * pair, 2 * pair + 2)
                nc.vector.tensor_reduce(nmax[:, u % 2, hs], psS[:, hs, 0:(units[u][0] + 1) * P], AX.X, ALU.max,
                                        negate=True).then_inc(mx.sem, 1)

            def invert(b, u):
                dve.wait_ge(exp.sem, exp.at(b, 2 * u + 2))
                nc.vector.reciprocal(rinv[:, u % 4, :], rsum[:, u % 4, :]).then_inc(inv.sem, 1)

            def copy_back(b, u):
                for k in range(units[u][0] + 1):
                    if by_dve(units[u][0], k):
                        n = jobs_before(u) + k
                        dve.wait_ge(turned.sem, turned.at(b, n + 1))
                        nc.vector.tensor_copy(pT[:, u % 2, k, :], psP[n % 2][:, :]).then_inc(back[True].sem, 1)

            def add(b, qb):
                dve.wait_ge(o.sem, o.at(b, qb + 1))
                xq = m.x[:, b * NT + qb, :]
                nc.vector.tensor_tensor(xq, xq, psO, ALU.add).then_inc(added.sem, 1)

            def step(b, par, s):
                if s:
                    b_, _, u = unit_of(b, par, s - 1)
                    invert(b_, u)
                b_, _, u = unit_of(b, par, s)
                maxima(b_, u, 0)
                if s - 1 in projections_of:
                    lower(b + 1, 1 - par, projections_of[s - 1][-1])
                maxima(b_, u, 1)
                for n in projections_of.get(s, [])[:-1]:
                    lower(b + 1, 1 - par, n)
                if s >= 2:
                    b_, _, u = unit_of(b, par, s - 2)
                    copy_back(b_, u)
                if s >= 6 and (s - 6) % NG == 0:
                    add(b, (s - 6) // NG)
            dve.sem_inc(back[True].sem, 1)
            dve.sem_inc(added.sem, 1)
            norm.dve_stats(dve, 0)
            norm.dve_apply(dve, 0, True)
            norm.dve_stats(dve, 1)
            norm.dve_apply(dve, 1)
            for n in range(NPJ):
                lower(0, 0, n)
            for s in range(LEAD):
                step(0, 0, s)

            def body(b, par):
                for s in range(LEAD, LEAD + NU):
                    step(b, par, s)
                    if s == NU:
                        norm.dve_stats(dve, b + 2)
                    if s == NU + 1:
                        norm.dve_apply(dve, b + 2)
            both_parities(dve, body)

        @block.scalar
        def _(act):
            def raise_(b, par, n):
                if n != 1:
                    act.wait_ge(proj.sem, proj.at(b, n + 1))
                    nc.scalar.copy(qS[:, par, n - 2, :] if n else latS[:, par, :], psJ[:, :]).then_inc(high.sem, 1)

            def exponents(b, u, pair, first):
                n = (units[u][0] + 1) * P
                if u >= 4:
                    act.wait_ge(turned.sem, turned.at(b, jobs_before(u - 3)))
                elif u == 3:
                    act.wait_ge(turned.sem, turned.before(b))
                elif not first:
                    act.wait_ge(turned.sem, turned.at(b - 1, jobs_before(NU + u - 3)))
                act.wait_ge(mx.sem, mx.at(b, 2 * u + pair + 1))
                for j in (2 * pair, 2 * pair + 1):
                    last = nc.scalar.activation(p[:, u % 4, j, 0:n], psS[:, j, 0:n], ACT.Exp,
                                                bias=nmax[:, u % 2, j:j + 1], accum_out=rsum[:, u % 4, j:j + 1])
                last.then_inc(exp.sem, 1)

            def copy_back(b, u):
                for k in range(units[u][0] + 1):
                    if not by_dve(units[u][0], k):
                        n = jobs_before(u) + k
                        act.wait_ge(turned.sem, turned.at(b, n + 1))
                        nc.scalar.copy(pT[:, u % 2, k, :], psP[n % 2][:, :]).then_inc(back[False].sem, 1)

            def copy_z(b, u):
                qb, g = units[u]
                act.wait_ge(z.sem, z.at(b, u + 1))
                nc.scalar.copy(zT[:, qb % 2, g, :], psZ).then_inc(z_sb.sem, 1)

            def step(b, par, s, first=False):
                b_, _, u = unit_of(b, par, s)
                exponents(b_, u, 0, first)
                if s >= 3:
                    b_, _, u = unit_of(b, par, s - 3)
                    copy_z(b_, u)
                if s >= 2:
                    b_, _, u = unit_of(b, par, s - 2)
                    copy_back(b_, u)
                jobs = projections_of.get(s, [])
                for n in jobs[:-1]:
                    raise_(b + 1, 1 - par, n)
                b_, _, u = unit_of(b, par, s)
                exponents(b_, u, 1, first)
                for n in jobs[-1:]:
                    raise_(b + 1, 1 - par, n)
            act.sem_inc(back[False].sem, 1)
            act.sem_inc(z_sb.sem, 1)
            act.sem_inc(exp.sem, 1)
            norm.act(act, 0, 0)
            for n in range(NPJ):
                raise_(0, 0, n)
            norm.act(act, 1, 1)
            for s in range(LEAD):
                step(0, 0, s, True)

            def body(b, par):
                for s in range(LEAD, LEAD + NU):
                    step(b, par, s)
                norm.act(act, b + 2, par)
            both_parities(act, body)

        @block.tensor
        def _(pe):
            def project(b, par, n):
                if n:
                    pe.wait_ge(low.sem, low.at(b, n))
                else:
                    pe.wait_ge(norm.out.sem, norm.out.at(b))
                if n == 1:
                    for k in range(NT):
                        last = nc.tensor.matmul(psJ[:, k * LD:(k + 1) * LD], xnT[:, par, k * P:(k + 1) * P],
                                                m.Wdown[:, 0:LD], start=True, stop=True)
                    last.then_inc(proj.sem, 1)
                else:
                    w = m.Wqk0[:, n - 2, :] if n else m.Wdown[:, :]
                    nc.tensor.matmul(psJ[:, :], w, xnT[:, par, :], start=True, stop=True).then_inc(proj.sem, 1)

            def score(b, par, u, first):
                qb, g = units[u]
                n = (qb + 1) * P
                if qb == 0:
                    pe.wait_ge(low.sem, low.at(b, 2 + HG * (g + 1)))
                for pair in range(2):
                    if u:
                        pe.wait_ge(exp.sem, exp.at(b, 2 * u - 1 + pair))
                    elif first:
                        pe.wait_ge(exp.sem, exp.before(b))
                    else:
                        pe.wait_ge(exp.sem, exp.at(b - 1, 2 * NU - 1 + pair))
                    for j in (2 * pair, 2 * pair + 1):
                        nc.tensor.matmul(psS[:, j, 0:n], qS[:, par, g * HG + j, qb * P:n], latS[:, par, 0:n],
                                         start=True, stop=False)
                        last = nc.tensor.matmul(psS[:, j, qb * P:n], m.identb[:, :], m.causal[:, :],
                                                start=False, stop=True)
                    last.then_inc(scores.sem, 1)

            def turn(b, u, blocks):
                pe.wait_ge(normed.sem, normed.at(b, u + 1))
                for k in blocks:
                    n = jobs_before(u) + k
                    if n >= 2:
                        dve = by_dve(units[all_jobs[n - 2][0]][0], all_jobs[n - 2][1])
                        pe.wait_ge(back[dve].sem, back[dve].at(b, copies(dve, n - 1)))
                    else:
                        pe.wait_ge(back[True].sem, back[True].before(b))
                        pe.wait_ge(back[False].sem, back[False].before(b))
                    for j in range(HG):
                        last = nc.tensor.transpose(psP[n % 2][:, j * P:(j + 1) * P], p[:, u % 4, j, k * P:(k + 1) * P],
                                                   m.ident[:, :])
                    last.then_inc(turned.sem, 1)

            def attend(b, par, u):
                qb, g = units[u]
                pe.wait_ge(back[False].sem, back[False].at(b, copies(False, jobs_before(u + 1))))
                if qb:
                    pe.wait_ge(back[True].sem, back[True].at(b, copies(True, jobs_before(u + 1))))
                if u:
                    pe.wait_ge(z_sb.sem, z_sb.at(b, u))
                else:
                    pe.wait_ge(z_sb.sem, z_sb.before(b))
                if u == 0:
                    pe.wait_ge(added.sem, added.before(b))
                elif g == 0:
                    pe.wait_ge(added.sem, added.at(b, u // NG))
                for k in range(qb + 1):
                    for j in range(HG):
                        last = nc.tensor.matmul(psZ[j * LD:(j + 1) * LD, :], lat[:, par, k, :],
                                                pT[:, u % 2, k, j * P:(j + 1) * P], start=(k == 0), stop=(k == qb))
                last.then_inc(z.sem, 1)

            def project_out(b, qb):
                pe.wait_ge(z_sb.sem, z_sb.at(b, NG * (qb + 1)))
                for g in range(NG):
                    last = nc.tensor.matmul(psO, zT[:, qb % 2, g, :], m.Wvo0[:, g, :], start=(g == 0), stop=(g == NG - 1))
                last.then_inc(o.sem, 1)

            def step(b, par, s, first=False):
                b_, par_, u = unit_of(b, par, s)
                score(b_, par_, u, first)
                if s >= 3:
                    b_, par_, u = unit_of(b, par, s - 3)
                    attend(b_, par_, u)
                if s >= 2:
                    b_, _, u = unit_of(b, par, s - 2)
                    turn(b_, u, range(min(units[u][0] + 1, 2)))
                jobs = projections_of.get(s, [])
                for n in jobs[:1]:
                    project(b + 1, 1 - par, n)
                if s >= 2:
                    turn(b_, u, range(2, units[u][0] + 1))
                for n in jobs[1:]:
                    project(b + 1, 1 - par, n)
                if s >= 6 and (s - 6) % NG == 0:
                    project_out(b, (s - 6) // NG)
            pe.sem_inc(turned.sem, 1)
            norm.pe(pe, 0, True)
            for n in range(NPJ):
                project(0, 0, n)
            pe.wait_ge(low.sem, low.at(0))
            norm.pe(pe, 1)
            for s in range(LEAD):
                step(0, 0, s, True)

            def body(b, par):
                for s in range(LEAD, LEAD + NU):
                    step(b, par, s)
                pe.wait_ge(low.sem, low.at(b + 1))
                norm.pe(pe, b + 2)
            both_parities(pe, body)


def local_stage(nc, m, tag):
    NBK, WB = L // P, P // QW
    NG = H // HG
    NPJ = H + NG
    c = lambda name, per=1, free=0: Count(m, f"{tag}_{name}", per, free)
    scores, mx, exp, inv = c("scores", H), c("row_maxima", H), c("probabilities", H), c("row_sums_inverted", H)
    normed, turned = c("probabilities_normed", H), c("probabilities_transposed", H)
    back_act, back_dve = c("pT_copied_act", H // 2), c("pT_copied_dve", H // 2)
    proj, proj_act, proj_dve = c("projections", NPJ), c("projections_copied_act", NPJ // 2), c("projections_copied_dve", NPJ // 2)
    keys = c("windows_copied")
    z, z_act, z_dve = c("z", NW), c("z_copied_act", NW // 2), c("z_copied_dve", NW // 2)
    first, o, o_sb, oT, added = c("first_token"), c("attended"), c("attended_copied"), c("attended_transposed"), c("x_added", 1, 1)
    cleared = m.semaphore(f"{tag}_margins_cleared")
    ctx = ExitStack()
    with ctx:
        sb = lambda n, s: ctx.enter_context(nc.sbuf_tensor(f"{tag}_{n}", s, F32))
        xnT = sb("xnT", [P, 2, QW + L])
        kwin = sb("kwin", [P, 2, NW, KW])
        xwin = sb("xwin", [KW, 2, NW, D])
        qT = sb("qT", [P, H, L])
        p = sb("p", [P, 2, H, KW])
        pT = sb("pT", [KW, 2, H, P])
        zT = sb("zT", [P, H, L])
        ot = sb("ot", [P, L])
        nmax = sb("nmax", [P, 2, H])
        rsum = sb("rsum", [P, 2, H])
        rinv = sb("rinv", [P, 2, H])
        psS, psP, psZ = m.ps[0:4], m.ps[4:6], m.ps[6:8]
        norm = Norm(nc, m, tag, lambda par: xnT[:, par, QW - 1:QW - 1 + L], psZ[1])
        block = ctx.enter_context(nc.Block())

        @block.gpsimd
        def _(pool):
            def normalise(b, bk):
                for g in range(NG):
                    pg = p[:, bk % 2, g * HG:(g + 1) * HG, :]
                    pool.wait_ge(inv.sem, inv.at(b, bk * NG + g + 1))
                    nc.gpsimd.tensor_tensor(pg, pg, bc(rinv[:, bk % 2, g * HG:(g + 1) * HG], 2, KW), ALU.mult).then_inc(normed.sem, 1)
            norm.pool_rstd(pool, 0)
            normalise(0, 0)

            def body(b, par):
                for bk in range(1, NBK):
                    normalise(b, bk)
                    if bk == 1:
                        norm.pool_rstd(pool, b + 1)
                normalise(b + 1, 0)
            both_parities(pool, body)

        def copy_projection(copy, b, par, n):
            if n < H:
                return copy(qT[:, n, :], psZ[n % 2][:, :])
            w = (n - H) * WB
            return copy(xwin[:, par, w:w + WB, :], psZ[n % 2][0:KW, :].rearrange("k (w d) -> k w d", d=D))

        @block.vector
        def _(dve):
            dve.sem_inc(added.sem, 1)
            nc.vector.memset(xnT[:, :, :], 0.0).then_inc(cleared, 1)

            def windows(b, par):
                dve.wait_ge(norm.out.sem, norm.out.at(b))
                nc.vector.tensor_copy(kwin[:, par, :, 0:QW], xnT[:, par, 0:L].rearrange("p (w k) -> p w k", k=QW))
                nc.vector.tensor_copy(kwin[:, par, :, QW:2 * QW], xnT[:, par, QW:QW + L].rearrange("p (w k) -> p w k", k=QW))
                nc.vector.tensor_copy(kwin[:, par, :, 2 * QW:KW], bc(xnT[:, par, QW - 1:QW], 1, NW)).then_inc(keys.sem, 1)

            def projection(b, par, n):
                dve.wait_ge(proj.sem, proj.at(b, n + 1))
                copy_projection(nc.vector.tensor_copy, b, par, n).then_inc(proj_dve.sem, 1)

            def maximum(b, u):
                bk, g = divmod(u, NG)
                dve.wait_ge(scores.sem, scores.at(b, u + 1))
                nc.vector.tensor_reduce(nmax[:, bk % 2, g * HG:(g + 1) * HG],
                                        psS[g][:, 0:HG * KW].rearrange("p (h k) -> p h k", k=KW),
                                        AX.X, ALU.max, negate=True).then_inc(mx.sem, 1)

            def invert(b, u):
                bk, g = divmod(u, NG)
                dve.wait_ge(exp.sem, exp.at(b, u + 1))
                hs = slice(g * HG, (g + 1) * HG)
                nc.vector.reciprocal(rinv[:, bk % 2, hs], rsum[:, bk % 2, hs]).then_inc(inv.sem, 1)

            def copy_z(b, n):
                dve.wait_ge(z.sem, z.at(b, n + 1))
                nc.vector.tensor_copy(zT[:, :, n * QW:(n + 1) * QW], psZ[1][:, :].rearrange("p (h q) -> p h q", q=QW)).then_inc(z_dve.sem, 1)

            def copy_back(b, u):
                bk, g = divmod(u, NG)
                dve.wait_ge(turned.sem, turned.at(b, u + 1))
                nc.vector.tensor_copy(pT[:, bk % 2, g * HG:(g + 1) * HG, :],
                                      psP[1][0:KW, :].rearrange("k (h q) -> k h q", q=P)).then_inc(back_dve.sem, 1)
            norm.dve_stats(dve, 0)
            norm.dve_apply(dve, 0, True)
            windows(0, 0)
            for n in range(1, NPJ, 2):
                projection(0, 0, n)
            for g in range(NG):
                maximum(0, g)
                if g:
                    invert(0, g - 1)
            invert(0, 3)
            copy_back(0, 1)
            copy_back(0, 3)

            def body(b, par):
                for bk in range(1, NBK):
                    u, w = bk * NG, (bk - 1) * WB
                    maximum(b, u)
                    if bk > 1:
                        copy_back(b, u - 1)
                    maximum(b, u + 1)
                    invert(b, u)
                    maximum(b, u + 2)
                    copy_z(b, w + 1)
                    invert(b, u + 1)
                    maximum(b, u + 3)
                    invert(b, u + 2)
                    copy_z(b, w + 3)
                    invert(b, u + 3)
                    copy_back(b, u + 1)
                    if bk == 1:
                        norm.dve_stats(dve, b + 1)
                    if bk == 2:
                        norm.dve_apply(dve, b + 1)
                windows(b + 1, 1 - par)
                projection(b + 1, 1 - par, 1)
                copy_back(b, H - 1)
                for n in range(3, NPJ, 2):
                    projection(b + 1, 1 - par, n)
                maximum(b + 1, 0)
                maximum(b + 1, 1)
                invert(b + 1, 0)
                copy_z(b, NW - 3)
                maximum(b + 1, 2)
                invert(b + 1, 1)
                maximum(b + 1, 3)
                invert(b + 1, 2)
                copy_z(b, NW - 1)
                invert(b + 1, 3)
                copy_back(b + 1, 1)
                copy_back(b + 1, 3)
                dve.wait_ge(oT.sem, oT.at(b))
                xb = m.x[:, bass.ds(b * NT, NT), :]
                nc.vector.tensor_tensor(xb, xb, psZ[1][:, :].rearrange("p (k o) -> p k o", o=D), ALU.add).then_inc(added.sem, 1)
            both_parities(dve, body)

        @block.scalar
        def _(act):
            def projection(b, par, n):
                act.wait_ge(proj.sem, proj.at(b, n + 1))
                copy_projection(nc.scalar.copy, b, par, n).then_inc(proj_act.sem, 1)

            def exponents(b, u):
                bk, g = divmod(u, NG)
                act.wait_ge(mx.sem, mx.at(b, u + 1))
                for j in range(HG):
                    h = g * HG + j
                    last = nc.scalar.activation(p[:, bk % 2, h, :], psS[g][:, j * KW:(j + 1) * KW], ACT.Exp,
                                                bias=nmax[:, bk % 2, h:h + 1], accum_out=rsum[:, bk % 2, h:h + 1])
                last.then_inc(exp.sem, 1)

            def copy_z(b, n):
                act.wait_ge(z.sem, z.at(b, n + 1))
                nc.scalar.copy(zT[:, :, n * QW:(n + 1) * QW], psZ[0][:, :].rearrange("p (h q) -> p h q", q=QW)).then_inc(z_act.sem, 1)

            def copy_back(b, u):
                bk, g = divmod(u, NG)
                act.wait_ge(turned.sem, turned.at(b, u + 1))
                nc.scalar.copy(pT[:, bk % 2, g * HG:(g + 1) * HG, :],
                               psP[0][0:KW, :].rearrange("k (h q) -> k h q", q=P)).then_inc(back_act.sem, 1)
            act.wait_ge(cleared, 1)
            norm.act(act, 0, 0)
            for n in range(0, NPJ, 2):
                projection(0, 0, n)
            for g in range(NG):
                exponents(0, g)
            copy_back(0, 0)
            copy_back(0, 2)

            def body(b, par):
                for bk in range(1, NBK):
                    u, w = bk * NG, (bk - 1) * WB
                    exponents(b, u)
                    if bk == NBK - 1:
                        norm.act(act, b + 1, 1 - par)
                    exponents(b, u + 1)
                    copy_z(b, w)
                    exponents(b, u + 2)
                    exponents(b, u + 3)
                    copy_back(b, u)
                    copy_z(b, w + 2)
                    copy_back(b, u + 2)
                for n in range(0, NPJ, 2):
                    projection(b + 1, 1 - par, n)
                exponents(b + 1, 0)
                copy_z(b, NW - 4)
                exponents(b + 1, 1)
                exponents(b + 1, 2)
                copy_z(b, NW - 2)
                exponents(b + 1, 3)
                copy_back(b + 1, 0)
                act.wait_ge(first.sem, first.at(b))
                nc.scalar.activation(ot[:, 0:1], psZ[0][:, 0:1], ACT.Identity, bias=m.b_out[:, 0:1])
                act.wait_ge(o.sem, o.at(b))
                nc.scalar.activation(ot[:, 1:L], psZ[1][:, 0:L - 1], ACT.Identity, bias=m.b_out[:, 0:1]).then_inc(o_sb.sem, 1)
                copy_back(b + 1, 2)
            both_parities(act, body)

        @block.tensor
        def _(pe):
            def project(b, par, n):
                if n >= 2:
                    copied = (proj_act, proj_dve)[n % 2]
                    pe.wait_ge(copied.sem, copied.at(b, n // 2))
                if n < H:
                    last = nc.tensor.matmul(psZ[n % 2][:, :], m.Wqk1[:, n, :], xnT[:, par, QW:QW + L], start=True, stop=True)
                else:
                    if n == H:
                        pe.wait_ge(keys.sem, keys.at(b))
                    for j in range(WB):
                        last = nc.tensor.transpose(psZ[n % 2][0:KW, j * D:(j + 1) * D],
                                                   kwin[:, par, (n - H) * WB + j, :], m.ident[:, :])
                last.then_inc(proj.sem, 1)

            def score(b, par, u, first_block=False):
                bk, g = divmod(u, NG)
                if not first_block:
                    pe.wait_ge(exp.sem, exp.at(b, u - NG + 1))
                out = psS[g]
                nc.tensor.matmul(out[:, 0:HG * KW], m.identb[:, :],
                                 m.window[:, min(bk, 1), :, :].rearrange("p h k -> p (h k)"),
                                 start=True, stop=False, skip_group_check=True)
                for i in range(HG):
                    for j in range(WB):
                        q = bk * P + j * QW
                        last = nc.tensor.matmul(out[j * QW:(j + 1) * QW, i * KW:(i + 1) * KW],
                                                qT[:, g * HG + i, q:q + QW], kwin[:, par, bk * WB + j, :],
                                                start=False, stop=(i == HG - 1), skip_group_check=True)
                last.then_inc(scores.sem, 1)

            def turn(b, u):
                bk, g = divmod(u, NG)
                if u >= 2:
                    back = (back_act, back_dve)[u % 2]
                    pe.wait_ge(back.sem, back.at(b, u // 2))
                pe.wait_ge(normed.sem, normed.at(b, u + 1))
                for i in range(HG):
                    last = nc.tensor.transpose(psP[u % 2][0:KW, i * P:(i + 1) * P], p[:, bk % 2, g * HG + i, :],
                                               m.ident[:, :])
                last.then_inc(turned.sem, 1)

            def attend(b, par, n):
                bk, j = divmod(n, WB)
                if j == 0:
                    pe.wait_ge(back_act.sem, back_act.at(b, (bk + 1) * NG // 2))
                    pe.wait_ge(back_dve.sem, back_dve.at(b, (bk + 1) * NG // 2))
                if n == 1:
                    pe.wait_ge(added.sem, added.before(b))
                elif n == 9:
                    pe.wait_ge(norm.out.sem, norm.out.at(b + 1))
                elif n in (12, 13):
                    copied = (proj_act, proj_dve)[n % 2]
                    pe.wait_ge(copied.sem, copied.at(b + 1))
                elif n >= 2:
                    copied = (z_act, z_dve)[n % 2]
                    pe.wait_ge(copied.sem, copied.at(b, n // 2))
                nc.tensor.matmul(psZ[n % 2][:, :], xwin[:, par, n, :], pT[:, bk % 2, :, j * QW:(j + 1) * QW],
                                 start=True, stop=True).then_inc(z.sem, 1)
            norm.pe(pe, 0, True)
            pe.wait_ge(norm.out.sem, norm.out.at(0))
            for n in range(NPJ):
                project(0, 0, n)
            pe.wait_ge(proj_act.sem, proj_act.at(0))
            pe.wait_ge(proj_dve.sem, proj_dve.at(0))
            for g in range(NG):
                score(0, 0, g, True)
            for g in range(NG):
                turn(0, g)

            def body(b, par):
                for bk in range(1, NBK):
                    u, w = bk * NG, (bk - 1) * WB
                    score(b, par, u)
                    if bk > 1:
                        turn(b, u - 1)
                    if bk == NBK - 1:
                        pe.wait_ge(z_dve.sem, z_dve.at(b, 4))
                        norm.pe(pe, b + 1)
                    score(b, par, u + 1)
                    attend(b, par, w)
                    score(b, par, u + 2)
                    attend(b, par, w + 1)
                    score(b, par, u + 3)
                    attend(b, par, w + 2)
                    turn(b, u)
                    attend(b, par, w + 3)
                    turn(b, u + 1)
                    turn(b, u + 2)
                pe.wait_ge(norm.out.sem, norm.out.at(b + 1))
                pe.wait_ge(z_act.sem, z_act.at(b, 6))
                project(b + 1, 1 - par, 0)
                pe.wait_ge(z_dve.sem, z_dve.at(b, 6))
                project(b + 1, 1 - par, 1)
                turn(b, H - 1)
                for n in range(2, NPJ):
                    project(b + 1, 1 - par, n)
                for g in range(NG):
                    score(b + 1, 1 - par, g)
                    attend(b, par, NW - WB + g)
                pe.wait_ge(back_act.sem, back_act.at(b))
                pe.wait_ge(back_dve.sem, back_dve.at(b))
                turn(b + 1, 0)
                turn(b + 1, 1)
                pe.wait_ge(z_act.sem, z_act.at(b))
                nc.tensor.matmul(psZ[0][:, 0:2], m.M_first[:, :], xnT[:, par, QW - 1:QW + 1], start=True, stop=True).then_inc(first.sem, 1)
                pe.wait_ge(z_dve.sem, z_dve.at(b))
                for h in range(H):
                    last = nc.tensor.matmul(psZ[1][:, :], m.M1[:, h, :], zT[:, h, :], start=(h == 0), stop=(h == H - 1))
                last.then_inc(o.sem, 1)
                turn(b + 1, 2)
                turn(b + 1, 3)
                pe.wait_ge(o_sb.sem, o_sb.at(b))
                for k in range(NT):
                    last = nc.tensor.transpose(psZ[1][:, k * D:(k + 1) * D], ot[:, k * P:(k + 1) * P], m.ident[:, :])
                last.then_inc(oT.sem, 1)
            both_parities(pe, body)


def program(nc, x_in, Wq0, Wkv_down, Wk_up, Wv_up, Wout0, gate_w, gate_b, expert_w, expert_b,
            w_qkv, w_out, b_out, w_th, prototypes, Bf, Af, bias1, temp, out):
    ctx = ExitStack()
    with ctx:
        class m:
            in_stage = []

            @classmethod
            def semaphore(cls, name):
                cls.in_stage.append(nc.alloc_semaphore(name))
                return cls.in_stage[-1]

            @classmethod
            def end_stage(cls):
                nc.clear_and_free_semaphores(cls.in_stage)
                nc.all_engine_barrier()
                cls.in_stage = []
        sb = lambda n, s, dt=F32: ctx.enter_context(nc.sbuf_tensor(n, s, dt))
        m.x = sb("x_res", [P, (NB + 2) * NT, D])
        m.ident = sb("ident", [P, P])
        m.neg_half = sb("neg_half", [P, NT])
        m.xn = sb("xn", [P, NT, D])
        m.st = sb("st", [P, NT, 6])
        m.sums = sb("sums", [P, 4, NT])
        m.mean = sb("mean", [P, NT])
        m.var = sb("var", [P, NT])
        m.eps = sb("eps", [P, NT])
        m.var_eps = sb("var_eps", [P, NT])
        m.rstd = sb("rstd", [P, NT])
        m.gate_w = sb("gate_w", [P, NE])
        m.gate_b = sb("gate_b", [P, NE])
        m.expert_w = sb("expert_w", [P, NE * D])
        m.expert_b = sb("expert_b", [P, NT, D])
        m.half = sb("half", [P, 2, NT])
        m.rank_back = sb("rank_back", [P, NPROTO])
        m.protoT = sb("protoT", [P, NPROTO])
        m.proto_sq = sb("proto_sq", [P, NPROTO])
        m.proto_b = sb("proto_b", [P, NT, D])
        m.neg_inv_t = sb("neg_inv_t", [P, 1])
        m.BT = sb("BT", [P, NR // P, P])
        m.AT = sb("AT", [P, NR // P, D])
        m.Wqk0 = sb("Wqk0", [P, H, HG * LD])
        m.Wvo0 = sb("Wvo0", [P, H // HG, D])
        m.Wdown = sb("Wdown", [P, HG * LD])
        m.Wqk1 = sb("Wqk1", [P, H, D])
        m.M1 = sb("M1", [P, H, D])
        m.M_first = sb("M_first", [P, D])
        m.b_out = sb("b_out", [P, 1])
        m.identb = sb("identb", [P, P], BF16)
        m.causal = sb("causal", [P, P], BF16)
        m.window = sb("window", [P, 2, HG, KW], BF16)
        m.psS = ctx.enter_context(nc.psum_tensor("banks0to3", [P, 4 * 512], F32))
        m.ps = [m.psS[:, i * 512:(i + 1) * 512] for i in range(4)]
        m.ps += [ctx.enter_context(nc.psum_tensor(f"bank{i}", [P, 512], F32))[:, :] for i in range(4, 8)]

        x_view = x_in.rearrange("b (k p) d -> p (b k) d", p=P)
        out_view = out.rearrange("b (k p) d -> p (b k) d", p=P)
        prep_stage(nc, m, locals())
        m.end_stage()
        for n, stage in enumerate((moe_stage, latent_stage, moe_stage, proto_stage, local_stage, proto_stage)):
            stage(nc, m, f"s{n}")
            m.end_stage()
        stored = nc.alloc_semaphore("stored")
        with nc.Block() as block:
            @block.sync
            def _(sp):
                for q in range(4):
                    sp.dma_start(out_view[:, q * 16:(q + 1) * 16, :], m.x[:, q * 16:(q + 1) * 16, :]).then_inc(stored, 16)
                sp.wait_ge(stored, 64)


def prep_stage(nc, m, a):
    def sem(name):
        return m.semaphore("prep_" + name)
    loaded, bias_loaded, x_loaded = sem("weights_loaded"), sem("biases_loaded"), sem("x_loaded")
    cleared, filled, ident_ready = sem("cleared"), sem("filled"), sem("ident_ready")
    masks0, masks1, masks2, masks_ready = sem("masks_cleared"), sem("masks_causal"), sem("masks_rows"), sem("masks_ready")
    turned, copied = sem("transposed"), sem("transposes_copied")
    small_steps, sq_ready, scaled, scaled_used = sem("small_steps"), sem("proto_squared"), sem("wout_scaled"), sem("wout_scaled_used")
    products, products_copied, folded = sem("products"), sem("products_copied"), sem("folded")
    NC = H // 2
    ctx = ExitStack()
    with ctx:
        sb = lambda n, s, dt=F32: ctx.enter_context(nc.sbuf_tensor("prep_" + n, s, dt))
        wqkv = sb("wqkv", [P, 3, NC, P])
        wo1 = sb("wo1", [P, NC, D])
        wo0 = sb("wo0", [P, NC, D])
        wq0 = sb("wq0", [P, NC, P])
        wku = sb("wku", [LD, NC, P])
        wvu = sb("wvu", [LD, NC, P])
        Bn = sb("Bn", [P, NR // P, P])
        An = sb("An", [P, NR])
        protos = sb("protos", [NPROTO, P])
        t = sb("temp", [P, 3])
        th = sb("th", [P, NC, H])
        T1 = sb("T1", [P, 3, NC, P])
        T0q = sb("T0q", [P, NC, P])
        T0k = sb("T0k", [P, NC, LD])
        T0v = sb("T0v", [P, NC, LD])
        proto2 = sb("proto2", [P, NPROTO])
        ones = sb("ones", [P, P])
        causal = sb("causal", [P, P])
        window = sb("window", [P, 2, HG, KW])
        back = sb("rank_int", [P, NPROTO], mybir.dt.int32)
        wsc = sb("wo1_scaled", [P, 2, H, D])

        groups = []
        for w in range(3):
            for half in range(2):
                q = slice(half * 4, half * 4 + 4)
                groups.append((T1[:, w, q, :], [wqkv[:, w, c, :] for c in range(8)[q]]))
        for half in range(2):
            q = slice(half * 4, half * 4 + 4)
            groups.append((T0q[:, q, :], [wq0[:, c, :] for c in range(8)[q]]))
        groups.append((T0k[:, :, :], [wku[:, c, :] for c in range(NC)]))
        groups.append((T0v[:, :, :], [wvu[:, c, :] for c in range(NC)]))
        groups.append((m.BT[:, :, :], [Bn[:, c, :] for c in range(NR // P)]))
        groups.append((m.AT[:, :, :], [An[:, c * P:(c + 1) * P] for c in range(NR // P)]))
        groups.append((m.protoT[:, :], [protos[:, :]]))

        block = ctx.enter_context(nc.Block())

        @block.sync
        def _(sp):
            loads = [(wqkv[:, w, :, :].rearrange("p c n -> p (c n)"), a["w_qkv"][:, w * H * HD:(w + 1) * H * HD])
                     for w in range(3)]
            loads += [
                (wq0[:, :, :].rearrange("p c n -> p (c n)"), a["Wq0"].rearrange("d h k -> d (h k)")),
                (wku[:, :, :].rearrange("p c n -> p (c n)"), a["Wk_up"].rearrange("d h k -> d (h k)")),
                (wvu[:, :, :].rearrange("p c n -> p (c n)"), a["Wv_up"].rearrange("d h k -> d (h k)")),
                (Bn[:, :, :], a["Bf"].rearrange("n r i -> (n r) i").rearrange("(c p) i -> p c i", p=P)),
                (An[:, :].rearrange("o (n r) -> o n r", r=RANK), a["Af"].rearrange("n o r -> o n r")),
                (protos[:, :], a["prototypes"]),
                (wo0[:, :, :], a["Wout0"].rearrange("h k o -> (h k) o").rearrange("(c p) o -> p c o", p=P)),
                (wo1[:, :, :], a["w_out"].rearrange("(c p) o -> p c o", p=P)),
                (m.Wdown[:, :].rearrange("d (r c) -> d r c", c=LD), bc(a["Wkv_down"], 1, HG)),
                (m.gate_w[:, :], a["gate_w"]),
                (m.gate_b[:, :], a["gate_b"].partition_broadcast(P)),
                (m.expert_w[:, :].rearrange("d (e o) -> d e o", o=D), a["expert_w"].rearrange("e d o -> d e o")),
                (m.b_out[:, :], a["b_out"].rearrange("(o u) -> o u", u=1)),
                (t[:, 0:1], a["temp"].partition_broadcast(P)),
            ]
            w_th = a["w_th"].rearrange("(c s) h -> s c h", s=2)
            loads += [(th[s * HD:(s + 1) * HD, :, :], w_th[s].partition_broadcast(HD)) for s in range(2)]
            for dst, src in loads:
                sp.dma_start(dst, src).then_inc(loaded, 16)
            m.n_loads = len(loads)
            sp.wait_ge(cleared, 2)
            for k in range(NT):
                sp.dma_start(m.expert_b[32 * k:32 * k + NE, k, :], a["expert_b"]).then_inc(bias_loaded, 16)
                sp.dma_start(m.proto_b[32 * k:32 * k + NPROTO, k, :], a["bias1"]).then_inc(bias_loaded, 16)
            for q in range(4):
                sp.dma_start(m.x[:, q * 16:(q + 1) * 16, :], a["x_view"][:, q * 16:(q + 1) * 16, :]).then_inc(x_loaded, 16)
            sp.wait_ge(bias_loaded, 2 * NT * 16)
            sp.wait_ge(x_loaded, 64)

        @block.gpsimd
        def _(pool):
            for tile, value in ((m.ident[:, :], 0.0), (m.neg_half[:, :], -0.5), (m.eps[:, :], EPS),
                                (m.half[:, :, :], 0.5), (ones[:, :], 1.0), (m.x[:, NB * NT:, :], 0.0)):
                nc.gpsimd.memset(tile, value).then_inc(filled, 1)
            nc.gpsimd.memset(m.expert_b[:, :, :], 0.0).then_inc(cleared, 1)
            nc.gpsimd.memset(m.proto_b[:, :, :], 0.0).then_inc(cleared, 1)
            nc.gpsimd.memset(causal[:, :], 0.0).then_inc(masks0, 1)
            nc.gpsimd.memset(window[:, :, :, :], 0.0).then_inc(masks0, 1)
            pool.wait_ge(filled, 6)
            nc.gpsimd.affine_select(out=m.ident[:, :], in_=m.ident[:, :], compare_op=ALU.not_equal, fill=1.0,
                                    base=0, pattern=[[-1, P]], channel_multiplier=1).then_inc(ident_ready, 1)
            pool.wait_ge(ident_ready, 1)
            pool.wait_ge(masks0, 2)
            nc.gpsimd.affine_select(out=causal[:, :], in_=causal[:, :], compare_op=ALU.is_ge, fill=MASKED,
                                    base=0, pattern=[[-1, P]], channel_multiplier=1).then_inc(masks1, 1)
            for j in range(P // QW):
                q = slice(j * QW, (j + 1) * QW)
                pool.wait_ge(masks1, 1 + 2 * j)
                own = window[q, :, :, QW:2 * QW].rearrange("p a h k -> p (a h) k")
                nc.gpsimd.affine_select(out=own, in_=own, compare_op=ALU.is_ge, fill=MASKED,
                                        base=0, pattern=[[0, 2 * HG], [-1, QW]], channel_multiplier=1).then_inc(masks1, 1)
                pool.wait_ge(masks1, 2 + 2 * j)
                top = window[q, :, :, 0:16].rearrange("p a h k -> p (a h) k")
                nc.gpsimd.affine_select(out=top, in_=top, compare_op=ALU.is_ge, fill=MASKED,
                                        base=15, pattern=[[0, 2 * HG], [0, 16]], channel_multiplier=-1).then_inc(masks1, 1)
            pool.wait_ge(masks1, 1 + 2 * (P // QW))
            nc.gpsimd.memset(window[0:QW, 0, :, 0:QW], MASKED).then_inc(masks2, 1)
            nc.gpsimd.iota(back[:, :], pattern=[[-1, NPROTO]], base=NPROTO, channel_multiplier=0).then_inc(masks2, 1)
            pool.wait_ge(masks2, 2)
            pool.wait_ge(ident_ready, 1)
            nc.gpsimd.tensor_copy(m.causal[:, :], causal[:, :]).then_inc(masks_ready, 1)
            nc.gpsimd.tensor_copy(m.window[:, :, :, :], window[:, :, :, :]).then_inc(masks_ready, 1)
            nc.gpsimd.tensor_copy(m.identb[:, :], m.ident[:, :]).then_inc(masks_ready, 1)
            nc.gpsimd.tensor_copy(m.rank_back[:, :], back[:, :]).then_inc(masks_ready, 1)

        @block.vector
        def _(dve):
            dve.wait_ge(loaded, 16 * m.n_loads)
            nc.vector.tensor_scalar(t[:, 1:2], t[:, 0:1], -1.0, None, ALU.mult).then_inc(small_steps, 1)
            dve.wait_ge(small_steps, 1)
            nc.vector.tensor_tensor(t[:, 1:2], t[:, 0:1], t[:, 1:2], ALU.max).then_inc(small_steps, 1)
            dve.wait_ge(small_steps, 2)
            nc.vector.tensor_scalar(t[:, 1:2], t[:, 1:2], 0.1, -1.0, ALU.max, ALU.mult).then_inc(small_steps, 1)
            dve.wait_ge(small_steps, 3)
            nc.vector.reciprocal(m.neg_inv_t[:, :], t[:, 1:2])
            dve.wait_ge(copied, len(groups))
            nc.vector.tensor_tensor(proto2[:, :], m.protoT[:, :], m.protoT[:, :], ALU.mult).then_inc(sq_ready, 1)
            for c in range(NC):
                if c >= 2:
                    dve.wait_ge(scaled_used, c - 1)
                nc.vector.tensor_tensor(wsc[:, c % 2], bc(th[:, c, :], 2, D), bc(wo1[:, c, :], 1, H), ALU.mult)\
                  .then_inc(scaled, 1)

        @block.scalar
        def _(act):
            for n, (dst, srcs) in enumerate(groups):
                act.wait_ge(turned, n + 1)
                rows = sum(x.shape[0] for x in srcs)
                src = m.ps[n % 8][:, 0:rows]
                if len(dst.shape) == 3:
                    src = src.rearrange("p (c n) -> p c n", c=len(srcs))
                nc.scalar.copy(dst, src).then_inc(copied, 1)
            Wqk1 = m.Wqk1[:, :, :].rearrange("p (q c s) n -> p q c s n", s=2, c=4)
            Wqk0 = m.Wqk0[:, :, :].rearrange("p (c s) (r n) -> p c s r n", s=2, n=LD)
            act.wait_ge(products, 8)
            for s in range(2):
                for q in range(2):
                    nc.scalar.mul(Wqk1[:, q, :, s, :], m.ps[2 * s + q][:, :].rearrange("p (c n) -> p c n", c=4), HD ** -0.5)
                for r in range(HG):
                    nc.scalar.mul(Wqk0[:, :, s, r, :], m.ps[4 + s][:, 0:NC * LD].rearrange("p (c n) -> p c n", c=NC), HD ** -0.5)
            for j in range(HG):
                q = slice(j * LD, (j + 1) * LD)
                last = nc.scalar.copy(m.Wvo0[q, :, :], m.ps[6 + j % 2][q, :].rearrange("p (g o) -> p g o", o=D))
            last.then_inc(products_copied, 1)
            act.wait_ge(folded, 1)
            for j in range(4):
                nc.scalar.copy(m.M1[:, j * 4:(j + 1) * 4, :], m.ps[j][:, :].rearrange("p (h o) -> p h o", o=D))
            nc.scalar.copy(m.M_first[:, :], m.ps[4][:, 0:D])
            nc.scalar.copy(m.proto_sq[:, :], m.ps[5][:, 0:NPROTO])

        @block.tensor
        def _(pe):
            pe.wait_ge(loaded, 16 * m.n_loads)
            pe.wait_ge(ident_ready, 1)
            for n, (dst, srcs) in enumerate(groups):
                if n >= 8:
                    pe.wait_ge(copied, n - 7)
                rows = srcs[0].shape[0]
                for j, src in enumerate(srcs):
                    last = nc.tensor.transpose(m.ps[n % 8][:, j * rows:(j + 1) * rows], src, m.ident[0:rows, 0:rows])
                last.then_inc(turned, 1)
            pe.wait_ge(copied, len(groups))
            for s in range(2):
                k = slice(s * HD, (s + 1) * HD)
                for q in range(2):
                    for j in range(4):
                        c = 4 * q + j
                        last = nc.tensor.matmul(m.ps[2 * s + q][:, j * P:(j + 1) * P], T1[k, 0, c, :], T1[k, 1, c, :],
                                                start=True, stop=True)
                    last.then_inc(products, 1)
                for c in range(NC):
                    last = nc.tensor.matmul(m.ps[4 + s][:, c * LD:(c + 1) * LD], T0q[k, c, :], T0k[k, c, :],
                                            start=True, stop=True)
                last.then_inc(products, 1)
                for c in range(NC):
                    j, g = (2 * c + s) % HG, (2 * c + s) // HG
                    last = nc.tensor.matmul(m.ps[6 + s][j * LD:(j + 1) * LD, g * D:(g + 1) * D], T0v[k, c, :],
                                            wo0[k, c, :], start=True, stop=True)
                last.then_inc(products, 1)
            pe.wait_ge(products_copied, 1)
            pe.wait_ge(sq_ready, 1)
            pe.wait_ge(filled, 6)
            nc.tensor.matmul(m.ps[5][:, 0:NPROTO], ones[:, :], proto2[:, :], start=True, stop=True)
            for c in range(NC):
                nc.tensor.matmul(m.ps[4][:, 0:D], T1[:, 2, c, :], wo1[:, c, :], start=(c == 0), stop=(c == NC - 1))
                pe.wait_ge(scaled, c + 1)
                for j in range(4):
                    last = nc.tensor.matmul(m.ps[j][:, :], T1[:, 2, c, :],
                                            wsc[:, c % 2, j * 4:(j + 1) * 4, :].rearrange("p h o -> p (h o)"),
                                            start=(c == 0), stop=(c == NC - 1))
                last.then_inc(scaled_used, 1)
            pe.wait_ge(scaled_used, NC)
            pe.sem_inc(folded, 1)


_INS = ['L0_attn_x_bld', 'L0_attn_Wq', 'L0_attn_Wkv_down', 'L0_attn_Wk_up', 'L0_attn_Wv_up', 'L0_attn_Wout',
        'L0_ffn_gate_w', 'L0_ffn_gate_b', 'L0_ffn_expert_w', 'L0_ffn_expert_b', 'L1_attn_w_qkv', 'L1_attn_w_out',
        'L1_attn_b_out', 'L1_attn_w_th', 'L1_ffn_prototypes', 'L1_ffn_B', 'L1_ffn_A', 'L1_ffn_bias', 'L1_ffn_temp']


def kernel(**inputs):
    import numpy as _np
    import concourse.bacc as _bacc
    from concourse import mybir as _mybir
    from concourse.bass_utils import run_bass_kernel_spmd as _run

    nc = _bacc.Bacc("TRN2", target_bir_lowering=False, num_devices=1)
    arrays, args = {}, []
    for name in _INS:
        a = _np.ascontiguousarray(inputs[name])
        if name == 'L1_ffn_temp':
            a = a.reshape(1)
        arrays[f"in_{name}"] = a
        args.append(nc.dram_tensor(f"in_{name}", a.shape, _mybir.dt.from_np(a.dtype), kind="ExternalInput").ap())
    out = nc.dram_tensor("out", (NB, L, D), F32, kind="ExternalOutput").ap()
    program(nc, *args, out)
    r = _run(nc, [arrays], core_ids=[0])
    return r.results[0]["out"]
```
